# Optimizing a Trainium2 kernel written in Bass

```python
import numpy as np
import jax
import jax.numpy as jnp

def _softmax(x, axis=-1):
    return jax.nn.softmax(x, axis=axis)

def _gelu(x):
    return jax.nn.gelu(x, approximate=True)

def _silu(x):
    return jax.nn.silu(x)

def _sigmoid(x):
    return jax.nn.sigmoid(x)

def _layernorm(x, axis=-1, eps=1e-05):
    m = jnp.mean(x, axis=axis, keepdims=True)
    v = jnp.var(x, axis=axis, keepdims=True)
    return (x - m) / jnp.sqrt(v + eps)

def _scatter_add(tgt, idx, src, axis=0):
    return tgt.at[idx].add(src)

def _segment_sum(src, seg, n):
    return jax.ops.segment_sum(src, seg, n)
kernel_name = 'mk_vit_tower_cls_d1_tok_img768_r4_6610c6'

def setup_inputs(seed: int=0):
    np.random.seed(seed)
    _w = jnp.asarray

    def _rec_inputs():
        import jax
        import jax.numpy as jnp
        _rk = jax.random.key(seed)
        x = 7.57192e-06 + 1.00007 * jax.random.normal(jax.random.fold_in(_rk, 1), (128, 224, 224, 3), jnp.float32)
        cls_tok = 0.02 * jax.random.normal(jax.random.fold_in(_rk, 5), (1, 1, 192), jnp.float32)
        return (x, cls_tok)
    x, cls_tok = _rec_inputs()

    def _L0_tok_setup():
        import jax, jax.numpy as jnp
        import numpy as np
        PATCH = 16
        DIM = 192
        EPS = 0.001

        def _shifts(x):
            zw = jnp.zeros_like(x[:, :, :1, :])
            right = jnp.concatenate([zw, x[:, :, :-1, :]], axis=2)
            left = jnp.concatenate([x[:, :, 1:, :], zw], axis=2)
            zh = jnp.zeros_like(x[:, :1, :, :])
            down = jnp.concatenate([zh, x[:, :-1, :, :]], axis=1)
            up = jnp.concatenate([x[:, 1:, :, :], zh], axis=1)
            return [right, left, down, up]

        def _patchify(x, p):
            b, H, W, C = x.shape
            hh, ww = (H // p, W // p)
            x = x.reshape(b, hh, p, ww, p, C)
            x = x.transpose(0, 1, 3, 2, 4, 5)
            return x.reshape(b, hh * ww, p * p * C)
        key = jax.random.key(seed)
        k1, k2 = jax.random.split(key)
        b, H, Wd, C = (64, 224, 224, 3)
        F = PATCH * PATCH * 5 * C
        x = jax.random.normal(k1, (b, H, Wd, C), dtype=jnp.float32)
        gamma = jnp.ones((F,), dtype=jnp.float32)
        beta = jnp.zeros((F,), dtype=jnp.float32)
        W = jax.random.normal(k2, (F, DIM), dtype=jnp.float32)
        bb = jnp.zeros((DIM,), dtype=jnp.float32)
        return {'x': x, 'gamma': gamma, 'beta': beta, 'W': W, 'b': bb}
    _L0_tok_all = _L0_tok_setup()
    _L0_tok_in = {k: v for k, v in _L0_tok_all.items() if k in ('gamma', 'beta', 'W', 'b')}
    del _L0_tok_all

    def _L0_attn_setup():
        import jax, jax.numpy as jnp
        import numpy as np

        def depthwise_conv1d(x, w, pad):
            return jax.lax.conv_general_dilated(x, w, window_strides=(1,), padding=[(pad, pad)], dimension_numbers=('NCH', 'OIH', 'NCH'), feature_group_count=x.shape[1])
        key = jax.random.key(seed)
        ks = jax.random.split(key, 6)
        B, L, D, F = (2, 512, 192, 64)
        return {'x': jax.random.normal(ks[0], (B, L, D), jnp.float32), 'w_in': jax.random.normal(ks[1], (D, 4 * D), jnp.float32) * D ** (-0.5), 'b_in': jnp.zeros((4 * D,), jnp.float32), 'w_filt': jax.random.normal(ks[2], (F, D), jnp.float32) * F ** (-0.5), 'b_filt': jnp.zeros((D,), jnp.float32), 'w_short': jax.random.normal(ks[3], (D, 1, 3), jnp.float32) * 0.5, 'b_short': jnp.zeros((D,), jnp.float32), 'w_out': jax.random.normal(ks[4], (D, D), jnp.float32) * D ** (-0.5), 'b_out': jnp.zeros((D,), jnp.float32)}
    _L0_attn_all = _L0_attn_setup()
    _L0_attn_in = {k: v for k, v in _L0_attn_all.items() if k in ('w_in', 'b_in', 'w_filt', 'b_filt', 'w_short', 'b_short', 'w_out', 'b_out')}
    del _L0_attn_all

    def _L0_ffn_setup():
        import jax, jax.numpy as jnp
        import numpy as np
        DEPTH = 11

        def _fff_forward(inputs, weights_in, weights_out, depth=DEPTH):
            B, S, _ = inputs.shape
            n_nodes = weights_in.shape[0]
            max_index = n_nodes - 1
            all_logits = jnp.einsum('bsd,nd->bsn', inputs, weights_in)

            def step(prev_idx, _):
                sel = jnp.clip(prev_idx, 0, max_index)
                logits = jnp.take_along_axis(all_logits, sel[..., None], axis=-1)[..., 0]
                new_idx = jnp.clip(2 * sel + 1 + (logits > 0).astype(sel.dtype), 0, max_index)
                return (new_idx, (logits, new_idx))
            idx0 = jnp.zeros((B, S), dtype=jnp.int32)
            _, (logits_seq, idx_seq) = jax.lax.scan(step, idx0, None, length=depth - 1)
            logits = jnp.concatenate([jnp.zeros((1, B, S), all_logits.dtype), logits_seq], axis=0)
            node_idx = jnp.concatenate([idx0[None], idx_seq], axis=0)
            act = jax.nn.gelu(logits, approximate=False)
            onehot = jax.nn.one_hot(node_idx, n_nodes, dtype=act.dtype)
            coeff = jnp.einsum('dbs,dbsn->bsn', act, onehot)
            return jnp.einsum('bsn,nd->bsd', coeff, weights_out)
        key = jax.random.key(seed)
        k1, k2, k3 = jax.random.split(key, 3)
        B, S, D = (4, 1024, 192)
        n_nodes = 2 * DEPTH - 1
        return {'inputs': jax.random.normal(k1, (B, S, D), dtype=jnp.float32), 'weights_in': jax.random.normal(k2, (n_nodes, D), dtype=jnp.float32), 'weights_out': jax.random.normal(k3, (n_nodes, D), dtype=jnp.float32)}
    _L0_ffn_all = _L0_ffn_setup()
    _L0_ffn_in = {k: v for k, v in _L0_ffn_all.items() if k in ('weights_in', 'weights_out')}
    del _L0_ffn_all
    return {'x': x, 'cls_tok': cls_tok, 'L0_tok_gamma': _L0_tok_in['gamma'], 'L0_tok_beta': _L0_tok_in['beta'], 'L0_tok_W': _L0_tok_in['W'], 'L0_tok_b': _L0_tok_in['b'], 'L0_attn_w_in': _L0_attn_in['w_in'], 'L0_attn_b_in': _L0_attn_in['b_in'], 'L0_attn_w_filt': _L0_attn_in['w_filt'], 'L0_attn_b_filt': _L0_attn_in['b_filt'], 'L0_attn_w_short': _L0_attn_in['w_short'], 'L0_attn_b_short': _L0_attn_in['b_short'], 'L0_attn_w_out': _L0_attn_in['w_out'], 'L0_attn_b_out': _L0_attn_in['b_out'], 'L0_ffn_weights_in': _L0_ffn_in['weights_in'], 'L0_ffn_weights_out': _L0_ffn_in['weights_out']}

def reference(x, cls_tok, L0_tok_gamma, L0_tok_beta, L0_tok_W, L0_tok_b, L0_attn_w_in, L0_attn_b_in, L0_attn_w_filt, L0_attn_b_filt, L0_attn_w_short, L0_attn_b_short, L0_attn_w_out, L0_attn_b_out, L0_ffn_weights_in, L0_ffn_weights_out):
    import jax
    import jax.numpy as jnp

    def _L0_tok_ref(x, gamma, beta, W, b):
        import jax, jax.numpy as jnp
        import numpy as np
        PATCH = 16
        DIM = 192
        EPS = 0.001

        def _shifts(x):
            zw = jnp.zeros_like(x[:, :, :1, :])
            right = jnp.concatenate([zw, x[:, :, :-1, :]], axis=2)
            left = jnp.concatenate([x[:, :, 1:, :], zw], axis=2)
            zh = jnp.zeros_like(x[:, :1, :, :])
            down = jnp.concatenate([zh, x[:, :-1, :, :]], axis=1)
            up = jnp.concatenate([x[:, 1:, :, :], zh], axis=1)
            return [right, left, down, up]

        def _patchify(x, p):
            b, H, W, C = x.shape
            hh, ww = (H // p, W // p)
            x = x.reshape(b, hh, p, ww, p, C)
            x = x.transpose(0, 1, 3, 2, 4, 5)
            return x.reshape(b, hh * ww, p * p * C)
        x5 = jnp.concatenate([x] + _shifts(x), axis=-1)
        tokens = _patchify(x5, PATCH)
        mu = jnp.mean(tokens, axis=-1, keepdims=True)
        var = jnp.mean(jnp.square(tokens - mu), axis=-1, keepdims=True)
        ln = (tokens - mu) * jax.lax.rsqrt(var + EPS) * gamma + beta
        return jnp.einsum('bnf,fd->bnd', ln, W) + b

    def _L0_attn_ref(x, w_in, b_in, w_filt, b_filt, w_short, b_short, w_out, b_out):
        import jax, jax.numpy as jnp
        import numpy as np

        def depthwise_conv1d(x, w, pad):
            return jax.lax.conv_general_dilated(x, w, window_strides=(1,), padding=[(pad, pad)], dimension_numbers=('NCH', 'OIH', 'NCH'), feature_group_count=x.shape[1])
        B, L, D = x.shape
        F = w_filt.shape[0]
        x_short = depthwise_conv1d(x.transpose(0, 2, 1), w_short, 1).transpose(0, 2, 1) + b_short
        proj = x @ w_in + b_in
        x_proj, z_proj, v1, v2 = jnp.split(proj, 4, axis=-1)
        z = jax.nn.silu(z_proj)
        t = jnp.arange(L, dtype=jnp.float32)[:, None]
        f = jnp.arange(F, dtype=jnp.float32)[None, :]
        pos_basis = jnp.sin(t * f / F)
        filt = (pos_basis @ w_filt + b_filt).T
        conv = depthwise_conv1d(x_proj.transpose(0, 2, 1), filt[:, None, :], L // 2)[:, :, :L]
        y = conv.transpose(0, 2, 1) * v1 * v2 * z
        return (y + x_short) @ w_out + b_out

    def _L0_ffn_ref(inputs, weights_in, weights_out):
        import jax, jax.numpy as jnp
        import numpy as np
        DEPTH = 11

        def _fff_forward(inputs, weights_in, weights_out, depth=DEPTH):
            B, S, _ = inputs.shape
            n_nodes = weights_in.shape[0]
            max_index = n_nodes - 1
            all_logits = jnp.einsum('bsd,nd->bsn', inputs, weights_in)

            def step(prev_idx, _):
                sel = jnp.clip(prev_idx, 0, max_index)
                logits = jnp.take_along_axis(all_logits, sel[..., None], axis=-1)[..., 0]
                new_idx = jnp.clip(2 * sel + 1 + (logits > 0).astype(sel.dtype), 0, max_index)
                return (new_idx, (logits, new_idx))
            idx0 = jnp.zeros((B, S), dtype=jnp.int32)
            _, (logits_seq, idx_seq) = jax.lax.scan(step, idx0, None, length=depth - 1)
            logits = jnp.concatenate([jnp.zeros((1, B, S), all_logits.dtype), logits_seq], axis=0)
            node_idx = jnp.concatenate([idx0[None], idx_seq], axis=0)
            act = jax.nn.gelu(logits, approximate=False)
            onehot = jax.nn.one_hot(node_idx, n_nodes, dtype=act.dtype)
            coeff = jnp.einsum('dbs,dbsn->bsn', act, onehot)
            return jnp.einsum('bsn,nd->bsd', coeff, weights_out)
        return _fff_forward(inputs, weights_in, weights_out)
    h = _L0_tok_ref(x, L0_tok_gamma, L0_tok_beta, L0_tok_W, L0_tok_b)
    h = jnp.concatenate([jnp.broadcast_to(cls_tok, (h.shape[0], 1, h.shape[2])), h], axis=1)
    h = h + _L0_attn_ref(_layernorm(h, axis=-1), L0_attn_w_in, L0_attn_b_in, L0_attn_w_filt, L0_attn_b_filt, L0_attn_w_short, L0_attn_b_short, L0_attn_w_out, L0_attn_b_out)
    h = h + _L0_ffn_ref(_layernorm(h, axis=-1), L0_ffn_weights_in, L0_ffn_weights_out)
    return h

_drawn_inputs = setup_inputs


def setup_inputs(seed=0):
    import zlib

    import numpy as np

    out = dict(_drawn_inputs(seed))
    spreads = {'L0_tok_gamma': (1.0, 0.2),
     'L0_tok_beta': (0.0, 0.1),
     'L0_tok_b': (0.0, 2.0),
     'L0_attn_b_in': (0.0, 0.1),
     'L0_attn_b_filt': (0.0, 0.1),
     'L0_attn_b_short': (0.0, 0.8),
     'L0_attn_b_out': (0.0, 2.0)}
    factors = {}
    for name, (base, spread) in spreads.items():
        noise = np.random.default_rng([zlib.crc32(name.encode()), seed]).standard_normal(out[name].shape)
        drawn = base * np.exp(spread * noise) if base else spread * noise
        out[name] = jnp.asarray(drawn.astype(out[name].dtype))
    for name, factor in factors.items():
        out[name] = (out[name] * factor).astype(out[name].dtype)
    return out
```

```python
import numpy as np
import concourse.bass as bass
from concourse import mybir

F32 = mybir.dt.float32
F32R = mybir.dt.float32r
ALU = mybir.AluOpType
ACT = mybir.ActivationFunctionType
AXIS = mybir.AxisListType

NIMG, IMG, CH, PATCH, DIM = 128, 224, 3, 16, 192
GRID = IMG // PATCH
NTOK = GRID * GRID + 1
QUAD = 4
NBATCH = -(-NTOK // QUAD)
PTOK = NBATCH * QUAD
HALF = DIM // 2
ROWF = IMG * CH
LEAD, PITCH = 4, 680
BAND = PATCH + 2
PXF = PATCH * CH
NFEAT = PATCH * PATCH * 5 * CH
NSHIFT = 5
RINGF = PXF + 2 * CH
PATF = BAND * RINGF
NCHUNK = 8
COPY_POOL = (3, 8, 13)
PATCH_SLOT = [2 if w in COPY_POOL else (w - sum(v < w for v in COPY_POOL)) % 2 for w in range(GRID)]
WCOL = DIM + 2
KROW = NFEAT // 128
HCOL = DIM + 2
SPAD = NTOK // 2
TAP0 = 112
TAP1 = NTOK - TAP0
TAP1L = PTOK - TAP0
HANK = TAP0 + NTOK
GPADW = 424
CG = 8
NGROUP = DIM // CG
FFREQ = 64
NODES, NODEX = 21, 32
INNER = 15
TOK_EPS, LN_EPS = 1e-3, 1e-5
PIXEL_OF = ((0, 0), (0, -1), (0, 1), (-1, 0), (1, 0))

COPY_GAP = 1200
COPY_AT = [s * COPY_GAP + 111 - (di + 1) * RINGF - (dj + 1) * CH for s, (di, dj) in enumerate(PIXEL_OF)]


def constants():
    t = np.arange(NTOK, dtype=np.float64)[None, :]
    f = np.arange(FFREQ, dtype=np.float64)[:, None]
    basis = np.ones((FFREQ + 1, NTOK), np.float32)
    basis[:FFREQ] = np.sin(t * f / FFREQ)
    count = np.zeros((NCHUNK * 128, 1), np.float32)
    for di, dj in PIXEL_OF:
        for i in range(PATCH):
            at = (i + di + 1) * RINGF + (dj + 1) * CH
            count[at:at + PXF] += 1
    count = count.reshape(NCHUNK, 128).T
    return {"c_basis": basis, "c_count": count / np.float32(NFEAT)}


def build(nc, x, cls_tok, gamma, beta, W, tok_b, w_in, b_in, w_filt, b_filt, w_short, b_short,
          w_out, b_out, wn_in, wn_out, c_basis, c_count, out):
    def dram(name, shape):
        return nc.dram_tensor(name, shape, F32, kind="Internal").ap()

    wscr = dram("placed_weights", [NSHIFT * COPY_GAP, DIM])
    filt_scr = dram("padded_filter", [DIM, GPADW])
    h_scr = dram("h_tokens", [NIMG, PTOK, HCOL])
    gate_scr = dram("gates", [NIMG, PTOK, DIM])
    proj_scr = dram("x_proj", [PTOK, DIM, NIMG])
    short_scr = dram("x_short", [HALF, 2, PTOK + 4, NIMG])

    class Region:
        def __init__(self, start):
            self.at = start

        def take(self, name, shape, dt=F32):
            size = 4 * int(np.prod(shape[1:]))
            t = nc.alloc_sbuf_tensor_at(name, shape, dt, offset=self.at)
            self.at += -(-size // 32) * 32
            return t

    base = -(-nc.sbuf_base // 32) * 32
    fixed = Region(base)
    ident = fixed.take("ident", [128, 128])
    zeros = fixed.take("zeros", [128, ROWF])
    w_out_sb = fixed.take("w_out_sb", [HALF + 1, 2, DIM])
    node_out = fixed.take("node_out", [128, QUAD, DIM])
    node_inT = fixed.take("node_inT", [HALF, 2, NODEX])
    taps = fixed.take("taps", [HALF, 2, 3])
    taps_b = fixed.take("taps_b", [HALF, 2])
    half_neg = fixed.take("half_neg", [128, 16])
    big = fixed.at

    r1 = Region(big)
    band = [r1.take(f"band{s}", [128, BAND, PITCH]) for s in range(2)]
    wf_hi = r1.take("wf_hi", [128, NCHUNK, WCOL], F32R)
    wf_lo = r1.take("wf_lo", [128, NCHUNK, WCOL], F32R)
    xT_hi = [r1.take(f"xT_hi{s}", [128, NCHUNK, 128], F32R) for s in range(2)]
    xT_lo = [r1.take(f"xT_lo{s}", [128, NCHUNK, 128], F32R) for s in range(2)]
    praw = [r1.take(f"praw{s}", [128, GRID, WCOL]) for s in range(2)]
    htile = [r1.take(f"htile{s}", [128, GRID, HCOL]) for s in range(2)]
    prep_end = r1.at
    patch = [r1.take(f"patch{s}", [128, NCHUNK * 128]) for s in range(3)]
    sq_rows = r1.take("sq_rows", [128, 2, 2, ROWF])
    sq_cols = r1.take("sq_cols", [128, GRID + 1, PATCH, 6])
    tok_bias = r1.take("tok_bias", [128, DIM])
    core_sum = [r1.take(f"core_sum{s}", [128, GRID]) for s in range(2)]
    row_sum = r1.take("row_sum", [128, 2, 2, GRID])
    col_sum = r1.take("col_sum", [128, 2, GRID + 1])
    col_dif = r1.take("col_dif", [128, GRID + 1])
    sum_a = r1.take("sum_a", [128, GRID])
    sum_b = r1.take("sum_b", [128, GRID])
    musq = r1.take("musq", [128, GRID])
    tvar = r1.take("tvar", [128, GRID])
    trstd = [r1.take(f"trstd{s}", [128, GRID]) for s in range(2)]
    bn6 = r1.take("bn6", [128, GRID, 6])
    hvar = r1.take("hvar", [128, GRID])
    pr = Region(big + 4 * BAND * PITCH)
    w_nat = pr.take("w_nat", [128, KROW, DIM])
    w_sc = pr.take("w_scaled", [128, KROW, DIM])
    pr2 = Region(big + 8 * BAND * PITCH + 8 * NCHUNK * WCOL)
    w_sh = pr2.take("w_shown", [128, NSHIFT, NCHUNK, DIM])
    wf = pr2.take("wf", [128, NCHUNK, WCOL])
    gam = pr2.take("gam", [128, KROW])
    bet = pr2.take("bet", [128, KROW])
    ones = pr2.take("ones", [128, 128])
    csum = pr2.take("csum", [128, DIM])
    bias_row = pr2.take("bias_row", [1, DIM])
    cnt = pr2.take("cnt", [128, NCHUNK])
    cnt_neg = pr2.take("cnt_neg", [128, NCHUNK])
    filt_w = pr2.take("filt_w", [FFREQ + 1, DIM])
    filt_b = pr2.take("filt_basis", [FFREQ + 1, NTOK])
    filt_p = pr2.take("filt_pad", [HALF, 2, GPADW])
    nodes = pr2.take("nodes", [NODEX, DIM])
    node_m = pr2.take("node_mean", [NODEX, 1])
    cls_h = pr2.take("cls_h", [128, HCOL])
    cls6 = pr2.take("cls6", [128, 6])
    cls_v = pr2.take("cls_v", [128, 1])

    r2 = Region(big)
    win = r2.take("win", [HALF + 1, 2, 4 * DIM])
    win_hi = r2.take("win_hi", [HALF + 1, 2, 4 * DIM], F32R)
    win_lo = r2.take("win_lo", [HALF + 1, 2, 4 * DIM], F32R)
    hin = [r2.take(f"hin{s}", [128, QUAD, HCOL]) for s in range(2)]
    xn = [r2.take(f"xn{s}", [128, QUAD, DIM]) for s in range(2)]
    xnT = [r2.take(f"xnT{s}", [HALF, 2, QUAD + 2, 128]) for s in range(2)]
    xn_hi = [r2.take(f"xn_hi{s}", [HALF + 1, 2, QUAD * 128], F32R) for s in range(2)]
    xn_lo = [r2.take(f"xn_lo{s}", [HALF + 1, 2, QUAD * 128], F32R) for s in range(2)]
    silu = [r2.take(f"silu{p}", [128, 2, DIM]) for p in range(2)]
    szv = [r2.take(f"szv{p}", [128, 2, DIM]) for p in range(2)]
    gate = [r2.take(f"gate{s}", [128, QUAD, DIM]) for s in range(2)]
    short = [r2.take(f"short{s}", [HALF, 2, QUAD * 128]) for s in range(2)]
    proj = [r2.take(f"proj{s}", [HALF, 2, QUAD, 128]) for s in range(2)]

    r3 = Region(big)
    Y = r3.take("Y", [128, PTOK, DIM])
    after_y = r3.at
    src0 = [r3.take(f"src0_{s}", [TAP0, CG, 128]) for s in range(2)]
    src1 = [r3.take(f"src1_{s}", [TAP1L, CG, 128]) for s in range(2)]
    toep = [r3.take(f"toep{s}", [TAP0, CG, HANK]) for s in range(2)]

    r4 = Region(after_y)
    gy = [r4.take(f"gy{s}", [128, QUAD, DIM]) for s in range(2)]
    sh = [r4.take(f"sh{s}", [HALF, 2, QUAD * 128]) for s in range(2)]
    hb = [r4.take(f"hb{s}", [128, QUAD, HCOL]) for s in range(2)]
    h2 = [r4.take(f"h2_{s}", [128, QUAD, DIM]) for s in range(2)]
    ob = [r4.take(f"ob{s}", [128, QUAD, DIM]) for s in range(2)]
    uT = r4.take("uT", [HALF + 1, 2, QUAD * 128])
    h2T = r4.take("h2T", [HALF, 2, QUAD * 128])
    bn4 = r4.take("bn4", [128, QUAD, 6])
    mv4 = r4.take("mv4", [128, QUAD, 2])
    var4 = r4.take("var4", [128, QUAD])
    rstd4 = [r4.take(f"rstd4_{s}", [128, QUAD]) for s in range(2)]
    logit = r4.take("logit", [128, QUAD, NODEX])
    gel = r4.take("gel", [128, QUAD, NODEX])
    branch = r4.take("branch", [128, QUAD, INNER, 2])
    visit = r4.take("visit", [128, QUAD, NODEX])
    act = r4.take("act", [128, QUAD, NODEX])
    coef = r4.take("coef", [128, QUAD, NODEX])
    tail = r4.take("tail", [128, QUAD])
    coefT = r4.take("coefT", [128, 128])
    assert max(r1.at, r2.at, r3.at, r4.at) <= nc.sbuf_usable_end, (r1.at, r2.at, r3.at, r4.at)
    assert pr.at <= big + 8 * BAND * PITCH and pr2.at <= prep_end, (pr.at, pr2.at, prep_end)

    ps = nc.alloc_psum_tensor("psum", [128, 8, 512], F32)

    S = nc.alloc_semaphore

    BIAS_STEP = 13
    carried = S("carried")
    phase_left = S("phase_left")
    w_loaded, gb_loaded, tables_loaded, small_loaded = S("w_loaded"), S("gb_loaded"), S("tables_loaded"), S("small_loaded")
    consts_set, ident_set = S("consts_set"), S("ident_set")
    prep_dve, prep_pe, prep_pool = S("prep_dve"), S("prep_pe"), S("prep_pool")
    cleared = S("cleared")
    scaled_stored, filter_stored, shifted_loaded = S("scaled_stored"), S("filter_stored"), S("shifted_loaded")
    pads_stored, cls_stored = S("pads_stored"), S("cls_stored")
    band_loaded = [S(f"band_loaded{s}") for s in range(2)]
    ring_zeroed = S("ring_zeroed")
    patch_dve, patch_pool = S("patch_dve"), S("patch_pool")
    xT_in_psum, xT_hi_ready, xT_lo_ready = S("xT_in_psum"), S("xT_hi_ready"), S("xT_lo_ready")
    tok_in_psum, tok_copied = S("tok_in_psum"), S("tok_copied")
    core_squared, edge_squared, edges_summed = S("core_squared"), S("edge_squared"), S("edges_summed")
    tvar_ready, trstd_ready, h_ready, hstat_ready = S("tvar_ready"), S("trstd_ready"), S("h_ready"), S("hstat_ready")
    h_stored = [S(f"h_stored{s}") for s in range(2)]
    h_made, bn_made = S("h_made"), S("bn_made")
    dve_step = S("dve_step")
    pool_step = S("pool_step")
    win_loaded, win_split, win_his = S("win_loaded"), S("win_split"), S("win_his")
    hin_loaded = [S(f"hin_loaded{s}") for s in range(2)]
    xn_ready, xnT_in_psum, xnT_ready, xn_hi_ready, xn_lo_ready = (
        S("xn_ready"), S("xnT_in_psum"), S("xnT_ready"), S("xn_hi_ready"), S("xn_lo_ready"))
    halo_ready, centre_ready, short_ready = S("halo_ready"), S("centre_ready"), S("short_ready")
    zv_in_psum, silu_ready, gate_ready = S("zv_in_psum"), S("silu_ready"), S("gate_ready")
    proj_in_psum, proj_ready = S("proj_in_psum"), S("proj_ready")
    gate_stored = [S(f"gate_stored{s}") for s in range(2)]
    short_stored = [S(f"short_stored{s}") for s in range(2)]
    proj_stored = [S(f"proj_stored{s}") for s in range(2)]
    taps_loaded = [S(f"taps_loaded{s}") for s in range(2)]
    conv_in_psum, conv_kept_act, conv_kept_dve, y_padded = (
        S("conv_in_psum"), S("conv_kept_act"), S("conv_kept_dve"), S("y_padded"))
    gy_loaded = [S(f"gy_loaded{s}") for s in range(2)]
    y_ready, yT_in_psum, u_ready, mix_in_psum, h2_ready = (
        S("y_ready"), S("yT_in_psum"), S("u_ready"), S("mix_in_psum"), S("h2_ready"))
    var_ready, rstd_ready = S("var_ready"), S("rstd_ready")
    h2T_in_psum, h2T_ready, logit_in_psum, logit_ready = (
        S("h2T_in_psum"), S("h2T_ready"), S("logit_in_psum"), S("logit_ready"))
    gel_ready, coef_ready, coefT_in_psum, coefT_ready = (
        S("gel_ready"), S("coef_ready"), S("coefT_in_psum"), S("coefT_ready"))
    node_in_psum, out_ready, tree_set = S("node_in_psum"), S("out_ready"), S("tree_set")
    out_stored = [S(f"out_stored{s}") for s in range(2)]

    def wait(eng, sem, value):
        if not isinstance(value, int) or value > 0:
            eng.wait_ge(sem, value)

    def hold(eng, sem, value):
        if not isinstance(value, int) or value > 0:
            eng.wait_ge(sem, value)
            if not isinstance(value, int):
                eng.sem_inc(carried, 1)

    def leave(eng, n):
        eng.drain().then_inc(phase_left, 1)
        eng.wait_ge(phase_left, 5 * n)

    def bands(eng, tile):
        for hh in range(3):
            tile(hh, hh % 2, hh // 2, hh == 0, False)
        with eng.Fori(0, (GRID - 4) // 2) as j:
            tile(2 * j + 3, 1, j + 1, False, False)
            tile(2 * j + 4, 0, j + 2, False, False)
        tile(GRID - 1, 1, (GRID - 1) // 2, False, True)

    def batches(eng, step, lag, n=NBATCH):
        def peeled(i):
            step(i, i % 2, i // 2, lambda d: 0 <= i - d < n)

        first = 4
        pairs = (n - 1 - first) // 2
        for i in range(first):
            peeled(i)
        with eng.Fori(0, pairs) as j:
            for k in range(2):
                i = first + k
                step(2 * j + i, i % 2, j + i // 2, lambda d: True)
        for i in range(first + 2 * pairs, n + lag):
            peeled(i)

    def prepared(eng):
        eng.wait_ge(prep_dve, 3)
        eng.wait_ge(prep_pool, 3)
        eng.wait_ge(filter_stored, 16)
        eng.wait_ge(cls_stored, 16)

    def lay_out(eng, n, s, ww):
        slot = PATCH_SLOT[ww]
        back = next(d for d in range(1, GRID + 1) if PATCH_SLOT[(ww - d) % GRID] == slot)
        if not isinstance(n, int) or n >= back:
            hold(eng, xT_in_psum, n - back + 1) if eng is nc.gpsimd else eng.wait_ge(xT_in_psum, n - back + 1)
        at = LEAD - CH + PXF * ww
        return eng.tensor_copy(patch[slot][:, 0:PATF].rearrange("p (r f) -> p r f", f=RINGF),
                               band[s][:, :, at:at + RINGF])

    def place_weights(eng, odd):
        eng.wait_ge(prep_dve, 1)
        eng.wait_ge(cleared, 16)
        for i in range(PATCH):
            src = w_sc[8 * i:8 * i + 8, CH * NSHIFT * odd:CH * NSHIFT * (odd + 1), :].rearrange("p (s c) d -> p s (c d)", c=CH)
            dst = bass.AP(tensor=wscr.tensor, offset=(111 + i * RINGF + CH * odd) * DIM,
                          ap=[[2 * CH * DIM, 8], [COPY_GAP * DIM, NSHIFT], [1, CH * DIM]])
            eng.dma_start(dst, src).then_inc(scaled_stored, 16)

    def rep(row, n):
        return bass.AP(tensor=row.tensor, offset=row.offset, ap=[[0, n]] + [list(a) for a in row.ap])

    with nc.Block() as block:
        @block.sync
        def _(sp):
            sp.dma_start(w_nat[:, :, :], W.rearrange("(p k) d -> p k d", k=KROW)).then_inc(w_loaded, 16)
            sp.dma_start(gam[:, :], gamma.rearrange("(p k) -> p k", k=KROW)).then_inc(gb_loaded, 16)
            sp.dma_start(bet[:, :], beta.rearrange("(p k) -> p k", k=KROW)).then_inc(gb_loaded, 16)
            sp.dma_start(bias_row[:, :], rep(tok_b, 1)).then_inc(gb_loaded, 16)
            for dst, src in ((cnt[:, :], c_count),
                             (filt_w[0:FFREQ, :], w_filt), (filt_w[FFREQ:FFREQ + 1, :], rep(b_filt, 1)),
                             (filt_b[:, :], c_basis), (nodes[0:NODES, :], wn_in),
                             (nodes[NODES:NODEX, :], rep(wn_in[NODES - 1, :], NODEX - NODES)),
                             (cls_h[:, 0:DIM], rep(cls_tok[0, 0, :], 128))):
                sp.dma_start(dst, src).then_inc(tables_loaded, 16)
            sp.wait_ge(consts_set, 7)
            z = zeros[:, 0:600]
            sp.dma_start(wscr.rearrange("(p k) d -> p (k d)", p=120).rearrange("p (k f) -> p k f", f=600),
                         bass.AP(tensor=z.tensor, offset=z.offset, ap=[[z.ap[0][0], 120], [0, 16], [1, 600]])).then_inc(cleared, 16)
            sp.dma_start(band[0][:, 0, LEAD:LEAD + ROWF], zeros[:, :]).then_inc(ring_zeroed, 16)
            sp.wait_ge(ring_zeroed, 16)

            def load_band(hh, s, lo, hi):
                src = x.rearrange("b h w c -> b (h w c)")[:, bass.ds((PATCH * hh - 1 + lo) * ROWF, (hi - lo) * ROWF)]
                sp.dma_start(band[s][:, lo:hi, LEAD:LEAD + ROWF],
                             src.rearrange("b (r f) -> b r f", f=ROWF)).then_inc(band_loaded[s], 16)

            load_band(0, 0, 1, BAND)
            place_weights(sp, 0)
            sp.wait_ge(scaled_stored, 32 * PATCH)
            for s in range(NSHIFT):
                sp.dma_start(w_sh[:, s, :, :], wscr[COPY_AT[s]:COPY_AT[s] + 128 * NCHUNK, :].rearrange("(c p) d -> p c d", p=128))\
                    .then_inc(shifted_loaded, 16)
            sp.wait_ge(prep_dve, 2)
            sp.dma_start(filt_scr.rearrange("(h p) k -> p h k", p=HALF), filt_p[:, :, :]).then_inc(filter_stored, 16)
            sp.dma_start(h_scr[:, NTOK:PTOK, :], zeros[:, 0:(PTOK - NTOK) * HCOL].rearrange("p (l d) -> p l d", d=HCOL))\
                .then_inc(pads_stored, 16)
            sp.dma_start(short_scr[:, :, PTOK, :], zeros[0:HALF, 0:256].rearrange("p (h b) -> p h b", h=2))\
                .then_inc(pads_stored, 16)
            sp.wait_ge(prep_pool, 2)
            sp.dma_start(h_scr[:, 0, :], cls_h[:, :]).then_inc(cls_stored, 16)
            sp.dma_start(w_out_sb[0:HALF, :, :], w_out.rearrange("(h p) d -> p h d", p=HALF)).then_inc(small_loaded, 16)
            sp.dma_start(w_out_sb[HALF:HALF + 1, 1, :], rep(b_out, 1)).then_inc(small_loaded, 16)
            sp.dma_start(taps[:, :, :], w_short.rearrange("(h p) o k -> p h (o k)", p=HALF)).then_inc(small_loaded, 16)
            sp.dma_start(taps_b[:, :], b_short.rearrange("(h p) -> p h", p=HALF), allow_slow_non_contiguous=True).then_inc(small_loaded, 16)
            for q in range(QUAD):
                sp.dma_start(node_out[NODEX * q:NODEX * q + NODES, q, :], wn_out).then_inc(small_loaded, 16)
                sp.dma_start(node_out[NODEX * q + NODES:NODEX * (q + 1), q, :],
                             rep(wn_out[NODES - 1, :], NODEX - NODES)).then_inc(small_loaded, 16)
            sp.wait_ge(prep_dve, 3)
            sp.wait_ge(prep_pe, 4)
            sp.wait_ge(prep_pool, 3)

            def store_h(hh, s):
                sp.wait_ge(hstat_ready, hh + 1)
                sp.dma_start(h_scr[:, bass.ds(GRID * hh + 1, GRID), :], htile[s][:, :, :]).then_inc(h_stored[s], 16)

            def left_band(hh):
                hold(sp, patch_dve, (GRID - len(COPY_POOL)) * (hh - 1))
                hold(sp, patch_pool, len(COPY_POOL) * (hh - 1))

            load_band(1, 1, 0, BAND)
            with sp.Fori(0, (GRID - 4) // 2) as j:
                for k in range(2):
                    hh = 2 * j + 2 + k
                    left_band(hh)
                    hold(sp, edge_squared, 2 * (hh - 1))
                    sp.wait_ge(core_squared, GRID * (hh - 1))
                    load_band(hh, k, 0, BAND)
                    store_h(hh - 2, k)
            for hh in (GRID - 2, GRID - 1):
                s = hh % 2
                left_band(hh)
                hold(sp, edge_squared, 2 * (hh - 1))
                sp.wait_ge(core_squared, GRID * (hh - 1))
                if hh == GRID - 1:
                    sp.dma_start(band[s][:, BAND - 1, LEAD:LEAD + ROWF], zeros[:, :]).then_inc(ring_zeroed, 16)
                    sp.wait_ge(ring_zeroed, 32)
                    load_band(hh, s, 0, BAND - 1)
                else:
                    load_band(hh, s, 0, BAND)
                store_h(hh - 2, s)
            store_h(GRID - 2, 0)
            store_h(GRID - 1, 1)
            for s in range(2):
                sp.wait_ge(h_stored[s], 16 * GRID // 2)
            sp.wait_ge(pads_stored, 32)
            sp.wait_ge(cls_stored, 16)
            sp.wait_ge(filter_stored, 16)
            leave(sp, 1)

            sp.dma_start(win[0:HALF, :, :], w_in.rearrange("(h p) n -> p h n", p=HALF)).then_inc(win_loaded, 16)
            sp.dma_start(win[HALF:HALF + 1, 1, :], rep(b_in, 1)).then_inc(win_loaded, 16)

            def load_hin(i, s):
                sp.dma_start(hin[s][:, :, :], h_scr[:, bass.ds(QUAD * i, QUAD), :]).then_inc(hin_loaded[s], 16)

            load_hin(0, 0)

            def step2(i, s, turn, on):
                if on(0) and on(-1):
                    wait(sp, xn_ready, i)
                    load_hin(i + 1, 1 - s)
                if on(1):
                    b, p = i - 1, 1 - s
                    sp.wait_ge(short_ready, 2 * b + 2)
                    sp.dma_start(short_scr[:, :, bass.ds(QUAD * b, QUAD), :].rearrange("p h l b -> p h (l b)"),
                                 short[p][:, :, :]).then_inc(short_stored[p], 16)
                    for hf in range(2):
                        sp.wait_ge(proj_ready, 2 * b + hf + 1)
                        dst = proj_scr[bass.ds(QUAD * b, QUAD), hf * HALF:(hf + 1) * HALF, :]
                        sp.dma_start(dst.rearrange("l d b -> d l b"), proj[p][:, hf, :, :]).then_inc(proj_stored[p], 16)
                    sp.wait_ge(gate_ready, 2 * b + 2)
                    sp.dma_start(gate_scr[:, bass.ds(QUAD * b, QUAD), :], gate[p][:, :, :]).then_inc(gate_stored[p], 16)

            batches(sp, step2, 1)
            for s in range(2):
                n = NBATCH // 2
                sp.wait_ge(short_stored[s], 16 * n)
                sp.wait_ge(proj_stored[s], 32 * n)
                sp.wait_ge(gate_stored[s], 16 * n)
            leave(sp, 2)

            def load_group(g, s):
                sem = taps_loaded[s]
                win0 = bass.AP(tensor=filt_scr.tensor, offset=g * (CG * GPADW), ap=[[1, TAP0], [GPADW, CG], [1, HANK]])
                sp.dma_start(toep[s][:, :, :], win0).then_inc(sem, 16)
                sp.dma_start(src0[s][:, :, :], proj_scr[0:TAP0, bass.ds(g * CG, CG), :]).then_inc(sem, 16)
                sp.dma_start(src1[s][:, :, :], proj_scr[TAP0:PTOK, bass.ds(g * CG, CG), :]).then_inc(sem, 16)

            load_group(0, 0)
            load_group(1, 1)
            with sp.Fori(0, NGROUP // 2 - 1) as j:
                for s in range(2):
                    g = 2 * j + s
                    sp.wait_ge(conv_in_psum, 2 * g + 2)
                    load_group(g + 2, s)
            leave(sp, 3)

            def load4(i, s):
                sp.dma_start(gy[s][:, :, :], gate_scr[:, bass.ds(QUAD * i, QUAD), :]).then_inc(gy_loaded[s], 16)
                sp.dma_start(sh[s][:, :, :], short_scr[:, :, bass.ds(QUAD * i + 1, QUAD), :].rearrange("p h l b -> p h (l b)"))\
                    .then_inc(gy_loaded[s], 16)
                sp.dma_start(hb[s][:, :, :], h_scr[:, bass.ds(QUAD * i, QUAD), :]).then_inc(gy_loaded[s], 16)

            load4(0, 0)

            def step4(i, s, turn, on):
                if on(0) and on(-1):
                    wait(sp, yT_in_psum, 2 * i)
                    wait(sp, u_ready, 2 * i)
                    wait(sp, h2_ready, 2 * i)
                    load4(i + 1, 1 - s)
                if on(2):
                    b = i - 2
                    sp.wait_ge(out_ready, 2 * b + 2)
                    n = NTOK - QUAD * (NBATCH - 1) if isinstance(b, int) and b == NBATCH - 1 else QUAD
                    sp.dma_start(out[:, bass.ds(QUAD * b, n), :], ob[s][:, 0:n, :]).then_inc(out_stored[s], 16)

            batches(sp, step4, 2)
            for s in range(2):
                sp.wait_ge(out_stored[s], 16 * NBATCH // 2)

        @block.gpsimd
        def _(pool):
            nc.gpsimd.memset(ident[:, :], 0.0).then_inc(ident_set, 1)
            nc.gpsimd.memset(wf[:, :, :], 0.0).then_inc(prep_pool, 1)
            pool.wait_ge(ident_set, 1)
            nc.gpsimd.affine_select(out=ident[:, :], in_=ident[:, :], compare_op=ALU.not_equal, fill=1.0,
                                    base=0, pattern=[[-1, 128]], channel_multiplier=1).then_inc(ident_set, 1)
            pool.wait_ge(prep_dve, 2)
            pool.wait_ge(consts_set, 7)
            nc.gpsimd.tensor_tensor(cls_h[:, DIM + 1:HCOL], cls_v[:, :], half_neg[:, 0:1], ALU.pow).then_inc(prep_pool, 1)
            pool.wait_ge(prep_dve, 3)
            pool.wait_ge(prep_pe, 4)
            pool.wait_ge(scaled_stored, 32 * PATCH)
            nc.gpsimd.memset(band[1][:, :, 0:LEAD], 0.0)
            nc.gpsimd.memset(band[1][:, :, LEAD + ROWF:PITCH], 0.0)
            for s in range(3):
                nc.gpsimd.memset(patch[s][:, PATF:], 0.0)
            pool.drain().then_inc(prep_pool, 1)

            def rsqrt_tokens(hh, s):
                pool.wait_ge(tvar_ready, hh + 1)
                nc.gpsimd.tensor_tensor(trstd[s][:, :], tvar[:, :], half_neg[:, 0:GRID], ALU.pow).then_inc(trstd_ready, 1)

            def rsqrt_h(hh, s):
                hold(pool, h_ready, hh + 1)
                nc.gpsimd.tensor_scalar(hvar[:, :], htile[s][:, :, DIM + 1], LN_EPS, None, ALU.add).then_inc(pool_step, 1)
                pool.wait_ge(pool_step, hh + 1)
                nc.gpsimd.tensor_tensor(htile[s][:, :, DIM + 1], hvar[:, :], half_neg[:, 0:GRID], ALU.pow)\
                    .then_inc(hstat_ready, 1)

            def tile(hh, s, turn, first, last):
                if not first:
                    rsqrt_tokens(hh - 1, 1 - s)
                hold(pool, band_loaded[s], 16 * (turn + 1))
                for ww in COPY_POOL:
                    lay_out(nc.gpsimd, GRID * hh + ww, s, ww).then_inc(patch_pool, 1)
                if not first:
                    rsqrt_h(hh - 1, 1 - s)
                if last:
                    rsqrt_tokens(hh, s)
                    rsqrt_h(hh, s)

            bands(pool, tile)
            leave(pool, 1)

            nc.gpsimd.memset(xnT[0][:, :, 0:2, :], 0.0).then_inc(halo_ready, 1)
            for s in range(2):
                nc.gpsimd.memset(xn_hi[s][HALF:HALF + 1, 1, :].bitcast(F32), 1.0).then_inc(halo_ready, 1)
                nc.gpsimd.memset(xn_lo[s][HALF:HALF + 1, 1, :].bitcast(F32), 0.0).then_inc(halo_ready, 1)

            def step2(i, s, turn, on):
                if on(-1):
                    hold(pool, xnT_ready, 2 * i + 2)
                    hold(pool, short_ready, 2 * i)
                    nc.gpsimd.tensor_copy(xnT[1 - s][:, :, 0:2, :], xnT[s][:, :, QUAD:QUAD + 2, :]).then_inc(halo_ready, 1)

            batches(pool, step2, 0)
            leave(pool, 2)

            nc.gpsimd.memset(Y[:, NTOK:PTOK, :], 0.0).then_inc(y_padded, 1)
            leave(pool, 3)

            def step4(i, s, turn, on):
                if on(0):
                    pool.wait_ge(gy_loaded[s], 48 * (turn + 1))
                    nc.gpsimd.tensor_tensor(gy[s][:, :, :], gy[s][:, :, :], Y[:, bass.ds(QUAD * i, QUAD), :], ALU.mult)\
                        .then_inc(y_ready, 1)
                    pool.wait_ge(var_ready, i + 1)
                    nc.gpsimd.tensor_tensor(rstd4[s][:, :], var4[:, :], half_neg[:, 0:QUAD], ALU.pow).then_inc(rstd_ready, 1)

            batches(pool, step4, 0)

        @block.scalar
        def _(act_e):
            place_weights(act_e, 1)
            prepared(act_e)

            sq_core = ps[:, 6:8, :].rearrange("p k b -> p (k b)")[:, 0:PATCH * PXF].rearrange("p (r f) -> p r f", f=PXF)

            def tile(hh, s, turn, first, last):
                act_e.wait_ge(band_loaded[s], 16 * (turn + 1))
                for ww in range(GRID):
                    n = GRID * hh + ww
                    nfirst = first and ww < 2
                    act_e.wait_ge(xT_in_psum, n + 1)
                    if not nfirst:
                        act_e.wait_ge(tok_in_psum, n - 1)
                    k = 2 * (ww % 2)
                    nc.scalar.activation(xT_hi[ww % 2][:, :, :].rearrange("p c b -> p (c b)"),
                                         ps[:, k:k + 2, :].rearrange("p k b -> p (k b)"), ACT.Copy).then_inc(xT_hi_ready, 1)
                    if ww == 0 and not first:
                        wait(act_e, tvar_ready, hh - 1)
                    v = LEAD + PXF * ww
                    wait(act_e, core_squared, n)
                    nc.scalar.activation(sq_core, band[s][:, 1:1 + PATCH, v:v + PXF], ACT.Square,
                                         accum_out=core_sum[s][:, ww:ww + 1]).then_inc(core_squared, 1)
                    if ww == 2:
                        wait(act_e, edges_summed, 3 * hh)
                        rows = bass.AP(tensor=band[s][:, :, :].tensor, offset=band[s][:, 0, LEAD:LEAD + 1].offset,
                                       ap=[band[s][:, :, :].ap[0], [PATCH * PITCH, 2], [PITCH, 2], [1, ROWF]])
                        nc.scalar.activation(sq_rows[:, :, :, :], rows, ACT.Square).then_inc(edge_squared, 1)
                        cols = bass.AP(tensor=band[s][:, :, :].tensor, offset=band[s][:, 1, LEAD - CH:LEAD].offset,
                                       ap=[band[s][:, :, :].ap[0], [PXF, GRID + 1], [PITCH, PATCH], [1, 6]])
                        nc.scalar.activation(sq_cols[:, :, :, :], cols, ACT.Square).then_inc(edge_squared, 1)
                    if not (first and ww == 0):
                        copy_token(n - 1, s if ww else 1 - s, (ww - 1) % GRID, hh if ww else hh - 1, first)
                if last:
                    copy_token(GRID * GRID - 1, s, GRID - 1, hh, False)

            def copy_token(n, s, ww, hh, first):
                act_e.wait_ge(tok_in_psum, n + 1)
                if ww == 0 and not first:
                    wait(act_e, h_ready, hh - 1)
                nc.scalar.activation(praw[s][:, ww, :], ps[:, 4 + ww % 2, 0:WCOL], ACT.Copy).then_inc(tok_copied, 1)

            bands(act_e, tile)
            leave(act_e, 1)

            act_e.wait_ge(win_loaded, 32)
            nc.scalar.activation(win_hi[0:HALF, 0, :], win[0:HALF, 0, :], ACT.Copy).then_inc(win_his, 1)
            nc.scalar.activation(win_hi[:, 1, :], win[:, 1, :], ACT.Copy).then_inc(win_his, 1)

            def step2(i, s, turn, on):
                if on(0):
                    for hf in range(2):
                        act_e.wait_ge(xnT_in_psum, 2 * i + hf + 1)
                        if hf == 0 and not (isinstance(i, int) and i < 2):
                            act_e.wait_ge(short_ready, 2 * i - 2)
                            act_e.wait_ge(halo_ready, 5 + i - 1)
                            act_e.wait_ge(xn_lo_ready, 2 * i - 2)
                        nc.scalar.activation(xnT[s][:, hf, 2:2 + QUAD, :], ps[0:HALF, hf, :], ACT.Copy).then_inc(xnT_ready, 1)
                    for hf in range(2):
                        act_e.wait_ge(xnT_ready, 2 * i + hf + 1)
                        if hf == 0:
                            wait(act_e, proj_in_psum, 2 * i - 2)
                            wait(act_e, zv_in_psum, 6 * i - 6)
                        nc.scalar.activation(xn_hi[s][0:HALF, hf, :], xnT[s][:, hf, 2:2 + QUAD, :], ACT.Copy).then_inc(xn_hi_ready, 1)
                    act_e.wait_ge(halo_ready, 5 + i)
                    for hf in range(2):
                        if hf == 0:
                            wait(act_e, short_stored[s], 16 * turn)
                        nc.scalar.activation(short[s][:, hf, :], xnT[s][:, hf, 1:1 + QUAD, :], ACT.Identity,
                                             bias=taps_b[:, hf:hf + 1], scale=taps[:, hf, 1:2]).then_inc(centre_ready, 1)
                if on(1):
                    b, p = i - 1, 1 - s
                    for pr_ in range(2):
                        act_e.wait_ge(zv_in_psum, 6 * b + 3 * pr_ + 1)
                        nc.scalar.activation(silu[pr_][:, :, :], ps[:, 2 + 3 * pr_, 0:2 * DIM], ACT.Silu).then_inc(silu_ready, 1)
                        if pr_ == 0:
                            for hf in range(2):
                                act_e.wait_ge(proj_in_psum, 2 * b + hf + 1)
                                if hf == 0:
                                    wait(act_e, proj_stored[p], 32 * (turn - 1 if s == 0 else turn))
                                nc.scalar.activation(proj[p][:, hf, :, :], ps[0:HALF, hf, :], ACT.Copy).then_inc(proj_ready, 1)

            batches(act_e, step2, 1)
            leave(act_e, 2)

            with act_e.Fori(0, NGROUP // 2) as j:
                for s in range(2):
                    g = 2 * j + s
                    act_e.wait_ge(conv_in_psum, 2 * g + 1)
                    v = ps[:, 4 * s:4 * s + 2, 0:2 * NTOK].rearrange("p k (c l) -> p l k c", c=2)[:, ::-1, :, :]
                    dst = Y[:, 0:NTOK, bass.ds(CG * g, 4)].rearrange("p l (k c) -> p l k c", k=2)
                    nc.scalar.activation(dst, v, ACT.Copy).then_inc(conv_kept_act, 1)
            leave(act_e, 3)

            def step4(i, s, turn, on):
                if on(1):
                    b, p = i - 1, 1 - s
                    for hf in range(2):
                        act_e.wait_ge(h2T_in_psum, 2 * b + hf + 1)
                        if hf == 0:
                            wait(act_e, logit_in_psum, b)
                        nc.scalar.activation(h2T[:, hf, :], ps[0:HALF, hf, :], ACT.Copy).then_inc(h2T_ready, 1)
                    act_e.wait_ge(logit_ready, b + 1)
                    act_e.wait_ge(rstd_ready, b + 1)
                    wait(act_e, coef_ready, b)
                    for q in range(QUAD):
                        nc.scalar.activation(gel[:, q, :], logit[:, q, :], ACT.Gelu,
                                             scale=rstd4[p][:, q:q + 1]).then_inc(gel_ready, 1)
                    act_e.wait_ge(coefT_in_psum, b + 1)
                    wait(act_e, node_in_psum, 2 * b)
                    nc.scalar.activation(coefT[:, :], ps[:, 7, 2 * DIM:512], ACT.Copy).then_inc(coefT_ready, 1)

            batches(act_e, step4, 1)

        @block.vector
        def _(dve):
            count = [0]

            def own(ins):
                count[0] += 1
                ins.then_inc(dve_step, 1)
                dve.wait_ge(dve_step, count[0])

            for t, v in ((zeros[:, :], 0.0), (half_neg[:, :], -0.5), (ones[:, :], 1.0), (filt_p[:, :, :], 0.0),
                         (node_out[:, :, :], 0.0),
                         (band[0][:, :, 0:LEAD], 0.0), (band[0][:, :, LEAD + ROWF:PITCH], 0.0)):
                nc.vector.memset(t, v).then_inc(consts_set, 1)
            dve.wait_ge(w_loaded, 16)
            dve.wait_ge(gb_loaded, 48)
            nc.vector.tensor_tensor(w_sc[:, :, :], w_nat[:, :, :], gam[:, :].unsqueeze(2).to_broadcast([128, KROW, DIM]),
                                    ALU.mult).then_inc(prep_dve, 1)
            dve.wait_ge(tables_loaded, 16 * 7)
            own(nc.vector.tensor_reduce(node_m[:, :], nodes[:, :], AXIS.X, ALU.add))
            own(nc.vector.tensor_scalar(node_m[:, :], node_m[:, :], 1.0 / DIM, None, ALU.mult))
            own(nc.vector.tensor_scalar(nodes[:, :], nodes[:, :], node_m[:, 0:1], None, ALU.subtract))
            own(nc.vector.bn_stats(cls6[:, :], cls_h[:, 0:DIM]))
            own(nc.vector.bn_aggr(cls_h[:, DIM:HCOL], cls6[:, :]))
            own(nc.vector.tensor_scalar(cls_v[:, :], cls_h[:, DIM + 1:HCOL], LN_EPS, None, ALU.add))
            own(nc.vector.tensor_scalar(cnt_neg[:, :], cnt[:, :], -1.0, None, ALU.mult))
            dve.wait_ge(prep_pe, 1)
            for hf in range(2):
                own(nc.vector.tensor_copy(filt_p[:, hf, SPAD:SPAD + NTOK], ps[0:HALF, hf, 0:NTOK]))
                own(nc.vector.tensor_copy(node_inT[:, hf, :], ps[0:HALF, 2 + hf, 0:NODEX]))
            dve.drain().then_inc(prep_dve, 1)
            dve.wait_ge(prep_pe, 2)
            own(nc.vector.tensor_copy(csum[:, :], ps[:, 4, 0:DIM]))
            dve.wait_ge(prep_pe, 3)
            own(nc.vector.tensor_tensor(bias_row[:, :], ps[0:1, 5, 0:DIM], bias_row[:, :], ALU.add))
            dve.wait_ge(prep_pe, 4)
            own(nc.vector.tensor_copy(tok_bias[:, :], ps[:, 6, 0:DIM]))
            dve.wait_ge(shifted_loaded, 16 * NSHIFT)
            dve.wait_ge(prep_pool, 1)
            own(nc.vector.tensor_tensor(wf[:, :, 0:DIM], w_sh[:, 0, :, :], w_sh[:, 1, :, :], ALU.add))
            for s in range(2, NSHIFT):
                own(nc.vector.tensor_tensor(wf[:, :, 0:DIM], wf[:, :, 0:DIM], w_sh[:, s, :, :], ALU.add))
            for j in range(NCHUNK):
                own(nc.vector.scalar_tensor_tensor(wf[:, j, 0:DIM], csum[:, :], cnt_neg[:, j:j + 1], wf[:, j, 0:DIM],
                                                   ALU.mult, ALU.add))
            own(nc.vector.tensor_copy(wf[:, :, DIM], cnt[:, :]))
            own(nc.vector.tensor_copy(wf_hi[:, :, :], wf[:, :, :]))
            own(nc.vector.tensor_tensor(wf_lo[:, :, :], wf[:, :, :], wf_hi[:, :, :].bitcast(F32), ALU.subtract))
            dve.drain().then_inc(prep_dve, 1)

            chain = count[0]
            CHAIN = 9

            def dve_patch(hh, s, turn, ww):
                if ww == 0:
                    dve.wait_ge(band_loaded[s], 16 * (turn + 1))
                if ww not in COPY_POOL:
                    lay_out(nc.vector, GRID * hh + ww, s, ww).then_inc(patch_dve, 1)

            def tile(hh, s, turn, first, last):
                if first:
                    dve_patch(hh, s, turn, 0)
                for ww in range(GRID):
                    n = GRID * hh + ww
                    if ww + 1 < GRID:
                        dve_patch(hh, s, turn, ww + 1)
                    elif not last:
                        dve_patch(hh + 1, 1 - s, turn + s, 0)
                    dve.wait_ge(xT_hi_ready, n + 1)
                    if not (first and ww < 2):
                        dve.wait_ge(tok_in_psum, n - 1)
                    k = 2 * (ww % 2)
                    nc.vector.tensor_tensor(xT_lo[ww % 2][:, :, :].rearrange("p c b -> p (c b)"),
                                            ps[:, k:k + 2, :].rearrange("p k b -> p (k b)"),
                                            xT_hi[ww % 2][:, :, :].rearrange("p c b -> p (c b)").bitcast(F32),
                                            ALU.subtract).then_inc(xT_lo_ready, 1)
                    if ww == 4:
                        edge_sums(hh, s)
                    if not first:
                        finish(hh - 1, 1 - s, ww)
                if last:
                    for ww in range(GRID):
                        finish(hh, s, ww)

            def link(ins, hh, k):
                ins.then_inc(dve_step, 1)
                dve.wait_ge(dve_step, chain + CHAIN * hh + k + 1)

            def edge_sums(hh, s):
                dve.wait_ge(edge_squared, 2 * hh + 2)
                nc.vector.tensor_reduce(row_sum[:, :, :, :], sq_rows[:, :, :, :].rearrange("p a b (w f) -> p a b w f", f=PXF),
                                        AXIS.X, ALU.add).then_inc(edges_summed, 1)
                for side in range(2):
                    nc.vector.tensor_reduce(col_sum[:, side, :], sq_cols[:, :, :, CH * side:CH * side + CH],
                                            AXIS.XY, ALU.add).then_inc(edges_summed, 1)

            def finish(hh, s, ww):
                if ww == 0:
                    dve.wait_ge(core_squared, GRID * hh + GRID)
                    dve.wait_ge(edges_summed, 3 * hh + 3)
                    dve.wait_ge(tok_copied, GRID * hh + GRID)
                    link(nc.vector.tensor_tensor(sum_a[:, :], row_sum[:, 0, 0, :], row_sum[:, 0, 1, :], ALU.subtract), hh, 0)
                    link(nc.vector.tensor_tensor(sum_b[:, :], row_sum[:, 1, 1, :], row_sum[:, 1, 0, :], ALU.subtract), hh, 1)
                    link(nc.vector.tensor_tensor(col_dif[:, :], col_sum[:, 0, :], col_sum[:, 1, :], ALU.subtract), hh, 2)
                    link(nc.vector.tensor_tensor(sum_a[:, :], sum_a[:, :], sum_b[:, :], ALU.add), hh, 3)
                    link(nc.vector.tensor_tensor(sum_b[:, :], col_dif[:, 0:GRID], col_dif[:, 1:GRID + 1], ALU.subtract), hh, 4)
                    link(nc.vector.scalar_tensor_tensor(sum_a[:, :], core_sum[s][:, :], 5.0, sum_a[:, :], ALU.mult, ALU.add), hh, 5)
                    link(nc.vector.tensor_tensor(sum_a[:, :], sum_a[:, :], sum_b[:, :], ALU.add), hh, 6)
                    link(nc.vector.tensor_tensor(musq[:, :], praw[s][:, :, DIM], praw[s][:, :, DIM], ALU.mult), hh, 7)
                    link(nc.vector.scalar_tensor_tensor(sum_a[:, :], sum_a[:, :], 1.0 / NFEAT, musq[:, :], ALU.mult, ALU.subtract), hh, 8)
                    wait(dve, trstd_ready, hh)
                    nc.vector.tensor_scalar(tvar[:, :], sum_a[:, :], 0.0, TOK_EPS, ALU.max, ALU.add).then_inc(tvar_ready, 1)
                end = ww == GRID - 1
                if ww == 2:
                    dve.wait_ge(trstd_ready, hh + 1)
                    if not isinstance(hh, int) or hh >= 2:
                        dve.wait_ge(h_stored[s], 16 * slot_turn(hh, s))
                for w in FINISH[0][ww]:
                    nc.vector.scalar_tensor_tensor(htile[s][:, w, 0:DIM], praw[s][:, w, 0:DIM], trstd[s][:, w:w + 1],
                                                   tok_bias[:, :], ALU.mult, ALU.add).then_inc(h_made, 1)
                for w in FINISH[1][ww]:
                    dve.wait_ge(h_made, GRID * hh + w + 1)
                    nc.vector.bn_stats(bn6[:, w, :], htile[s][:, w, 0:DIM]).then_inc(bn_made, 1)
                if FINISH[2][ww]:
                    hold(dve, bn_made, GRID * hh + FINISH[2][ww][-1] + 1)
                for w in FINISH[2][ww]:
                    ins = nc.vector.bn_aggr(htile[s][:, w, DIM:HCOL], bn6[:, w, :])
                if end:
                    ins.then_inc(h_ready, 1)

            def slot_turn(hh, s):
                return hh // 2 if isinstance(hh, int) else turn_of[0]

            turn_of = [0]
            first_slice = [2 + 11 * w // GRID for w in range(GRID)]
            FINISH = [[[w for w in range(GRID) if min(first_slice[w] + d, GRID - 1) == ww] for ww in range(GRID)]
                      for d in range(3)]

            def tile_outer(hh, s, turn, first, last):
                turn_of[0] = turn if s == 1 else turn - 1
                tile(hh, s, turn, first, last)

            bands(dve, tile_outer)
            leave(dve, 1)

            for hf, parts in ((0, HALF), (1, HALF + 1)):
                dve.wait_ge(win_his, hf + 1)
                nc.vector.tensor_tensor(win_lo[0:parts, hf, :], win[0:parts, hf, :], win_hi[0:parts, hf, :].bitcast(F32),
                                        ALU.subtract).then_inc(win_split, 1)

            def norm(i, s, turn):
                dve.wait_ge(hin_loaded[s], 16 * (turn + 1))
                if not (isinstance(i, int) and i < 2):
                    dve.wait_ge(xnT_in_psum, 2 * (i - 1))
                for q in range(QUAD):
                    ins = nc.vector.tensor_scalar(xn[s][:, q, :], hin[s][:, q, 0:DIM], hin[s][:, q, DIM:DIM + 1],
                                                  hin[s][:, q, DIM + 1:HCOL], ALU.subtract, ALU.mult)
                ins.then_inc(xn_ready, 1)

            norm(0, 0, 0)
            steps2 = count[0]

            def step2(i, s, turn, on):
                if on(0):
                    if on(-1):
                        norm(i + 1, 1 - s, turn + (1 if s == 1 else 0))
                    for hf in range(2):
                        dve.wait_ge(xn_hi_ready, 2 * i + hf + 1)
                        if hf == 0:
                            wait(dve, proj_in_psum, 2 * i - 2)
                            wait(dve, zv_in_psum, 6 * i - 6)
                        nc.vector.tensor_tensor(xn_lo[s][0:HALF, hf, :], xnT[s][:, hf, 2:2 + QUAD, :].rearrange("p l b -> p (l b)"),
                                                xn_hi[s][0:HALF, hf, :].bitcast(F32), ALU.subtract).then_inc(xn_lo_ready, 1)
                    for hf in range(2):
                        dve.wait_ge(centre_ready, 2 * i + hf + 1)
                        nc.vector.scalar_tensor_tensor(short[s][:, hf, :], xnT[s][:, hf, 0:QUAD, :].rearrange("p l b -> p (l b)"),
                                                       taps[:, hf, 0:1], short[s][:, hf, :], ALU.mult, ALU.add).then_inc(left_ready, 1)
                    for hf in range(2):
                        dve.wait_ge(left_ready, 2 * i + hf + 1)
                        nc.vector.scalar_tensor_tensor(short[s][:, hf, :], xnT[s][:, hf, 2:2 + QUAD, :].rearrange("p l b -> p (l b)"),
                                                       taps[:, hf, 2:3], short[s][:, hf, :], ALU.mult, ALU.add).then_inc(short_ready, 1)
                if on(1):
                    b, p = i - 1, 1 - s
                    for pr_ in range(2):
                        dve.wait_ge(silu_ready, 2 * b + pr_ + 1)
                        dve.wait_ge(zv_in_psum, 6 * b + 3 * pr_ + 2)
                        nc.vector.tensor_tensor(szv[pr_][:, :, :], ps[:, 3 + 3 * pr_, 0:2 * DIM].rearrange("p (l d) -> p l d", l=2),
                                                silu[pr_][:, :, :], ALU.mult).then_inc(szv_ready, 1)
                        dve.wait_ge(szv_ready, 2 * b + pr_ + 1)
                        dve.wait_ge(zv_in_psum, 6 * b + 3 * pr_ + 3)
                        if pr_ == 0:
                            wait(dve, gate_stored[p], 16 * (turn - 1 if s == 0 else turn))
                        nc.vector.tensor_tensor(gate[p][:, 2 * pr_:2 * pr_ + 2, :],
                                                ps[:, 4 + 3 * pr_, 0:2 * DIM].rearrange("p (l d) -> p l d", l=2),
                                                szv[pr_][:, :, :], ALU.mult).then_inc(gate_ready, 1)

            left_ready, szv_ready = S("left_ready"), S("szv_ready")
            batches(dve, step2, 1)
            leave(dve, 2)

            with dve.Fori(0, NGROUP // 2) as j:
                for s in range(2):
                    g = 2 * j + s
                    dve.wait_ge(conv_in_psum, 2 * g + 2)
                    v = ps[:, 4 * s + 2:4 * s + 4, 0:2 * NTOK].rearrange("p k (c l) -> p l k c", c=2)[:, ::-1, :, :]
                    dst = Y[:, 0:NTOK, bass.ds(CG * g + 4, 4)].rearrange("p l (k c) -> p l k c", k=2)
                    nc.vector.tensor_copy(dst, v).then_inc(conv_kept_dve, 1)
            leave(dve, 3)

            nc.vector.memset(uT[HALF:HALF + 1, 1, :], 1.0).then_inc(tree_set, 1)
            nc.vector.memset(visit[:, :, :], 1.0).then_inc(tree_set, 1)
            nc.vector.memset(coef[:, :, :], 0.0).then_inc(tree_set, 1)
            dve.wait_ge(tree_set, 3)
            tree_step = S("tree_step")
            TREE = 9

            def tree(b):
                def link4(ins, k):
                    ins.then_inc(tree_step, 1)
                    dve.wait_ge(tree_step, TREE * b + k + 1)

                dve.wait_ge(logit_in_psum, b + 1)
                if not (isinstance(b, int) and b < 1):
                    dve.wait_ge(gel_ready, QUAD * b)
                nc.vector.tensor_copy(logit[:, :, :], ps[:, 6, 2 * DIM:512].rearrange("p (q n) -> p q n", q=QUAD))\
                    .then_inc(logit_ready, 1)
                dve.wait_ge(logit_ready, b + 1)
                nc.vector.tensor_scalar(branch[:, :, :, 0], logit[:, :, 0:INNER], 0.0, None, ALU.is_le).then_inc(tree_step, 1)
                link4(nc.vector.tensor_scalar(branch[:, :, :, 1], logit[:, :, 0:INNER], 0.0, None, ALU.is_gt), 1)
                p0 = 0
                for level in range(4):
                    n = 2 ** level
                    kids = visit[:, :, 2 * p0 + 1:2 * p0 + 1 + 2 * n].rearrange("p q (n c) -> p q n c", c=2)
                    link4(nc.vector.tensor_tensor(kids, branch[:, :, p0:p0 + n, :],
                                                  visit[:, :, p0:p0 + n].unsqueeze(3).to_broadcast([128, QUAD, n, 2]),
                                                  ALU.mult), 2 + level)
                    p0 += n
                dve.wait_ge(gel_ready, QUAD * (b + 1))
                link4(nc.vector.tensor_tensor(act[:, :, 0:NODEX - 1], visit[:, :, 0:NODEX - 1], gel[:, :, 0:NODEX - 1], ALU.mult), 6)
                wait(dve, coefT_in_psum, b)
                kids = coef[:, :, 1:NODEX - 1].rearrange("p q (n c) -> p q n c", c=2)
                link4(nc.vector.tensor_tensor(kids, branch[:, :, :, :],
                                              act[:, :, 0:INNER].unsqueeze(3).to_broadcast([128, QUAD, INNER, 2]), ALU.mult), 7)
                link4(nc.vector.tensor_reduce(tail[:, :], act[:, :, INNER:NODEX - 1], AXIS.X, ALU.add), 8)
                nc.vector.scalar_tensor_tensor(coef[:, :, NODEX - 1], gel[:, :, NODES - 1], 5.0, tail[:, :], ALU.mult, ALU.add)\
                    .then_inc(coef_ready, 1)

            def step4(i, s, turn, on):
                if on(2):
                    b = i - 2
                    for k in range(2):
                        dve.wait_ge(node_in_psum, 2 * b + k + 1)
                        if k == 0:
                            wait(dve, out_stored[s], 16 * (turn - 1))
                        nc.vector.tensor_tensor(ob[s][:, 2 * k:2 * k + 2, :],
                                                ps[:, 6 + k, 0:2 * DIM].rearrange("p (l d) -> p l d", l=2),
                                                h2[s][:, 2 * k:2 * k + 2, :], ALU.add).then_inc(out_ready, 1)
                if on(0):
                    dve.wait_ge(gy_loaded[s], 48 * (turn + 1))
                    for hf in range(2):
                        dve.wait_ge(yT_in_psum, 2 * i + hf + 1)
                        if hf == 0:
                            wait(dve, mix_in_psum, 2 * i)
                        nc.vector.tensor_tensor(uT[0:HALF, hf, :], ps[0:HALF, 2 + hf, :], sh[s][:, hf, :], ALU.add)\
                            .then_inc(u_ready, 1)
                if on(1):
                    tree(i - 1)
                if on(0):
                    for k in range(2):
                        dve.wait_ge(mix_in_psum, 2 * i + k + 1)
                        if k == 0 and not (isinstance(i, int) and i < 2):
                            dve.wait_ge(out_ready, 2 * i - 2)
                            dve.wait_ge(h2T_in_psum, 2 * i - 2)
                        nc.vector.tensor_tensor(h2[s][:, 2 * k:2 * k + 2, :],
                                                ps[:, 4 + k, 0:2 * DIM].rearrange("p (l d) -> p l d", l=2),
                                                hb[s][:, 2 * k:2 * k + 2, 0:DIM], ALU.add).then_inc(h2_ready, 1)
                    dve.wait_ge(h2_ready, 2 * i + 2)
                    for q in range(QUAD):
                        ins = nc.vector.bn_stats(bn4[:, q, :], h2[s][:, q, :])
                    ins.then_inc(stat_step, 1)
                    hold(dve, stat_step, 2 * i + 1)
                    for q in range(QUAD):
                        ins = nc.vector.bn_aggr(mv4[:, q, :], bn4[:, q, :])
                    ins.then_inc(stat_step, 1)
                    dve.wait_ge(stat_step, 2 * i + 2)
                    wait(dve, rstd_ready, i)
                    nc.vector.tensor_scalar(var4[:, :], mv4[:, :, 1], LN_EPS, None, ALU.add).then_inc(var_ready, 1)

            stat_step = S("stat_step")
            batches(dve, step4, 2)

        @block.tensor
        def _(pe):
            pe.wait_ge(ident_set, 2)
            pe.wait_ge(tables_loaded, 16 * 7)
            pe.wait_ge(dve_step, 3)
            for hf in range(2):
                nc.tensor.matmul(ps[0:HALF, hf, 0:NTOK], filt_w[:, hf * HALF:(hf + 1) * HALF], filt_b[:, :], start=True, stop=True)
                last = nc.tensor.transpose(ps[0:HALF, 2 + hf, 0:NODEX], nodes[:, hf * HALF:(hf + 1) * HALF], ident[0:NODEX, 0:NODEX])
            last.then_inc(prep_pe, 1)
            pe.wait_ge(prep_dve, 1)
            pe.wait_ge(consts_set, 7)
            for k in range(KROW):
                last = nc.tensor.matmul(ps[:, 4, 0:DIM], ones[:, :], w_sc[:, k, :], start=(k == 0), stop=(k == KROW - 1))
            last.then_inc(prep_pe, 1)
            for k in range(KROW):
                last = nc.tensor.matmul(ps[0:1, 5, 0:DIM], bet[:, k:k + 1], w_nat[:, k, :], start=(k == 0), stop=(k == KROW - 1))
            last.then_inc(prep_pe, 1)
            pe.wait_ge(dve_step, BIAS_STEP)
            nc.tensor.matmul(ps[:, 6, 0:DIM], ones[0:1, :], bias_row[:, :], start=True, stop=True).then_inc(prep_pe, 1)

            def transposes(n, s, ww, hh, first):
                own = GRID - len(COPY_POOL)
                if ww in COPY_POOL:
                    pe.wait_ge(patch_pool, len(COPY_POOL) * hh + COPY_POOL.index(ww) + 1)
                else:
                    pe.wait_ge(patch_dve, own * hh + ww - sum(v < ww for v in COPY_POOL) + 1)
                if not (first and ww < 2):
                    pe.wait_ge(xT_lo_ready, n - 1)
                for c in range(NCHUNK):
                    last = nc.tensor.transpose(ps[:, 2 * (ww % 2) + c // 4, 128 * (c % 4):128 * (c % 4) + 128],
                                               patch[PATCH_SLOT[ww]][:, 128 * c:128 * c + 128], ident[:, :])
                last.then_inc(xT_in_psum, 1)

            def products(n, w, first):
                o = ps[:, 4 + w % 2, 0:WCOL]
                if not (first and w < 2):
                    pe.wait_ge(tok_copied, n - 1)
                hi, lo = xT_hi[w % 2], xT_lo[w % 2]
                pe.wait_ge(xT_hi_ready, n + 1)
                for c in range(NCHUNK):
                    nc.tensor.matmul(o, hi[:, c, :], wf_hi[:, c, :], start=(c == 0), stop=False)
                    nc.tensor.matmul(o, hi[:, c, :], wf_lo[:, c, :], start=False, stop=False)
                pe.wait_ge(xT_lo_ready, n + 1)
                for c in range(NCHUNK):
                    last = nc.tensor.matmul(o, lo[:, c, :], wf_hi[:, c, :], start=False, stop=(c == NCHUNK - 1))
                last.then_inc(tok_in_psum, 1)

            prepared(pe)

            def tile(hh, s, turn, first, last_band):
                for ww in range(GRID):
                    n = GRID * hh + ww
                    transposes(n, s, ww, hh, first)
                    if not (first and ww == 0):
                        products(n - 1, (ww - 1) % GRID, first)
                if last_band:
                    products(GRID * GRID - 1, GRID - 1, False)

            bands(pe, tile)
            leave(pe, 1)

            pe.wait_ge(win_split, 2)
            pe.wait_ge(halo_ready, 5)
            K = (HALF, HALF + 1)

            def split3(o, lhs, rhs, hf_list=(0, 1)):
                for hf in hf_list:
                    (ah, al), (bh, bl) = lhs(hf), rhs(hf)
                    nc.tensor.matmul(o, ah, bh, start=(hf == 0), stop=False)
                    nc.tensor.matmul(o, ah, bl, start=False, stop=False)
                    last = nc.tensor.matmul(o, al, bh, start=False, stop=(hf == 1))
                return last

            def step2(i, s, turn, on):
                if on(0):
                    pe.wait_ge(xn_ready, i + 1)
                    for hf in range(2):
                        if isinstance(i, int) and i == 1:
                            pe.wait_ge(xnT_ready, hf + 1)
                        elif not isinstance(i, int) or i >= 2:
                            pe.wait_ge(proj_ready, 2 * (i - 2) + hf + 1)
                        for q in range(QUAD):
                            last = nc.tensor.transpose(ps[0:HALF, hf, 128 * q:128 * q + 128],
                                                       xn[s][:, q, hf * HALF:(hf + 1) * HALF], ident[:, :])
                        last.then_inc(xnT_in_psum, 1)
                if on(1):
                    b, p = i - 1, 1 - s

                    def tok(q):
                        return lambda hf: (xn_hi[p][0:K[hf], hf, 128 * q:128 * q + 128], xn_lo[p][0:K[hf], hf, 128 * q:128 * q + 128])

                    pe.wait_ge(xn_hi_ready, 2 * b + 2)
                    pe.wait_ge(xn_lo_ready, 2 * b + 2)
                    for pr_ in range(2):
                        wait(pe, gate_ready, 2 * (b - 1) + pr_ + 1 if not isinstance(b, int) or b >= 1 else 0)
                        for part in range(3):
                            for q in range(2):
                                c0 = (part + 1) * DIM
                                last = split3(ps[:, 2 + 3 * pr_ + part, DIM * q:DIM * q + DIM], tok(2 * pr_ + q),
                                              lambda hf: (win_hi[0:K[hf], hf, c0:c0 + DIM], win_lo[0:K[hf], hf, c0:c0 + DIM]))
                            last.then_inc(zv_in_psum, 1)
                        if pr_ == 0:
                            for mh in range(2):
                                if on(0):
                                    pe.wait_ge(xnT_ready, 2 * i + mh + 1)
                                else:
                                    pe.wait_ge(proj_ready, 2 * b - 1 + mh)
                                last = split3(ps[0:HALF, mh, :],
                                              lambda hf: (win_hi[0:K[hf], hf, mh * HALF:(mh + 1) * HALF],
                                                          win_lo[0:K[hf], hf, mh * HALF:(mh + 1) * HALF]),
                                              lambda hf: (xn_hi[p][0:K[hf], hf, :], xn_lo[p][0:K[hf], hf, :]))
                                last.then_inc(proj_in_psum, 1)

            batches(pe, step2, 1)
            leave(pe, 2)

            def convolve(g, s, turn, first):
                pe.wait_ge(taps_loaded[s], 48 * (turn + 1))
                for c in range(CG):
                    if c == 0 and not first:
                        pe.wait_ge(conv_kept_act, g - 1)
                    if c == CG // 2 and not first:
                        pe.wait_ge(conv_kept_dve, g - 1)
                    o = ps[:, 4 * s + c // 2, NTOK * (c % 2):NTOK * (c % 2) + NTOK]
                    nc.tensor.matmul(o, src0[s][:, c, :], toep[s][:, c, 0:NTOK], start=True, stop=False)
                    last = nc.tensor.matmul(o, src1[s][0:TAP1, c, :], toep[s][0:TAP1, c, TAP0:TAP0 + NTOK], start=False, stop=True)
                    if c % 4 == 3:
                        last.then_inc(conv_in_psum, 1)

            convolve(0, 0, 0, True)
            convolve(1, 1, 0, True)
            with pe.Fori(0, NGROUP // 2 - 1) as j:
                for s in range(2):
                    convolve(2 * j + 2 + s, s, j + 1, False)
            leave(pe, 3)

            pe.wait_ge(small_loaded, 16 * (4 + 2 * QUAD))
            pe.wait_ge(tree_set, 3)

            def step4(i, s, turn, on):
                if on(1):
                    b, p = i - 1, 1 - s
                    pe.wait_ge(h2_ready, 2 * b + 2)
                    wait(pe, h2T_ready, 2 * b)
                    for hf in range(2):
                        for q in range(QUAD):
                            last = nc.tensor.transpose(ps[0:HALF, hf, 128 * q:128 * q + 128],
                                                       h2[p][:, q, hf * HALF:(hf + 1) * HALF], ident[:, :])
                        last.then_inc(h2T_in_psum, 1)
                if on(2):
                    b = i - 2
                    pe.wait_ge(coefT_ready, b + 1)
                    pe.wait_ge(logit_ready, b + 1)
                    for k in range(2):
                        nc.tensor.matmul(ps[:, 6 + k, 0:2 * DIM], coefT[:, :],
                                         node_out[:, 2 * k:2 * k + 2, :].rearrange("p l d -> p (l d)"), start=True, stop=True)\
                            .then_inc(node_in_psum, 1)
                if on(0):
                    pe.wait_ge(y_ready, i + 1)
                    for hf in range(2):
                        wait(pe, u_ready, 2 * i - 1 + hf if not isinstance(i, int) or i >= 1 else 0)
                        for q in range(QUAD):
                            last = nc.tensor.transpose(ps[0:HALF, 2 + hf, 128 * q:128 * q + 128],
                                                       gy[s][:, q, hf * HALF:(hf + 1) * HALF], ident[:, :])
                        last.then_inc(yT_in_psum, 1)
                if on(1):
                    b = i - 1
                    pe.wait_ge(h2T_ready, 2 * b + 2)
                    wait(pe, out_ready, 2 * b)
                    for q in range(QUAD):
                        for hf in range(2):
                            last = nc.tensor.matmul(ps[:, 6, 2 * DIM + NODEX * q:2 * DIM + NODEX * q + NODEX],
                                                    h2T[:, hf, 128 * q:128 * q + 128], node_inT[:, hf, :],
                                                    start=(hf == 0), stop=(hf == 1))
                    last.then_inc(logit_in_psum, 1)
                if on(0):
                    pe.wait_ge(u_ready, 2 * i + 2)
                    for k in range(2):
                        wait(pe, h2_ready, 2 * i - 1 + k if not isinstance(i, int) or i >= 1 else 0)
                        for q in range(2):
                            for hf in range(2):
                                kk = K[hf]
                                last = nc.tensor.matmul(ps[:, 4 + k, DIM * q:DIM * q + DIM],
                                                        uT[0:kk, hf, 128 * (2 * k + q):128 * (2 * k + q) + 128],
                                                        w_out_sb[0:kk, hf, :], start=(hf == 0), stop=(hf == 1))
                        last.then_inc(mix_in_psum, 1)
                if on(1):
                    b = i - 1
                    pe.wait_ge(coef_ready, b + 1)
                    nc.tensor.transpose(ps[:, 7, 2 * DIM:512], coef[:, :, :].rearrange("p q n -> p (q n)"), ident[:, :])\
                        .then_inc(coefT_in_psum, 1)

            batches(pe, step4, 2)


NAMES = ["x", "cls_tok", "L0_tok_gamma", "L0_tok_beta", "L0_tok_W", "L0_tok_b", "L0_attn_w_in", "L0_attn_b_in",
         "L0_attn_w_filt", "L0_attn_b_filt", "L0_attn_w_short", "L0_attn_b_short", "L0_attn_w_out", "L0_attn_b_out",
         "L0_ffn_weights_in", "L0_ffn_weights_out"]


def kernel(**inputs):
    import concourse.bacc as bacc
    from concourse.bass_utils import run_bass_kernel_spmd

    nc = bacc.Bacc("TRN2", target_bir_lowering=False, num_devices=1)
    arrays = {n: np.ascontiguousarray(inputs[n]) for n in NAMES}
    arrays.update(constants())
    args = [nc.dram_tensor(f"in_{n}", a.shape, F32, kind="ExternalInput").ap() for n, a in arrays.items()]
    result = nc.dram_tensor("out_0", (NIMG, NTOK, DIM), F32, kind="ExternalOutput").ap()
    build(nc, *args, result)
    r = run_bass_kernel_spmd(nc, [{f"in_{n}": a for n, a in arrays.items()}], core_ids=[0])
    return r.results[0]["out_0"]
```

```python
import numpy as np
import concourse.bass as bass
from concourse import mybir

F32 = mybir.dt.float32
F32R = mybir.dt.float32r
ALU = mybir.AluOpType
ACT = mybir.ActivationFunctionType
AXIS = mybir.AxisListType

NIMG, IMG, CH, PATCH, DIM = 128, 224, 3, 16, 192
GRID = IMG // PATCH
NTOK = GRID * GRID + 1
QUAD = 4
NBATCH = -(-NTOK // QUAD)
PTOK = NBATCH * QUAD
HALF = DIM // 2
ROWF = IMG * CH
LEAD, PITCH = 4, 680
BAND = PATCH + 2
PXF = PATCH * CH
NFEAT = PATCH * PATCH * 5 * CH
NSHIFT = 5
RINGF = PXF + 2 * CH
PATF = BAND * RINGF
NCHUNK = 8
COPY_POOL = (3, 8, 13)
PATCH_SLOT = [2 if w in COPY_POOL else (w - sum(v < w for v in COPY_POOL)) % 2 for w in range(GRID)]
WCOL = DIM + 2
KROW = NFEAT // 128
HCOL = DIM + 3
SPAD = NTOK // 2
TAP0 = 112
TAP1 = NTOK - TAP0
TAP1L = PTOK - TAP0
HANK = TAP0 + NTOK
GPADW = 424
CG = 8
NGROUP = DIM // CG
FFREQ = 64
NODES, NODEX = 21, 32
DIMN = DIM + NODEX
INNER = 15
TOK_EPS, LN_EPS = 1e-3, 1e-5
PIXEL_OF = ((0, 0), (0, -1), (0, 1), (-1, 0), (1, 0))

COPY_GAP = 1200
COPY_AT = [s * COPY_GAP + 111 - (di + 1) * RINGF - (dj + 1) * CH for s, (di, dj) in enumerate(PIXEL_OF)]


def constants():
    t = np.arange(NTOK, dtype=np.float64)[None, :]
    f = np.arange(FFREQ, dtype=np.float64)[:, None]
    basis = np.ones((FFREQ + 1, NTOK), np.float32)
    basis[:FFREQ] = np.sin(t * f / FFREQ)
    count = np.zeros((NCHUNK * 128, 1), np.float32)
    for di, dj in PIXEL_OF:
        for i in range(PATCH):
            at = (i + di + 1) * RINGF + (dj + 1) * CH
            count[at:at + PXF] += 1
    count = count.reshape(NCHUNK, 128).T
    return {"c_basis": basis, "c_count": count / np.float32(NFEAT)}


def build(nc, x, cls_tok, gamma, beta, W, tok_b, w_in, b_in, w_filt, b_filt, w_short, b_short,
          w_out, b_out, wn_in, wn_out, c_basis, c_count, out):
    def dram(name, shape):
        return nc.dram_tensor(name, shape, F32, kind="Internal").ap()

    wscr = dram("placed_weights", [NSHIFT * COPY_GAP, DIM])
    filt_scr = dram("padded_filter", [DIM, GPADW])
    h_scr = dram("h_tokens", [NIMG, PTOK, HCOL])
    gate_scr = dram("gates", [NIMG, PTOK, DIMN])
    proj_scr = dram("x_proj", [PTOK, DIM, NIMG])
    short_scr = dram("x_short", [HALF, 2, PTOK + 4, NIMG])

    class Region:
        def __init__(self, start):
            self.at = start

        def take(self, name, shape, dt=F32):
            size = 4 * int(np.prod(shape[1:]))
            t = nc.alloc_sbuf_tensor_at(name, shape, dt, offset=self.at)
            self.at += -(-size // 32) * 32
            return t

    base = -(-nc.sbuf_base // 32) * 32
    fixed = Region(base)
    ident = fixed.take("ident", [128, 128])
    zeros = fixed.take("zeros", [128, ROWF])
    w_out_sb = fixed.take("w_out_sb", [HALF + 1, 2, DIMN])
    node_out = fixed.take("node_out", [128, QUAD, DIM])
    node_inT = fixed.take("node_inT", [HALF, 2, NODEX])
    taps = fixed.take("taps", [HALF, 2, 3])
    taps_b = fixed.take("taps_b", [HALF, 2])
    half_neg = fixed.take("half_neg", [128, 16])
    big = fixed.at

    r1 = Region(big)
    band = [r1.take(f"band{s}", [128, BAND, PITCH]) for s in range(2)]
    wf_hi = r1.take("wf_hi", [128, NCHUNK, WCOL], F32R)
    wf_lo = r1.take("wf_lo", [128, NCHUNK, WCOL], F32R)
    xT_hi = [r1.take(f"xT_hi{s}", [128, NCHUNK, 128], F32R) for s in range(2)]
    xT_lo = [r1.take(f"xT_lo{s}", [128, NCHUNK, 128], F32R) for s in range(2)]
    praw = [r1.take(f"praw{s}", [128, GRID, WCOL]) for s in range(2)]
    htile = [r1.take(f"htile{s}", [128, GRID, HCOL]) for s in range(2)]
    prep_end = r1.at
    patch = [r1.take(f"patch{s}", [128, NCHUNK * 128]) for s in range(3)]
    sq_rows = r1.take("sq_rows", [128, 2, 2, ROWF])
    sq_cols = r1.take("sq_cols", [128, GRID + 1, PATCH, 6])
    tok_bias = r1.take("tok_bias", [128, DIM])
    core_sum = [r1.take(f"core_sum{s}", [128, GRID]) for s in range(2)]
    row_sum = r1.take("row_sum", [128, 2, 2, GRID])
    col_sum = r1.take("col_sum", [128, 2, GRID + 1])
    col_dif = r1.take("col_dif", [128, GRID + 1])
    sum_a = r1.take("sum_a", [128, GRID])
    sum_b = r1.take("sum_b", [128, GRID])
    musq = r1.take("musq", [128, GRID])
    tvar = r1.take("tvar", [128, GRID])
    trstd = [r1.take(f"trstd{s}", [128, GRID]) for s in range(2)]
    bn6 = r1.take("bn6", [128, GRID, 6])
    hvar = r1.take("hvar", [128, GRID])
    pr = Region(big + 4 * BAND * PITCH)
    w_nat = pr.take("w_nat", [128, KROW, DIM])
    w_sc = pr.take("w_scaled", [128, KROW, DIM])
    pr2 = Region(big + 8 * BAND * PITCH + 8 * NCHUNK * WCOL)
    w_sh = pr2.take("w_shown", [128, NSHIFT, NCHUNK, DIM])
    wf = pr2.take("wf", [128, NCHUNK, WCOL])
    gam = pr2.take("gam", [128, KROW])
    bet = pr2.take("bet", [128, KROW])
    ones = pr2.take("ones", [128, 128])
    csum = pr2.take("csum", [128, DIM])
    bias_row = pr2.take("bias_row", [1, DIM])
    cnt = pr2.take("cnt", [128, NCHUNK])
    cnt_neg = pr2.take("cnt_neg", [128, NCHUNK])
    filt_w = pr2.take("filt_w", [FFREQ + 1, DIM])
    filt_b = pr2.take("filt_basis", [FFREQ + 1, NTOK])
    filt_p = pr2.take("filt_pad", [HALF, 2, GPADW])
    nodes = pr2.take("nodes", [NODEX, DIM])
    node_m = pr2.take("node_mean", [NODEX, 1])
    cls_h = pr2.take("cls_h", [128, HCOL])
    cls6 = pr2.take("cls6", [128, 6])
    cls_v = pr2.take("cls_v", [128, 1])

    r2 = Region(big)
    win = r2.take("win", [HALF + 1, 2, 3 * DIM + DIMN])
    win_hi = r2.take("win_hi", [HALF + 1, 2, 3 * DIM + DIMN], F32R)
    win_lo = r2.take("win_lo", [HALF + 1, 2, 3 * DIM + DIMN], F32R)
    hin = [r2.take(f"hin{s}", [128, QUAD, HCOL]) for s in range(2)]
    xn = [r2.take(f"xn{s}", [128, QUAD, DIM]) for s in range(2)]
    xnT = [r2.take(f"xnT{s}", [HALF, 2, QUAD + 2, 128]) for s in range(2)]
    xn_hi = [r2.take(f"xn_hi{s}", [HALF + 1, 2, QUAD * 128], F32R) for s in range(2)]
    xn_lo = [r2.take(f"xn_lo{s}", [HALF + 1, 2, QUAD * 128], F32R) for s in range(2)]
    silu = [r2.take(f"silu{p}", [128, 2, DIM]) for p in range(2)]
    szv = [r2.take(f"szv{p}", [128, 2, DIMN]) for p in range(2)]
    gate = [r2.take(f"gate{s}", [128, QUAD, DIMN]) for s in range(2)]
    short = [r2.take(f"short{s}", [HALF, 2, QUAD * 128]) for s in range(2)]
    proj = [r2.take(f"proj{s}", [HALF, 2, QUAD, 128]) for s in range(2)]

    woT = zeros[0:HALF, 0:2 * (DIM + 1)].rearrange("p (h k) -> p h k", h=2)

    r3 = Region(big)
    Y = r3.take("Y", [128, PTOK, DIM])
    after_y = r3.at
    src0 = [r3.take(f"src0_{s}", [TAP0, CG, 128]) for s in range(2)]
    src1 = [r3.take(f"src1_{s}", [TAP1L, CG, 128]) for s in range(2)]
    toep = [r3.take(f"toep{s}", [TAP0, CG, HANK]) for s in range(2)]

    r4 = Region(after_y)
    gy = [r4.take(f"gy{s}", [128, QUAD, DIMN]) for s in range(2)]
    lgh = [r4.take(f"lgh{s}", [128, QUAD, NODEX]) for s in range(2)]
    sh = [r4.take(f"sh{s}", [HALF, 2, QUAD * 128]) for s in range(2)]
    hb = [r4.take(f"hb{s}", [128, QUAD, HCOL]) for s in range(2)]
    h2 = [r4.take(f"h2_{s}", [128, QUAD, DIM]) for s in range(2)]
    ob = [r4.take(f"ob{s}", [128, QUAD, DIM]) for s in range(2)]
    uT = [r4.take(f"uT{s}", [HALF + 1, 2, QUAD * 128]) for s in range(2)]
    bn4 = r4.take("bn4", [128, QUAD, 6])
    mv4 = r4.take("mv4", [128, QUAD, 2])
    var4 = r4.take("var4", [128, QUAD])
    rstd4 = [r4.take(f"rstd4_{s}", [128, QUAD]) for s in range(2)]
    logit = r4.take("logit", [128, QUAD, NODEX])
    gel = r4.take("gel", [128, QUAD, NODEX])
    branch = r4.take("branch", [128, QUAD, INNER, 2])
    visit = r4.take("visit", [128, QUAD, NODEX])
    act = r4.take("act", [128, QUAD, NODEX])
    coef = r4.take("coef", [128, QUAD, NODEX])
    tail = r4.take("tail", [128, QUAD])
    coefT = r4.take("coefT", [128, 128])
    assert max(r1.at, r2.at, r3.at, r4.at) <= nc.sbuf_usable_end, (r1.at, r2.at, r3.at, r4.at)
    assert pr.at <= big + 8 * BAND * PITCH and pr2.at <= prep_end, (pr.at, pr2.at, prep_end)

    ps = nc.alloc_psum_tensor("psum", [128, 8, 512], F32)

    S = nc.alloc_semaphore

    BIAS_STEP = 13
    carried = S("carried")
    phase_left = S("phase_left")
    w_loaded, gb_loaded, tables_loaded, small_loaded = S("w_loaded"), S("gb_loaded"), S("tables_loaded"), S("small_loaded")
    consts_set, ident_set, cls_step = S("consts_set"), S("ident_set"), S("cls_step")
    prep_dve, prep_pe, prep_pool = S("prep_dve"), S("prep_pe"), S("prep_pool")
    cleared = S("cleared")
    scaled_stored, filter_stored, shifted_loaded = S("scaled_stored"), S("filter_stored"), S("shifted_loaded")
    pads_stored, cls_stored = S("pads_stored"), S("cls_stored")
    band_loaded = [S(f"band_loaded{s}") for s in range(2)]
    ring_zeroed = S("ring_zeroed")
    patch_dve, patch_pool = S("patch_dve"), S("patch_pool")
    xT_in_psum, xT_hi_ready, xT_lo_ready = S("xT_in_psum"), S("xT_hi_ready"), S("xT_lo_ready")
    tok_in_psum, tok_copied = S("tok_in_psum"), S("tok_copied")
    core_squared, edge_squared, edges_summed = S("core_squared"), S("edge_squared"), S("edges_summed")
    tvar_ready, trstd_ready, h_ready, hstat_ready = S("tvar_ready"), S("trstd_ready"), S("h_ready"), S("hstat_ready")
    h_stored = [S(f"h_stored{s}") for s in range(2)]
    h_made, bn_made = S("h_made"), S("bn_made")
    dve_step = S("dve_step")
    pool_step = S("pool_step")
    win_loaded, win_split, win_his, win_nodes = S("win_loaded"), S("win_split"), S("win_his"), S("win_nodes")
    hin_loaded = [S(f"hin_loaded{s}") for s in range(2)]
    xn_ready, xnT_in_psum, xnT_ready, xn_hi_ready, xn_lo_ready = (
        S("xn_ready"), S("xnT_in_psum"), S("xnT_ready"), S("xn_hi_ready"), S("xn_lo_ready"))
    ones_set = S("ones_set")
    halo_ready, centre_ready, short_ready = S("halo_ready"), S("centre_ready"), S("short_ready")
    zv_in_psum, silu_ready, gate_ready = S("zv_in_psum"), S("silu_ready"), S("gate_ready")
    proj_in_psum, proj_ready = S("proj_in_psum"), S("proj_ready")
    gate_stored = [S(f"gate_stored{s}") for s in range(2)]
    short_stored = [S(f"short_stored{s}") for s in range(2)]
    proj_stored = [S(f"proj_stored{s}") for s in range(2)]
    taps_loaded = [S(f"taps_loaded{s}") for s in range(2)]
    conv_in_psum, conv_kept_act, conv_kept_dve, y_padded = (
        S("conv_in_psum"), S("conv_kept_act"), S("conv_kept_dve"), S("y_padded"))
    gy_loaded = [S(f"gy_loaded{s}") for s in range(2)]
    hb_loaded = [S(f"hb_loaded{s}") for s in range(2)]
    wo_turned, wo_copied, wo_nodes = S("wo_turned"), S("wo_copied"), S("wo_nodes")
    y_ready, yT_in_psum, u_ready, mix_in_psum, h2_ready = (
        S("y_ready"), S("yT_in_psum"), S("u_ready"), S("mix_in_psum"), S("h2_ready"))
    var_ready, rstd_ready = S("var_ready"), S("rstd_ready")
    lgh_ready, logit_ready = S("lgh_ready"), S("logit_ready")
    gel_ready, coef_ready, coefT_in_psum, coefT_ready = (
        S("gel_ready"), S("coef_ready"), S("coefT_in_psum"), S("coefT_ready"))
    node_in_psum, out_ready, tree_set = S("node_in_psum"), S("out_ready"), S("tree_set")
    out_stored = [S(f"out_stored{s}") for s in range(2)]

    def wait(eng, sem, value):
        if not isinstance(value, int) or value > 0:
            eng.wait_ge(sem, value)

    def hold(eng, sem, value):
        if not isinstance(value, int) or value > 0:
            eng.wait_ge(sem, value)
            if not isinstance(value, int):
                eng.sem_inc(carried, 1)

    def leave(eng, n):
        eng.drain().then_inc(phase_left, 1)
        eng.wait_ge(phase_left, 5 * n)

    def bands(eng, tile):
        for hh in range(3):
            tile(hh, hh % 2, hh // 2, hh == 0, False)
        with eng.Fori(0, (GRID - 4) // 2) as j:
            tile(2 * j + 3, 1, j + 1, False, False)
            tile(2 * j + 4, 0, j + 2, False, False)
        tile(GRID - 1, 1, (GRID - 1) // 2, False, True)

    def batches(eng, step, lag, n=NBATCH):
        def peeled(i):
            step(i, i % 2, i // 2, lambda d: 0 <= i - d < n)

        first = 4
        pairs = (n - 1 - first) // 2
        for i in range(first):
            peeled(i)
        with eng.Fori(0, pairs) as j:
            for k in range(2):
                i = first + k
                step(2 * j + i, i % 2, j + i // 2, lambda d: True)
        for i in range(first + 2 * pairs, n + lag):
            peeled(i)

    def prepared(eng):
        eng.wait_ge(prep_dve, 3)
        eng.wait_ge(prep_pool, 3)
        eng.wait_ge(filter_stored, 16)
        eng.wait_ge(cls_stored, 16)

    def lay_out(eng, n, s, ww):
        slot = PATCH_SLOT[ww]
        back = next(d for d in range(1, GRID + 1) if PATCH_SLOT[(ww - d) % GRID] == slot)
        if not isinstance(n, int) or n >= back:
            hold(eng, xT_in_psum, n - back + 1) if eng is nc.gpsimd else eng.wait_ge(xT_in_psum, n - back + 1)
        at = LEAD - CH + PXF * ww
        return eng.tensor_copy(patch[slot][:, 0:PATF].rearrange("p (r f) -> p r f", f=RINGF),
                               band[s][:, :, at:at + RINGF])

    def place_weights(eng, odd):
        eng.wait_ge(prep_dve, 1)
        eng.wait_ge(cleared, 16)
        for i in range(PATCH):
            src = w_sc[8 * i:8 * i + 8, CH * NSHIFT * odd:CH * NSHIFT * (odd + 1), :].rearrange("p (s c) d -> p s (c d)", c=CH)
            dst = bass.AP(tensor=wscr.tensor, offset=(111 + i * RINGF + CH * odd) * DIM,
                          ap=[[2 * CH * DIM, 8], [COPY_GAP * DIM, NSHIFT], [1, CH * DIM]])
            eng.dma_start(dst, src).then_inc(scaled_stored, 16)

    def rep(row, n):
        return bass.AP(tensor=row.tensor, offset=row.offset, ap=[[0, n]] + [list(a) for a in row.ap])

    with nc.Block() as block:
        @block.sync
        def _(sp):
            sp.dma_start(w_nat[:, :, :], W.rearrange("(p k) d -> p k d", k=KROW)).then_inc(w_loaded, 16)
            sp.dma_start(gam[:, :], gamma.rearrange("(p k) -> p k", k=KROW)).then_inc(gb_loaded, 16)
            sp.dma_start(bet[:, :], beta.rearrange("(p k) -> p k", k=KROW)).then_inc(gb_loaded, 16)
            sp.dma_start(bias_row[:, :], rep(tok_b, 1)).then_inc(gb_loaded, 16)
            for dst, src in ((cnt[:, :], c_count),
                             (filt_w[0:FFREQ, :], w_filt), (filt_w[FFREQ:FFREQ + 1, :], rep(b_filt, 1)),
                             (filt_b[:, :], c_basis), (nodes[0:NODES, :], wn_in),
                             (nodes[NODES:NODEX, :], rep(wn_in[NODES - 1, :], NODEX - NODES)),
                             (cls_h[:, 0:DIM], rep(cls_tok[0, 0, :], 128))):
                sp.dma_start(dst, src).then_inc(tables_loaded, 16)
            sp.wait_ge(consts_set, 7)
            z = zeros[:, 0:600]
            sp.dma_start(wscr.rearrange("(p k) d -> p (k d)", p=120).rearrange("p (k f) -> p k f", f=600),
                         bass.AP(tensor=z.tensor, offset=z.offset, ap=[[z.ap[0][0], 120], [0, 16], [1, 600]])).then_inc(cleared, 16)
            sp.dma_start(band[0][:, 0, LEAD:LEAD + ROWF], zeros[:, :]).then_inc(ring_zeroed, 16)
            sp.wait_ge(ring_zeroed, 16)

            def load_band(hh, s, lo, hi):
                src = x.rearrange("b h w c -> b (h w c)")[:, bass.ds((PATCH * hh - 1 + lo) * ROWF, (hi - lo) * ROWF)]
                sp.dma_start(band[s][:, lo:hi, LEAD:LEAD + ROWF],
                             src.rearrange("b (r f) -> b r f", f=ROWF)).then_inc(band_loaded[s], 16)

            load_band(0, 0, 1, BAND)
            place_weights(sp, 0)
            sp.wait_ge(scaled_stored, 32 * PATCH)
            for s in range(NSHIFT):
                sp.dma_start(w_sh[:, s, :, :], wscr[COPY_AT[s]:COPY_AT[s] + 128 * NCHUNK, :].rearrange("(c p) d -> p c d", p=128))\
                    .then_inc(shifted_loaded, 16)
            sp.wait_ge(prep_dve, 2)
            sp.dma_start(filt_scr.rearrange("(h p) k -> p h k", p=HALF), filt_p[:, :, :]).then_inc(filter_stored, 16)
            sp.dma_start(h_scr[:, NTOK:PTOK, :], zeros[:, 0:(PTOK - NTOK) * HCOL].rearrange("p (l d) -> p l d", d=HCOL))\
                .then_inc(pads_stored, 16)
            sp.dma_start(short_scr[:, :, PTOK, :], zeros[0:HALF, 0:256].rearrange("p (h b) -> p h b", h=2))\
                .then_inc(pads_stored, 16)
            sp.wait_ge(prep_pool, 2)
            sp.dma_start(h_scr[:, 0, :], cls_h[:, :]).then_inc(cls_stored, 16)
            sp.dma_start(w_out_sb[0:HALF, :, 0:DIM], w_out.rearrange("(h p) d -> p h d", p=HALF)).then_inc(small_loaded, 16)
            sp.dma_start(w_out_sb[HALF:HALF + 1, 1, 0:DIM], rep(b_out, 1)).then_inc(small_loaded, 16)
            sp.dma_start(taps[:, :, :], w_short.rearrange("(h p) o k -> p h (o k)", p=HALF)).then_inc(small_loaded, 16)
            sp.dma_start(taps_b[:, :], b_short.rearrange("(h p) -> p h", p=HALF), allow_slow_non_contiguous=True).then_inc(small_loaded, 16)
            for q in range(QUAD):
                sp.dma_start(node_out[NODEX * q:NODEX * q + NODES, q, :], wn_out).then_inc(small_loaded, 16)
                sp.dma_start(node_out[NODEX * q + NODES:NODEX * (q + 1), q, :],
                             rep(wn_out[NODES - 1, :], NODEX - NODES)).then_inc(small_loaded, 16)
            sp.wait_ge(prep_dve, 3)
            sp.wait_ge(prep_pe, 4)
            sp.wait_ge(prep_pool, 3)

            def store_h(hh, s):
                sp.wait_ge(hstat_ready, hh + 1)
                sp.dma_start(h_scr[:, bass.ds(GRID * hh + 1, GRID), :], htile[s][:, :, :]).then_inc(h_stored[s], 16)

            def left_band(hh):
                hold(sp, patch_dve, (GRID - len(COPY_POOL)) * (hh - 1))
                hold(sp, patch_pool, len(COPY_POOL) * (hh - 1))

            load_band(1, 1, 0, BAND)
            with sp.Fori(0, (GRID - 4) // 2) as j:
                for k in range(2):
                    hh = 2 * j + 2 + k
                    left_band(hh)
                    hold(sp, edge_squared, 2 * (hh - 1))
                    sp.wait_ge(core_squared, GRID * (hh - 1))
                    load_band(hh, k, 0, BAND)
                    store_h(hh - 2, k)
            for hh in (GRID - 2, GRID - 1):
                s = hh % 2
                left_band(hh)
                hold(sp, edge_squared, 2 * (hh - 1))
                sp.wait_ge(core_squared, GRID * (hh - 1))
                if hh == GRID - 1:
                    sp.dma_start(band[s][:, BAND - 1, LEAD:LEAD + ROWF], zeros[:, :]).then_inc(ring_zeroed, 16)
                    sp.wait_ge(ring_zeroed, 32)
                    load_band(hh, s, 0, BAND - 1)
                else:
                    load_band(hh, s, 0, BAND)
                store_h(hh - 2, s)
            store_h(GRID - 2, 0)
            store_h(GRID - 1, 1)
            for s in range(2):
                sp.wait_ge(h_stored[s], 16 * GRID // 2)
            sp.wait_ge(pads_stored, 32)
            sp.wait_ge(cls_stored, 16)
            sp.wait_ge(filter_stored, 16)
            leave(sp, 1)

            sp.dma_start(win[0:HALF, :, 0:4 * DIM], w_in.rearrange("(h p) n -> p h n", p=HALF)).then_inc(win_loaded, 16)
            sp.dma_start(win[HALF:HALF + 1, 1, 0:4 * DIM], rep(b_in, 1)).then_inc(win_loaded, 16)

            def load_hin(i, s):
                sp.dma_start(hin[s][:, :, :], h_scr[:, bass.ds(QUAD * i, QUAD), :]).then_inc(hin_loaded[s], 16)

            load_hin(0, 0)
            load_hin(1, 1)

            def step2(i, s, turn, on):
                if on(-2):
                    hold(sp, xn_ready, i + 1)
                    load_hin(i + 2, s)
                if on(1):
                    b, p = i - 1, 1 - s
                    sp.wait_ge(short_ready, 2 * b + 2)
                    sp.dma_start(short_scr[:, :, bass.ds(QUAD * b, QUAD), :].rearrange("p h l b -> p h (l b)"),
                                 short[p][:, :, :]).then_inc(short_stored[p], 16)
                    for hf in range(2):
                        sp.wait_ge(proj_ready, 2 * b + hf + 1)
                        dst = proj_scr[bass.ds(QUAD * b, QUAD), hf * HALF:(hf + 1) * HALF, :]
                        sp.dma_start(dst.rearrange("l d b -> d l b"), proj[p][:, hf, :, :]).then_inc(proj_stored[p], 16)
                    sp.wait_ge(gate_ready, 2 * b + 2)
                    sp.dma_start(gate_scr[:, bass.ds(QUAD * b, QUAD), :], gate[p][:, :, :]).then_inc(gate_stored[p], 16)

            batches(sp, step2, 1)
            for s in range(2):
                n = NBATCH // 2
                sp.wait_ge(short_stored[s], 16 * n)
                sp.wait_ge(proj_stored[s], 32 * n)
                sp.wait_ge(gate_stored[s], 16 * n)
            leave(sp, 2)

            def load_group(g, s):
                sem = taps_loaded[s]
                win0 = bass.AP(tensor=filt_scr.tensor, offset=g * (CG * GPADW), ap=[[1, TAP0], [GPADW, CG], [1, HANK]])
                sp.dma_start(toep[s][:, :, :], win0).then_inc(sem, 16)
                sp.dma_start(src0[s][:, :, :], proj_scr[0:TAP0, bass.ds(g * CG, CG), :]).then_inc(sem, 16)
                sp.dma_start(src1[s][:, :, :], proj_scr[TAP0:PTOK, bass.ds(g * CG, CG), :]).then_inc(sem, 16)

            load_group(0, 0)
            load_group(1, 1)
            with sp.Fori(0, NGROUP // 2 - 1) as j:
                for s in range(2):
                    g = 2 * j + s
                    sp.wait_ge(conv_in_psum, 2 * g + 2)
                    load_group(g + 2, s)
            leave(sp, 3)

            def load_gates(i, s):
                sp.dma_start(gy[s][:, :, :], gate_scr[:, bass.ds(QUAD * i, QUAD), :]).then_inc(gy_loaded[s], 16)
                sp.dma_start(sh[s][:, :, :], short_scr[:, :, bass.ds(QUAD * i + 1, QUAD), :].rearrange("p h l b -> p h (l b)"))\
                    .then_inc(gy_loaded[s], 16)

            def load_h(i, s):
                sp.dma_start(hb[s][:, :, :], h_scr[:, bass.ds(QUAD * i, QUAD), :]).then_inc(hb_loaded[s], 16)

            for i in range(2):
                load_gates(i, i)
                load_h(i, i)

            def step4(i, s, turn, on):
                if on(-2):
                    hold(sp, yT_in_psum, 2 * i + 2)
                    hold(sp, u_ready, 2 * i + 2)
                    hold(sp, lgh_ready, i + 1)
                    load_gates(i + 2, s)
                if on(2):
                    b = i - 2
                    hold(sp, out_ready, 2 * b + 2)
                    n = NTOK - QUAD * (NBATCH - 1) if isinstance(b, int) and b == NBATCH - 1 else QUAD
                    sp.dma_start(out[:, bass.ds(QUAD * b, n), :], ob[s][:, 0:n, :]).then_inc(out_stored[s], 16)
                if on(-2):
                    hold(sp, h2_ready, 2 * i + 2)
                    load_h(i + 2, s)

            batches(sp, step4, 2)
            for s in range(2):
                sp.wait_ge(out_stored[s], 16 * NBATCH // 2)

        @block.gpsimd
        def _(pool):
            nc.gpsimd.memset(ident[:, :], 0.0).then_inc(ident_set, 1)
            nc.gpsimd.memset(wf[:, :, :], 0.0).then_inc(prep_pool, 1)
            pool.wait_ge(ident_set, 1)
            nc.gpsimd.affine_select(out=ident[:, :], in_=ident[:, :], compare_op=ALU.not_equal, fill=1.0,
                                    base=0, pattern=[[-1, 128]], channel_multiplier=1).then_inc(ident_set, 1)
            pool.wait_ge(prep_dve, 2)
            pool.wait_ge(consts_set, 7)
            nc.gpsimd.tensor_tensor(cls_h[:, DIM + 1:DIM + 2], cls_v[:, :], half_neg[:, 0:1], ALU.pow).then_inc(cls_step, 1)
            pool.wait_ge(cls_step, 1)
            nc.gpsimd.tensor_tensor(cls_h[:, DIM + 2:HCOL], cls_v[:, :], cls_h[:, DIM + 1:DIM + 2], ALU.mult).then_inc(prep_pool, 1)
            pool.wait_ge(prep_dve, 3)
            pool.wait_ge(prep_pe, 4)
            pool.wait_ge(scaled_stored, 32 * PATCH)
            nc.gpsimd.memset(band[1][:, :, 0:LEAD], 0.0)
            nc.gpsimd.memset(band[1][:, :, LEAD + ROWF:PITCH], 0.0)
            for s in range(3):
                nc.gpsimd.memset(patch[s][:, PATF:], 0.0)
            pool.drain().then_inc(prep_pool, 1)

            def rsqrt_tokens(hh, s):
                pool.wait_ge(tvar_ready, hh + 1)
                nc.gpsimd.tensor_tensor(trstd[s][:, :], tvar[:, :], half_neg[:, 0:GRID], ALU.pow).then_inc(trstd_ready, 1)

            def rsqrt_h(hh, s):
                hold(pool, h_ready, hh + 1)
                nc.gpsimd.tensor_scalar(hvar[:, :], htile[s][:, :, DIM + 1], LN_EPS, None, ALU.add).then_inc(pool_step, 1)
                pool.wait_ge(pool_step, 2 * hh + 1)
                nc.gpsimd.tensor_tensor(htile[s][:, :, DIM + 1], hvar[:, :], half_neg[:, 0:GRID], ALU.pow).then_inc(pool_step, 1)
                pool.wait_ge(pool_step, 2 * hh + 2)
                nc.gpsimd.tensor_tensor(htile[s][:, :, DIM + 2], hvar[:, :], htile[s][:, :, DIM + 1], ALU.mult)\
                    .then_inc(hstat_ready, 1)

            def tile(hh, s, turn, first, last):
                if not first:
                    rsqrt_tokens(hh - 1, 1 - s)
                hold(pool, band_loaded[s], 16 * (turn + 1))
                for ww in COPY_POOL:
                    lay_out(nc.gpsimd, GRID * hh + ww, s, ww).then_inc(patch_pool, 1)
                if not first:
                    rsqrt_h(hh - 1, 1 - s)
                if last:
                    rsqrt_tokens(hh, s)
                    rsqrt_h(hh, s)

            bands(pool, tile)
            leave(pool, 1)

            nc.gpsimd.memset(xnT[0][:, :, 0:2, :], 0.0).then_inc(halo_ready, 1)
            for s in range(2):
                nc.gpsimd.memset(xn_hi[s][HALF:HALF + 1, 1, :].bitcast(F32), 1.0).then_inc(halo_ready, 1)
                nc.gpsimd.memset(xn_lo[s][HALF:HALF + 1, 1, :].bitcast(F32), 0.0).then_inc(halo_ready, 1)

            def step2(i, s, turn, on):
                if on(-1):
                    hold(pool, xnT_ready, 2 * i + 2)
                    hold(pool, short_ready, 2 * i)
                    nc.gpsimd.tensor_copy(xnT[1 - s][:, :, 0:2, :], xnT[s][:, :, QUAD:QUAD + 2, :]).then_inc(halo_ready, 1)

            batches(pool, step2, 0)
            leave(pool, 2)

            nc.gpsimd.memset(Y[:, NTOK:PTOK, :], 0.0).then_inc(y_padded, 1)
            leave(pool, 3)

            def gated(i, s, loads):
                pool.wait_ge(gy_loaded[s], 32 * loads)
                nc.gpsimd.tensor_tensor(gy[s][:, :, 0:DIM], gy[s][:, :, 0:DIM], Y[:, bass.ds(QUAD * i, QUAD), :], ALU.mult)\
                    .then_inc(y_ready, 1)

            def nodes_of_h(i, s, loads):
                pool.wait_ge(hb_loaded[s], 16 * loads)
                wait(pool, logit_ready, i - 1)
                nc.gpsimd.tensor_tensor(lgh[s][:, :, :], gy[s][:, :, DIM:DIMN],
                                        hb[s][:, :, DIM + 2:HCOL].to_broadcast([128, QUAD, NODEX]), ALU.mult).then_inc(lgh_ready, 1)

            gated(0, 0, 1)
            nodes_of_h(0, 0, 1)
            gated(1, 1, 1)

            def step4(i, s, turn, on):
                if on(-2):
                    gated(i + 2, s, turn + 2)
                if on(-1):
                    nodes_of_h(i + 1, 1 - s, turn + s + 1)
                if on(0):
                    pool.wait_ge(var_ready, i + 1)
                    nc.gpsimd.tensor_tensor(rstd4[s][:, :], var4[:, :], half_neg[:, 0:QUAD], ALU.pow).then_inc(rstd_ready, 1)

            batches(pool, step4, 0)

        @block.scalar
        def _(act_e):
            place_weights(act_e, 1)
            prepared(act_e)

            sq_core = ps[:, 6:8, :].rearrange("p k b -> p (k b)")[:, 0:PATCH * PXF].rearrange("p (r f) -> p r f", f=PXF)

            def tile(hh, s, turn, first, last):
                act_e.wait_ge(band_loaded[s], 16 * (turn + 1))
                for ww in range(GRID):
                    n = GRID * hh + ww
                    nfirst = first and ww < 2
                    act_e.wait_ge(xT_in_psum, n + 1)
                    if not nfirst:
                        act_e.wait_ge(tok_in_psum, n - 1)
                    k = 2 * (ww % 2)
                    nc.scalar.activation(xT_hi[ww % 2][:, :, :].rearrange("p c b -> p (c b)"),
                                         ps[:, k:k + 2, :].rearrange("p k b -> p (k b)"), ACT.Copy).then_inc(xT_hi_ready, 1)
                    if ww == 0 and not first:
                        wait(act_e, tvar_ready, hh - 1)
                    v = LEAD + PXF * ww
                    wait(act_e, core_squared, n)
                    nc.scalar.activation(sq_core, band[s][:, 1:1 + PATCH, v:v + PXF], ACT.Square,
                                         accum_out=core_sum[s][:, ww:ww + 1]).then_inc(core_squared, 1)
                    if ww == 2:
                        wait(act_e, edges_summed, 3 * hh)
                        rows = bass.AP(tensor=band[s][:, :, :].tensor, offset=band[s][:, 0, LEAD:LEAD + 1].offset,
                                       ap=[band[s][:, :, :].ap[0], [PATCH * PITCH, 2], [PITCH, 2], [1, ROWF]])
                        nc.scalar.activation(sq_rows[:, :, :, :], rows, ACT.Square).then_inc(edge_squared, 1)
                        cols = bass.AP(tensor=band[s][:, :, :].tensor, offset=band[s][:, 1, LEAD - CH:LEAD].offset,
                                       ap=[band[s][:, :, :].ap[0], [PXF, GRID + 1], [PITCH, PATCH], [1, 6]])
                        nc.scalar.activation(sq_cols[:, :, :, :], cols, ACT.Square).then_inc(edge_squared, 1)
                    if not (first and ww == 0):
                        copy_token(n - 1, s if ww else 1 - s, (ww - 1) % GRID, hh if ww else hh - 1, first)
                if last:
                    copy_token(GRID * GRID - 1, s, GRID - 1, hh, False)

            def copy_token(n, s, ww, hh, first):
                act_e.wait_ge(tok_in_psum, n + 1)
                if ww == 0 and not first:
                    wait(act_e, h_ready, hh - 1)
                nc.scalar.activation(praw[s][:, ww, :], ps[:, 4 + ww % 2, 0:WCOL], ACT.Copy).then_inc(tok_copied, 1)

            bands(act_e, tile)
            leave(act_e, 1)

            act_e.wait_ge(win_loaded, 32)
            act_e.wait_ge(win_nodes, 2)
            nc.scalar.activation(win_hi[0:HALF, 0, :], win[0:HALF, 0, :], ACT.Copy).then_inc(win_his, 1)
            nc.scalar.activation(win_hi[:, 1, :], win[:, 1, :], ACT.Copy).then_inc(win_his, 1)

            def step2(i, s, turn, on):
                if on(0):
                    for hf in range(2):
                        act_e.wait_ge(xnT_in_psum, 2 * i + hf + 1)
                        if hf == 0 and not (isinstance(i, int) and i < 2):
                            act_e.wait_ge(short_ready, 2 * i - 2)
                            act_e.wait_ge(halo_ready, 5 + i - 1)
                            act_e.wait_ge(xn_lo_ready, 2 * i - 2)
                        nc.scalar.activation(xnT[s][:, hf, 2:2 + QUAD, :], ps[0:HALF, hf, :], ACT.Copy).then_inc(xnT_ready, 1)
                    for hf in range(2):
                        act_e.wait_ge(xnT_ready, 2 * i + hf + 1)
                        if hf == 0:
                            wait(act_e, proj_in_psum, 2 * i - 2)
                            wait(act_e, zv_in_psum, 4 * i - 4)
                        nc.scalar.activation(xn_hi[s][0:HALF, hf, :], xnT[s][:, hf, 2:2 + QUAD, :], ACT.Copy).then_inc(xn_hi_ready, 1)
                    act_e.wait_ge(halo_ready, 5 + i)
                    for hf in range(2):
                        if hf == 0:
                            wait(act_e, short_stored[s], 16 * turn)
                        nc.scalar.activation(short[s][:, hf, :], xnT[s][:, hf, 1:1 + QUAD, :], ACT.Identity,
                                             bias=taps_b[:, hf:hf + 1], scale=taps[:, hf, 1:2]).then_inc(centre_ready, 1)
                if on(1):
                    b, p = i - 1, 1 - s
                    for pr_ in range(2):
                        act_e.wait_ge(zv_in_psum, 4 * b + 2 * pr_ + 1)
                        nc.scalar.activation(silu[pr_][:, :, :], ps[:, 2 + 3 * pr_:4 + 3 * pr_, 0:DIM], ACT.Silu).then_inc(silu_ready, 1)
                        if pr_ == 0:
                            for hf in range(2):
                                act_e.wait_ge(proj_in_psum, 2 * b + hf + 1)
                                if hf == 0:
                                    wait(act_e, proj_stored[p], 32 * (turn - 1 if s == 0 else turn))
                                nc.scalar.activation(proj[p][:, hf, :, :], ps[0:HALF, hf, :], ACT.Copy).then_inc(proj_ready, 1)

            batches(act_e, step2, 1)
            leave(act_e, 2)

            with act_e.Fori(0, NGROUP // 2) as j:
                for s in range(2):
                    g = 2 * j + s
                    act_e.wait_ge(conv_in_psum, 2 * g + 1)
                    v = ps[:, 4 * s:4 * s + 2, 0:2 * NTOK].rearrange("p k (c l) -> p l k c", c=2)[:, ::-1, :, :]
                    dst = Y[:, 0:NTOK, bass.ds(CG * g, 4)].rearrange("p l (k c) -> p l k c", k=2)
                    nc.scalar.activation(dst, v, ACT.Copy).then_inc(conv_kept_act, 1)
            leave(act_e, 3)

            def step4(i, s, turn, on):
                if on(1):
                    b = i - 1
                    act_e.wait_ge(coefT_in_psum, b + 1)
                    wait(act_e, node_in_psum, 2 * b)
                    nc.scalar.activation(coefT[:, :], ps[:, 4, 0:128], ACT.Copy).then_inc(coefT_ready, 1)
                if on(0):
                    act_e.wait_ge(logit_ready, i + 1)
                    act_e.wait_ge(rstd_ready, i + 1)
                    wait(act_e, coef_ready, i)
                    for q in range(QUAD):
                        nc.scalar.activation(gel[:, q, :], logit[:, q, :], ACT.Gelu,
                                             scale=rstd4[s][:, q:q + 1]).then_inc(gel_ready, 1)

            batches(act_e, step4, 1)

        @block.vector
        def _(dve):
            count = [0]

            def own(ins):
                count[0] += 1
                ins.then_inc(dve_step, 1)
                dve.wait_ge(dve_step, count[0])

            for t, v in ((zeros[:, :], 0.0), (half_neg[:, :], -0.5), (ones[:, :], 1.0), (filt_p[:, :, :], 0.0),
                         (node_out[:, :, :], 0.0),
                         (band[0][:, :, 0:LEAD], 0.0), (band[0][:, :, LEAD + ROWF:PITCH], 0.0)):
                nc.vector.memset(t, v).then_inc(consts_set, 1)
            dve.wait_ge(w_loaded, 16)
            dve.wait_ge(gb_loaded, 48)
            nc.vector.tensor_tensor(w_sc[:, :, :], w_nat[:, :, :], gam[:, :].unsqueeze(2).to_broadcast([128, KROW, DIM]),
                                    ALU.mult).then_inc(prep_dve, 1)
            dve.wait_ge(tables_loaded, 16 * 7)
            own(nc.vector.tensor_reduce(node_m[:, :], nodes[:, :], AXIS.X, ALU.add))
            own(nc.vector.tensor_scalar(node_m[:, :], node_m[:, :], 1.0 / DIM, None, ALU.mult))
            own(nc.vector.tensor_scalar(nodes[:, :], nodes[:, :], node_m[:, 0:1], None, ALU.subtract))
            own(nc.vector.bn_stats(cls6[:, :], cls_h[:, 0:DIM]))
            own(nc.vector.bn_aggr(cls_h[:, DIM:DIM + 2], cls6[:, :]))
            own(nc.vector.tensor_scalar(cls_v[:, :], cls_h[:, DIM + 1:DIM + 2], LN_EPS, None, ALU.add))
            own(nc.vector.tensor_scalar(cnt_neg[:, :], cnt[:, :], -1.0, None, ALU.mult))
            dve.wait_ge(prep_pe, 1)
            for hf in range(2):
                own(nc.vector.tensor_copy(filt_p[:, hf, SPAD:SPAD + NTOK], ps[0:HALF, hf, 0:NTOK]))
                own(nc.vector.tensor_copy(node_inT[:, hf, :], ps[0:HALF, 2 + hf, 0:NODEX]))
            dve.drain().then_inc(prep_dve, 1)
            dve.wait_ge(prep_pe, 2)
            own(nc.vector.tensor_copy(csum[:, :], ps[:, 4, 0:DIM]))
            dve.wait_ge(prep_pe, 3)
            own(nc.vector.tensor_tensor(bias_row[:, :], ps[0:1, 5, 0:DIM], bias_row[:, :], ALU.add))
            dve.wait_ge(prep_pe, 4)
            own(nc.vector.tensor_copy(tok_bias[:, :], ps[:, 6, 0:DIM]))
            dve.wait_ge(shifted_loaded, 16 * NSHIFT)
            dve.wait_ge(prep_pool, 1)
            own(nc.vector.tensor_tensor(wf[:, :, 0:DIM], w_sh[:, 0, :, :], w_sh[:, 1, :, :], ALU.add))
            for s in range(2, NSHIFT):
                own(nc.vector.tensor_tensor(wf[:, :, 0:DIM], wf[:, :, 0:DIM], w_sh[:, s, :, :], ALU.add))
            for j in range(NCHUNK):
                own(nc.vector.scalar_tensor_tensor(wf[:, j, 0:DIM], csum[:, :], cnt_neg[:, j:j + 1], wf[:, j, 0:DIM],
                                                   ALU.mult, ALU.add))
            own(nc.vector.tensor_copy(wf[:, :, DIM], cnt[:, :]))
            own(nc.vector.tensor_copy(wf_hi[:, :, :], wf[:, :, :]))
            own(nc.vector.tensor_tensor(wf_lo[:, :, :], wf[:, :, :], wf_hi[:, :, :].bitcast(F32), ALU.subtract))
            dve.drain().then_inc(prep_dve, 1)

            chain = count[0]
            CHAIN = 9

            def dve_patch(hh, s, turn, ww):
                if ww == 0:
                    dve.wait_ge(band_loaded[s], 16 * (turn + 1))
                if ww not in COPY_POOL:
                    lay_out(nc.vector, GRID * hh + ww, s, ww).then_inc(patch_dve, 1)

            def tile(hh, s, turn, first, last):
                if first:
                    dve_patch(hh, s, turn, 0)
                for ww in range(GRID):
                    n = GRID * hh + ww
                    if ww + 1 < GRID:
                        dve_patch(hh, s, turn, ww + 1)
                    elif not last:
                        dve_patch(hh + 1, 1 - s, turn + s, 0)
                    dve.wait_ge(xT_hi_ready, n + 1)
                    if not (first and ww < 2):
                        dve.wait_ge(tok_in_psum, n - 1)
                    k = 2 * (ww % 2)
                    nc.vector.tensor_tensor(xT_lo[ww % 2][:, :, :].rearrange("p c b -> p (c b)"),
                                            ps[:, k:k + 2, :].rearrange("p k b -> p (k b)"),
                                            xT_hi[ww % 2][:, :, :].rearrange("p c b -> p (c b)").bitcast(F32),
                                            ALU.subtract).then_inc(xT_lo_ready, 1)
                    if ww == 4:
                        edge_sums(hh, s)
                    if not first:
                        finish(hh - 1, 1 - s, ww)
                if last:
                    for ww in range(GRID):
                        finish(hh, s, ww)

            def link(ins, hh, k):
                ins.then_inc(dve_step, 1)
                dve.wait_ge(dve_step, chain + CHAIN * hh + k + 1)

            def edge_sums(hh, s):
                dve.wait_ge(edge_squared, 2 * hh + 2)
                nc.vector.tensor_reduce(row_sum[:, :, :, :], sq_rows[:, :, :, :].rearrange("p a b (w f) -> p a b w f", f=PXF),
                                        AXIS.X, ALU.add).then_inc(edges_summed, 1)
                for side in range(2):
                    nc.vector.tensor_reduce(col_sum[:, side, :], sq_cols[:, :, :, CH * side:CH * side + CH],
                                            AXIS.XY, ALU.add).then_inc(edges_summed, 1)

            def finish(hh, s, ww):
                if ww == 0:
                    dve.wait_ge(core_squared, GRID * hh + GRID)
                    dve.wait_ge(edges_summed, 3 * hh + 3)
                    dve.wait_ge(tok_copied, GRID * hh + GRID)
                    link(nc.vector.tensor_tensor(sum_a[:, :], row_sum[:, 0, 0, :], row_sum[:, 0, 1, :], ALU.subtract), hh, 0)
                    link(nc.vector.tensor_tensor(sum_b[:, :], row_sum[:, 1, 1, :], row_sum[:, 1, 0, :], ALU.subtract), hh, 1)
                    link(nc.vector.tensor_tensor(col_dif[:, :], col_sum[:, 0, :], col_sum[:, 1, :], ALU.subtract), hh, 2)
                    link(nc.vector.tensor_tensor(sum_a[:, :], sum_a[:, :], sum_b[:, :], ALU.add), hh, 3)
                    link(nc.vector.tensor_tensor(sum_b[:, :], col_dif[:, 0:GRID], col_dif[:, 1:GRID + 1], ALU.subtract), hh, 4)
                    link(nc.vector.scalar_tensor_tensor(sum_a[:, :], core_sum[s][:, :], 5.0, sum_a[:, :], ALU.mult, ALU.add), hh, 5)
                    link(nc.vector.tensor_tensor(sum_a[:, :], sum_a[:, :], sum_b[:, :], ALU.add), hh, 6)
                    link(nc.vector.tensor_tensor(musq[:, :], praw[s][:, :, DIM], praw[s][:, :, DIM], ALU.mult), hh, 7)
                    link(nc.vector.scalar_tensor_tensor(sum_a[:, :], sum_a[:, :], 1.0 / NFEAT, musq[:, :], ALU.mult, ALU.subtract), hh, 8)
                    wait(dve, trstd_ready, hh)
                    nc.vector.tensor_scalar(tvar[:, :], sum_a[:, :], 0.0, TOK_EPS, ALU.max, ALU.add).then_inc(tvar_ready, 1)
                end = ww == GRID - 1
                if ww == 2:
                    dve.wait_ge(trstd_ready, hh + 1)
                    if not isinstance(hh, int) or hh >= 2:
                        dve.wait_ge(h_stored[s], 16 * slot_turn(hh, s))
                for w in FINISH[0][ww]:
                    nc.vector.scalar_tensor_tensor(htile[s][:, w, 0:DIM], praw[s][:, w, 0:DIM], trstd[s][:, w:w + 1],
                                                   tok_bias[:, :], ALU.mult, ALU.add).then_inc(h_made, 1)
                for w in FINISH[1][ww]:
                    dve.wait_ge(h_made, GRID * hh + w + 1)
                    nc.vector.bn_stats(bn6[:, w, :], htile[s][:, w, 0:DIM]).then_inc(bn_made, 1)
                if FINISH[2][ww]:
                    hold(dve, bn_made, GRID * hh + FINISH[2][ww][-1] + 1)
                for w in FINISH[2][ww]:
                    ins = nc.vector.bn_aggr(htile[s][:, w, DIM:DIM + 2], bn6[:, w, :])
                if end:
                    ins.then_inc(h_ready, 1)

            def slot_turn(hh, s):
                return hh // 2 if isinstance(hh, int) else turn_of[0]

            turn_of = [0]
            first_slice = [2 + 11 * w // GRID for w in range(GRID)]
            FINISH = [[[w for w in range(GRID) if min(first_slice[w] + d, GRID - 1) == ww] for ww in range(GRID)]
                      for d in range(3)]

            def tile_outer(hh, s, turn, first, last):
                turn_of[0] = turn if s == 1 else turn - 1
                tile(hh, s, turn, first, last)

            bands(dve, tile_outer)
            leave(dve, 1)

            nc.vector.memset(win[HALF:HALF + 1, 1, 4 * DIM:], 0.0).then_inc(win_nodes, 1)
            nc.vector.tensor_copy(win[0:HALF, :, 4 * DIM:], node_inT[:, :, :]).then_inc(win_nodes, 1)
            for hf, parts in ((0, HALF), (1, HALF + 1)):
                dve.wait_ge(win_his, hf + 1)
                nc.vector.tensor_tensor(win_lo[0:parts, hf, :], win[0:parts, hf, :], win_hi[0:parts, hf, :].bitcast(F32),
                                        ALU.subtract).then_inc(win_split, 1)

            def norm(i, s, turn):
                dve.wait_ge(hin_loaded[s], 16 * (turn + 1))
                if not (isinstance(i, int) and i < 2):
                    dve.wait_ge(xnT_in_psum, 2 * (i - 1))
                for q in range(QUAD):
                    ins = nc.vector.tensor_scalar(xn[s][:, q, :], hin[s][:, q, 0:DIM], hin[s][:, q, DIM:DIM + 1],
                                                  hin[s][:, q, DIM + 1:DIM + 2], ALU.subtract, ALU.mult)
                ins.then_inc(xn_ready, 1)

            norm(0, 0, 0)
            steps2 = count[0]

            def step2(i, s, turn, on):
                if on(0):
                    if on(-1):
                        norm(i + 1, 1 - s, turn + (1 if s == 1 else 0))
                    for hf in range(2):
                        dve.wait_ge(xn_hi_ready, 2 * i + hf + 1)
                        if hf == 0:
                            wait(dve, proj_in_psum, 2 * i - 2)
                            wait(dve, zv_in_psum, 4 * i - 4)
                        nc.vector.tensor_tensor(xn_lo[s][0:HALF, hf, :], xnT[s][:, hf, 2:2 + QUAD, :].rearrange("p l b -> p (l b)"),
                                                xn_hi[s][0:HALF, hf, :].bitcast(F32), ALU.subtract).then_inc(xn_lo_ready, 1)
                    for hf in range(2):
                        dve.wait_ge(centre_ready, 2 * i + hf + 1)
                        nc.vector.scalar_tensor_tensor(short[s][:, hf, :], xnT[s][:, hf, 0:QUAD, :].rearrange("p l b -> p (l b)"),
                                                       taps[:, hf, 0:1], short[s][:, hf, :], ALU.mult, ALU.add).then_inc(left_ready, 1)
                    for hf in range(2):
                        dve.wait_ge(left_ready, 2 * i + hf + 1)
                        nc.vector.scalar_tensor_tensor(short[s][:, hf, :], xnT[s][:, hf, 2:2 + QUAD, :].rearrange("p l b -> p (l b)"),
                                                       taps[:, hf, 2:3], short[s][:, hf, :], ALU.mult, ALU.add).then_inc(short_ready, 1)
                if on(1):
                    b, p = i - 1, 1 - s
                    for pr_ in range(2):
                        dve.wait_ge(silu_ready, 2 * b + pr_ + 1)
                        nc.vector.tensor_tensor(szv[pr_][:, :, 0:DIM], ps[:, 2 + 3 * pr_:4 + 3 * pr_, DIM:2 * DIM],
                                                silu[pr_][:, :, :], ALU.mult).then_inc(szv_ready, 1)
                        dve.wait_ge(szv_ready, 2 * b + pr_ + 1)
                        dve.wait_ge(zv_in_psum, 4 * b + 2 * pr_ + 2)
                        if pr_ == 0:
                            wait(dve, gate_stored[p], 16 * (turn - 1 if s == 0 else turn))
                        nc.vector.tensor_tensor(gate[p][:, 2 * pr_:2 * pr_ + 2, :],
                                                ps[:, 4 + 3 * pr_, 0:2 * DIMN].rearrange("p (l d) -> p l d", l=2),
                                                szv[pr_][:, :, :], ALU.mult).then_inc(gate_ready, 1)

            left_ready, szv_ready = S("left_ready"), S("szv_ready")
            for p in range(2):
                nc.vector.memset(szv[p][:, :, DIM:], 1.0).then_inc(ones_set, 1)
            dve.wait_ge(ones_set, 2)
            batches(dve, step2, 1)
            leave(dve, 2)

            dve.wait_ge(wo_turned, 1)
            nc.vector.tensor_copy(woT[:, :, :], ps[0:HALF, 0:2, 0:DIM + 1]).then_inc(wo_copied, 1)
            dve.wait_ge(wo_turned, 2)
            nc.vector.tensor_copy(w_out_sb[0:HALF, 0, DIM:DIMN], ps[0:HALF, 2, 0:NODEX]).then_inc(wo_nodes, 1)
            nc.vector.tensor_copy(w_out_sb[:, 1, DIM:DIMN], ps[0:HALF + 1, 3, 0:NODEX]).then_inc(wo_nodes, 1)
            with dve.Fori(0, NGROUP // 2) as j:
                for s in range(2):
                    g = 2 * j + s
                    dve.wait_ge(conv_in_psum, 2 * g + 2)
                    v = ps[:, 4 * s + 2:4 * s + 4, 0:2 * NTOK].rearrange("p k (c l) -> p l k c", c=2)[:, ::-1, :, :]
                    dst = Y[:, 0:NTOK, bass.ds(CG * g + 4, 4)].rearrange("p l (k c) -> p l k c", k=2)
                    nc.vector.tensor_copy(dst, v).then_inc(conv_kept_dve, 1)
            leave(dve, 3)

            for s in range(2):
                nc.vector.memset(uT[s][HALF:HALF + 1, 1, :], 1.0).then_inc(tree_set, 1)
            nc.vector.memset(visit[:, :, :], 1.0).then_inc(tree_set, 1)
            nc.vector.memset(coef[:, :, :], 0.0).then_inc(tree_set, 1)
            dve.wait_ge(tree_set, 4)
            stat_step, visit_step, act_step = S("stat_step"), S("visit_step"), S("act_step")

            def add_short(i, s, loads):
                dve.wait_ge(gy_loaded[s], 32 * loads)
                for hf in range(2):
                    dve.wait_ge(yT_in_psum, 2 * i + hf + 1)
                    if hf == 0:
                        wait(dve, mix_in_psum, 2 * i - 2)
                    nc.vector.tensor_tensor(uT[s][0:HALF, hf, :], ps[0:HALF, hf, :], sh[s][:, hf, :], ALU.add)\
                        .then_inc(u_ready, 1)

            def add_h(b, s, k):
                dve.wait_ge(node_in_psum, 2 * b + k + 1)
                nc.vector.tensor_tensor(ob[s][:, 2 * k:2 * k + 2, :],
                                        ps[:, 6 + k, 0:2 * DIM].rearrange("p (l d) -> p l d", l=2),
                                        h2[s][:, 2 * k:2 * k + 2, :], ALU.add).then_inc(out_ready, 1)

            VISITS = 6

            def walk(b, k):
                if k == 0:
                    dve.wait_ge(logit_ready, b + 1)
                elif k > 1:
                    dve.wait_ge(visit_step, VISITS * b + k)
                if k < 2:
                    ins = nc.vector.tensor_scalar(branch[:, :, :, k], logit[:, :, 0:INNER], 0.0, None, (ALU.is_le, ALU.is_gt)[k])
                else:
                    n = 2 ** (k - 2)
                    p0 = n - 1
                    kids = visit[:, :, 2 * p0 + 1:2 * p0 + 1 + 2 * n].rearrange("p q (n c) -> p q n c", c=2)
                    ins = nc.vector.tensor_tensor(kids, branch[:, :, p0:p0 + n, :],
                                                  visit[:, :, p0:p0 + n].unsqueeze(3).to_broadcast([128, QUAD, n, 2]), ALU.mult)
                ins.then_inc(visit_step, 1)

            def coefficients(b, between):
                dve.wait_ge(gel_ready, QUAD * (b + 1))
                dve.wait_ge(visit_step, VISITS * (b + 1))
                nc.vector.tensor_tensor(act[:, :, 0:NODEX - 1], visit[:, :, 0:NODEX - 1], gel[:, :, 0:NODEX - 1], ALU.mult)\
                    .then_inc(act_step, 1)
                between(0)
                dve.wait_ge(act_step, 2 * b + 1)
                nc.vector.tensor_reduce(tail[:, :], act[:, :, INNER:NODEX - 1], AXIS.X, ALU.add).then_inc(act_step, 1)
                wait(dve, coefT_in_psum, b)
                kids = coef[:, :, 1:NODEX - 1].rearrange("p q (n c) -> p q n c", c=2)
                nc.vector.tensor_tensor(kids, branch[:, :, :, :],
                                        act[:, :, 0:INNER].unsqueeze(3).to_broadcast([128, QUAD, INNER, 2]), ALU.mult)
                dve.wait_ge(act_step, 2 * b + 2)
                nc.vector.scalar_tensor_tensor(coef[:, :, NODEX - 1], gel[:, :, NODES - 1], 5.0, tail[:, :], ALU.mult, ALU.add)\
                    .then_inc(coef_ready, 1)
                between(1)

            add_short(0, 0, 1)

            def step4(i, s, turn, on):
                if on(-1):
                    add_short(i + 1, 1 - s, turn + s + 1)

                def between(k):
                    if on(2):
                        if k == 0:
                            wait(dve, out_stored[s], 16 * (turn - 1))
                        add_h(i - 2, s, k)

                if on(1):
                    coefficients(i - 1, between)
                else:
                    between(0)
                    between(1)
                if on(0):
                    dve.wait_ge(hb_loaded[s], 16 * (turn + 1))
                    for k in range(2):
                        dve.wait_ge(mix_in_psum, 2 * i + k + 1)
                        if k == 0:
                            wait(dve, out_ready, 2 * i - 2)
                        nc.vector.tensor_tensor(h2[s][:, 2 * k:2 * k + 2, :],
                                                ps[:, 2 + k, 0:2 * DIMN].rearrange("p (l d) -> p l d", l=2)[:, :, 0:DIM],
                                                hb[s][:, 2 * k:2 * k + 2, 0:DIM], ALU.add).then_inc(h2_ready, 1)
                    dve.wait_ge(lgh_ready, i + 1)
                    wait(dve, gel_ready, QUAD * i)
                    nc.vector.tensor_tensor(logit[:, :, :].rearrange("p (k l) n -> p k l n", k=2),
                                            ps[:, 2:4, 0:2 * DIMN].rearrange("p k (l d) -> p k l d", l=2)[:, :, :, DIM:DIMN],
                                            lgh[s][:, :, :].rearrange("p (k l) n -> p k l n", k=2), ALU.add).then_inc(logit_ready, 1)
                    dve.wait_ge(h2_ready, 2 * i + 2)
                    for q in range(QUAD):
                        ins = nc.vector.bn_stats(bn4[:, q, :], h2[s][:, q, :])
                    ins.then_inc(stat_step, 1)
                    walk(i, 0)
                    walk(i, 1)
                    hold(dve, stat_step, 2 * i + 1)
                    for q in range(QUAD):
                        ins = nc.vector.bn_aggr(mv4[:, q, :], bn4[:, q, :])
                    ins.then_inc(stat_step, 1)
                    walk(i, 2)
                    dve.wait_ge(stat_step, 2 * i + 2)
                    wait(dve, rstd_ready, i)
                    nc.vector.tensor_scalar(var4[:, :], mv4[:, :, 1], LN_EPS, None, ALU.add).then_inc(var_ready, 1)
                    for k in range(3, VISITS):
                        walk(i, k)

            batches(dve, step4, 2)

        @block.tensor
        def _(pe):
            pe.wait_ge(ident_set, 2)
            pe.wait_ge(tables_loaded, 16 * 7)
            pe.wait_ge(dve_step, 3)
            for hf in range(2):
                nc.tensor.matmul(ps[0:HALF, hf, 0:NTOK], filt_w[:, hf * HALF:(hf + 1) * HALF], filt_b[:, :], start=True, stop=True)
                last = nc.tensor.transpose(ps[0:HALF, 2 + hf, 0:NODEX], nodes[:, hf * HALF:(hf + 1) * HALF], ident[0:NODEX, 0:NODEX])
            last.then_inc(prep_pe, 1)
            pe.wait_ge(prep_dve, 1)
            pe.wait_ge(consts_set, 7)
            for k in range(KROW):
                last = nc.tensor.matmul(ps[:, 4, 0:DIM], ones[:, :], w_sc[:, k, :], start=(k == 0), stop=(k == KROW - 1))
            last.then_inc(prep_pe, 1)
            for k in range(KROW):
                last = nc.tensor.matmul(ps[0:1, 5, 0:DIM], bet[:, k:k + 1], w_nat[:, k, :], start=(k == 0), stop=(k == KROW - 1))
            last.then_inc(prep_pe, 1)
            pe.wait_ge(dve_step, BIAS_STEP)
            nc.tensor.matmul(ps[:, 6, 0:DIM], ones[0:1, :], bias_row[:, :], start=True, stop=True).then_inc(prep_pe, 1)

            def transposes(n, s, ww, hh, first):
                own = GRID - len(COPY_POOL)
                if ww in COPY_POOL:
                    pe.wait_ge(patch_pool, len(COPY_POOL) * hh + COPY_POOL.index(ww) + 1)
                else:
                    pe.wait_ge(patch_dve, own * hh + ww - sum(v < ww for v in COPY_POOL) + 1)
                if not (first and ww < 2):
                    pe.wait_ge(xT_lo_ready, n - 1)
                for c in range(NCHUNK):
                    last = nc.tensor.transpose(ps[:, 2 * (ww % 2) + c // 4, 128 * (c % 4):128 * (c % 4) + 128],
                                               patch[PATCH_SLOT[ww]][:, 128 * c:128 * c + 128], ident[:, :])
                last.then_inc(xT_in_psum, 1)

            def products(n, w, first):
                o = ps[:, 4 + w % 2, 0:WCOL]
                if not (first and w < 2):
                    pe.wait_ge(tok_copied, n - 1)
                hi, lo = xT_hi[w % 2], xT_lo[w % 2]
                pe.wait_ge(xT_hi_ready, n + 1)
                for c in range(NCHUNK):
                    nc.tensor.matmul(o, hi[:, c, :], wf_hi[:, c, :], start=(c == 0), stop=False)
                    nc.tensor.matmul(o, hi[:, c, :], wf_lo[:, c, :], start=False, stop=False)
                pe.wait_ge(xT_lo_ready, n + 1)
                for c in range(NCHUNK):
                    last = nc.tensor.matmul(o, lo[:, c, :], wf_hi[:, c, :], start=False, stop=(c == NCHUNK - 1))
                last.then_inc(tok_in_psum, 1)

            prepared(pe)

            def tile(hh, s, turn, first, last_band):
                for ww in range(GRID):
                    n = GRID * hh + ww
                    transposes(n, s, ww, hh, first)
                    if not (first and ww == 0):
                        products(n - 1, (ww - 1) % GRID, first)
                if last_band:
                    products(GRID * GRID - 1, GRID - 1, False)

            bands(pe, tile)
            leave(pe, 1)

            pe.wait_ge(win_split, 2)
            pe.wait_ge(halo_ready, 5)
            K = (HALF, HALF + 1)

            def split3(o, lhs, rhs, hf_list=(0, 1)):
                for hf in hf_list:
                    (ah, al), (bh, bl) = lhs(hf), rhs(hf)
                    nc.tensor.matmul(o, ah, bh, start=(hf == 0), stop=False)
                    nc.tensor.matmul(o, ah, bl, start=False, stop=False)
                    last = nc.tensor.matmul(o, al, bh, start=False, stop=(hf == 1))
                return last

            def step2(i, s, turn, on):
                if on(0):
                    pe.wait_ge(xn_ready, i + 1)
                    for hf in range(2):
                        if isinstance(i, int) and i == 1:
                            pe.wait_ge(xnT_ready, hf + 1)
                        elif not isinstance(i, int) or i >= 2:
                            pe.wait_ge(proj_ready, 2 * (i - 2) + hf + 1)
                        for q in range(QUAD):
                            last = nc.tensor.transpose(ps[0:HALF, hf, 128 * q:128 * q + 128],
                                                       xn[s][:, q, hf * HALF:(hf + 1) * HALF], ident[:, :])
                        last.then_inc(xnT_in_psum, 1)
                if on(1):
                    b, p = i - 1, 1 - s

                    def tok(q):
                        return lambda hf: (xn_hi[p][0:K[hf], hf, 128 * q:128 * q + 128], xn_lo[p][0:K[hf], hf, 128 * q:128 * q + 128])

                    pe.wait_ge(xn_hi_ready, 2 * b + 2)
                    pe.wait_ge(xn_lo_ready, 2 * b + 2)
                    for pr_ in range(2):
                        if not isinstance(b, int) or b >= 1:
                            pe.wait_ge(gate_ready, 2 * (b - 1) + pr_ + 1)
                        for q in range(2):
                            last = split3(ps[:, 2 + 3 * pr_ + q, 0:2 * DIM], tok(2 * pr_ + q),
                                          lambda hf: (win_hi[0:K[hf], hf, DIM:3 * DIM], win_lo[0:K[hf], hf, DIM:3 * DIM]))
                        last.then_inc(zv_in_psum, 1)
                        for q in range(2):
                            last = split3(ps[:, 4 + 3 * pr_, DIMN * q:DIMN * (q + 1)], tok(2 * pr_ + q),
                                          lambda hf: (win_hi[0:K[hf], hf, 3 * DIM:], win_lo[0:K[hf], hf, 3 * DIM:]))
                        last.then_inc(zv_in_psum, 1)
                        if pr_ == 0:
                            for mh in range(2):
                                if on(0):
                                    pe.wait_ge(xnT_ready, 2 * i + mh + 1)
                                else:
                                    pe.wait_ge(proj_ready, 2 * b - 1 + mh)
                                last = split3(ps[0:HALF, mh, :],
                                              lambda hf: (win_hi[0:K[hf], hf, mh * HALF:(mh + 1) * HALF],
                                                          win_lo[0:K[hf], hf, mh * HALF:(mh + 1) * HALF]),
                                              lambda hf: (xn_hi[p][0:K[hf], hf, :], xn_lo[p][0:K[hf], hf, :]))
                                last.then_inc(proj_in_psum, 1)

            batches(pe, step2, 1)
            leave(pe, 2)

            def convolve(g, s, turn, first):
                pe.wait_ge(taps_loaded[s], 48 * (turn + 1))
                for c in range(CG):
                    if c == 0 and not first:
                        pe.wait_ge(conv_kept_act, g - 1)
                    if c == CG // 2 and not first:
                        pe.wait_ge(conv_kept_dve, g - 1)
                    o = ps[:, 4 * s + c // 2, NTOK * (c % 2):NTOK * (c % 2) + NTOK]
                    nc.tensor.matmul(o, src0[s][:, c, :], toep[s][:, c, 0:NTOK], start=True, stop=False)
                    last = nc.tensor.matmul(o, src1[s][0:TAP1, c, :], toep[s][0:TAP1, c, TAP0:TAP0 + NTOK], start=False, stop=True)
                    if c % 4 == 3:
                        last.then_inc(conv_in_psum, 1)

            pe.wait_ge(small_loaded, 16 * (4 + 2 * QUAD))
            for dh in range(2):
                for hf in range(2):
                    last = nc.tensor.transpose(ps[0:HALF, dh, HALF * hf:HALF * hf + K[hf]],
                                               w_out_sb[0:K[hf], hf, HALF * dh:HALF * dh + HALF], ident[0:K[hf], 0:K[hf]])
            last.then_inc(wo_turned, 1)
            pe.wait_ge(wo_copied, 1)
            for hf in range(2):
                for dh in range(2):
                    last = nc.tensor.matmul(ps[0:K[hf], 2 + hf, 0:NODEX], woT[:, dh, HALF * hf:HALF * hf + K[hf]],
                                            node_inT[:, dh, :], start=(dh == 0), stop=(dh == 1))
            last.then_inc(wo_turned, 1)
            pe.wait_ge(wo_nodes, 2)
            convolve(0, 0, 0, True)
            convolve(1, 1, 0, True)
            with pe.Fori(0, NGROUP // 2 - 1) as j:
                for s in range(2):
                    convolve(2 * j + 2 + s, s, j + 1, False)
            leave(pe, 3)

            pe.wait_ge(tree_set, 4)

            def turn_y(i, s):
                pe.wait_ge(y_ready, i + 1)
                for hf in range(2):
                    wait(pe, u_ready, 2 * i - 1 + hf if not isinstance(i, int) or i >= 1 else 0)
                    for q in range(QUAD):
                        last = nc.tensor.transpose(ps[0:HALF, hf, 128 * q:128 * q + 128],
                                                   gy[s][:, q, hf * HALF:(hf + 1) * HALF], ident[:, :])
                    last.then_inc(yT_in_psum, 1)

            turn_y(0, 0)

            def step4(i, s, turn, on):
                if on(-1):
                    turn_y(i + 1, 1 - s)
                if on(2):
                    b = i - 2
                    pe.wait_ge(coefT_ready, b + 1)
                    wait(pe, out_ready, 2 * b)
                    for k in range(2):
                        nc.tensor.matmul(ps[:, 6 + k, 0:2 * DIM], coefT[:, :],
                                         node_out[:, 2 * k:2 * k + 2, :].rearrange("p l d -> p (l d)"), start=True, stop=True)\
                            .then_inc(node_in_psum, 1)
                if on(0):
                    pe.wait_ge(u_ready, 2 * i + 2)
                    wait(pe, logit_ready, i)
                    for k in range(2):
                        for q in range(2):
                            for hf in range(2):
                                kk = K[hf]
                                last = nc.tensor.matmul(ps[:, 2 + k, DIMN * q:DIMN * (q + 1)],
                                                        uT[s][0:kk, hf, 128 * (2 * k + q):128 * (2 * k + q) + 128],
                                                        w_out_sb[0:kk, hf, :], start=(hf == 0), stop=(hf == 1))
                        last.then_inc(mix_in_psum, 1)
                if on(1):
                    pe.wait_ge(coef_ready, i)
                    nc.tensor.transpose(ps[:, 4, 0:128], coef[:, :, :].rearrange("p q n -> p (q n)"), ident[:, :])\
                        .then_inc(coefT_in_psum, 1)

            batches(pe, step4, 2)


NAMES = ["x", "cls_tok", "L0_tok_gamma", "L0_tok_beta", "L0_tok_W", "L0_tok_b", "L0_attn_w_in", "L0_attn_b_in",
         "L0_attn_w_filt", "L0_attn_b_filt", "L0_attn_w_short", "L0_attn_b_short", "L0_attn_w_out", "L0_attn_b_out",
         "L0_ffn_weights_in", "L0_ffn_weights_out"]


def kernel(**inputs):
    import concourse.bacc as bacc
    from concourse.bass_utils import run_bass_kernel_spmd

    nc = bacc.Bacc("TRN2", target_bir_lowering=False, num_devices=1)
    arrays = {n: np.ascontiguousarray(inputs[n]) for n in NAMES}
    arrays.update(constants())
    args = [nc.dram_tensor(f"in_{n}", a.shape, F32, kind="ExternalInput").ap() for n, a in arrays.items()]
    result = nc.dram_tensor("out_0", (NIMG, NTOK, DIM), F32, kind="ExternalOutput").ap()
    build(nc, *args, result)
    r = run_bass_kernel_spmd(nc, [{f"in_{n}": a for n, a in arrays.items()}], core_ids=[0])
    return r.results[0]["out_0"]
```

```python
import numpy as np
import concourse.bass as bass
from concourse import mybir

F32 = mybir.dt.float32
F32R = mybir.dt.float32r
ALU = mybir.AluOpType
ACT = mybir.ActivationFunctionType
AXIS = mybir.AxisListType

NIMG, IMG, CH, PATCH, DIM = 128, 224, 3, 16, 192
GRID = IMG // PATCH
NTOK = GRID * GRID + 1
QUAD = 4
NBATCH = -(-NTOK // QUAD)
PTOK = NBATCH * QUAD
HALF = DIM // 2
ROWF = IMG * CH
LEAD, PITCH = 4, 680
BAND = PATCH + 2
PXF = PATCH * CH
LEFTF = PXF * (GRID // 2) + 8
NFEAT = PATCH * PATCH * 5 * CH
NSHIFT = 5
RINGF = PXF + 2 * CH
PATF = BAND * RINGF
NCHUNK = 8
COPY_POOL = (4, 8, 13)
COPY_ACT = (6, 11)
OWN_DVE = [w for w in range(GRID) if w not in COPY_POOL + COPY_ACT]
EDGE_OPS = 6
PATCH_SLOT = [2 if w in COPY_POOL else (w - sum(v < w for v in COPY_POOL)) % 2 for w in range(GRID)]
WCOL = DIM + 2
KROW = NFEAT // 128
HCOL = DIM + 3
SPAD = NTOK // 2
TAP0 = 112
TAP1 = NTOK - TAP0
TAP1L = PTOK - TAP0
HANK = TAP0 + NTOK
GPADW = 424
CG = 8
HCG = CG // 2
NGROUP = DIM // CG
FFREQ = 64
NODES, NODEX = 21, 32
DIMN = DIM + NODEX
INNER = 15
TOK_EPS, LN_EPS = 1e-3, 1e-5
PIXEL_OF = ((0, 0), (0, -1), (0, 1), (-1, 0), (1, 0))

COPY_GAP = 1200
COPY_AT = [s * COPY_GAP + 111 - (di + 1) * RINGF - (dj + 1) * CH for s, (di, dj) in enumerate(PIXEL_OF)]


def constants():
    t = np.arange(NTOK, dtype=np.float64)[None, :]
    f = np.arange(FFREQ, dtype=np.float64)[:, None]
    basis = np.ones((FFREQ + 1, NTOK), np.float32)
    basis[:FFREQ] = np.sin(t * f / FFREQ)
    count = np.zeros((NCHUNK * 128, 1), np.float32)
    for di, dj in PIXEL_OF:
        for i in range(PATCH):
            at = (i + di + 1) * RINGF + (dj + 1) * CH
            count[at:at + PXF] += 1
    count = count.reshape(NCHUNK, 128).T
    return {"c_basis": basis, "c_count": count / np.float32(NFEAT)}


def build(nc, x, cls_tok, gamma, beta, W, tok_b, w_in, b_in, w_filt, b_filt, w_short, b_short,
          w_out, b_out, wn_in, wn_out, c_basis, c_count, out):
    def dram(name, shape):
        return nc.dram_tensor(name, shape, F32, kind="Internal").ap()

    wscr = dram("placed_weights", [NSHIFT * COPY_GAP, DIM])
    filt_scr = dram("padded_filter", [DIM, GPADW])
    h_scr = dram("h_tokens", [NIMG, PTOK, HCOL])
    gate_scr = dram("gates", [NIMG, PTOK, DIMN])
    proj_scr = dram("x_proj", [PTOK, DIM, NIMG])
    short_scr = dram("x_short", [HALF, 2, PTOK + 4, NIMG])

    class Region:
        def __init__(self, start):
            self.at = start

        def take(self, name, shape, dt=F32):
            size = 4 * int(np.prod(shape[1:]))
            t = nc.alloc_sbuf_tensor_at(name, shape, dt, offset=self.at)
            self.at += -(-size // 32) * 32
            return t

    base = -(-nc.sbuf_base // 32) * 32
    fixed = Region(base)
    ident = fixed.take("ident", [128, 128])
    zeros = fixed.take("zeros", [128, ROWF])
    w_out_sb = fixed.take("w_out_sb", [HALF + 1, 2, DIMN])
    node_out = fixed.take("node_out", [128, QUAD, DIM])
    node_inT = fixed.take("node_inT", [HALF, 2, NODEX])
    taps = fixed.take("taps", [HALF, 2, 3])
    taps_b = fixed.take("taps_b", [HALF, 2])
    half_neg = fixed.take("half_neg", [128, 16])
    big = fixed.at

    r1 = Region(big)
    band = [r1.take(f"band{s}", [128, BAND, PITCH]) for s in range(2)]
    wf_parts = r1.take("wf_parts", [128, NCHUNK, 2 * WCOL], F32R)
    wf_hi, wf_lo = wf_parts[:, :, 0:WCOL], wf_parts[:, :, WCOL:]
    xT_hi = [r1.take(f"xT_hi{s}", [128, NCHUNK, 128], F32R) for s in range(2)]
    xT_lo = [r1.take(f"xT_lo{s}", [128, NCHUNK, 128], F32R) for s in range(2)]
    praw = [r1.take(f"praw{s}", [128, GRID, WCOL]) for s in range(2)]
    htile = [r1.take(f"htile{s}", [128, GRID, HCOL]) for s in range(2)]
    prep_end = r1.at
    patch = [r1.take(f"patch{s}", [128, NCHUNK * 128]) for s in range(3)]
    sq_rows = r1.take("sq_rows", [128, 2, 2, ROWF])
    sq_cols = r1.take("sq_cols", [128, GRID + 1, PATCH, 6])
    tok_bias = r1.take("tok_bias", [128, DIM])
    core_sum = [r1.take(f"core_sum{s}", [128, GRID]) for s in range(2)]
    row_sum = r1.take("row_sum", [128, GRID])
    col_sum = r1.take("col_sum", [128, GRID + 1])
    sum_a = r1.take("sum_a", [128, GRID])
    sum_b = r1.take("sum_b", [128, GRID])
    musq = r1.take("musq", [128, GRID])
    tvar = r1.take("tvar", [128, GRID])
    trstd = [r1.take(f"trstd{s}", [128, GRID]) for s in range(2)]
    bn6 = r1.take("bn6", [128, GRID, 6])
    hvar = r1.take("hvar", [128, GRID])
    rows_in, rows_out = (bass.AP(tensor=sq_rows[:, :, :, :].tensor, offset=sq_rows[:, 0, b, 0:1].offset,
                                 ap=[sq_rows[:, :, :, :].ap[0], [step * ROWF, 2], [1, ROWF]]) for b, step in ((0, 3), (1, 1)))
    pr = Region(big + 4 * BAND * PITCH)
    w_nat = pr.take("w_nat", [128, KROW, DIM])
    w_sc = pr.take("w_scaled", [128, KROW, DIM])
    pr2 = Region(big + 8 * BAND * PITCH + 8 * NCHUNK * WCOL)
    w_sh = pr2.take("w_shown", [128, NSHIFT, NCHUNK, DIM])
    wf = pr2.take("wf", [128, NCHUNK, WCOL])
    gam = pr2.take("gam", [128, KROW])
    bet = pr2.take("bet", [128, KROW])
    ones = pr2.take("ones", [128, 128])
    csum = pr2.take("csum", [128, DIM])
    bias_row = pr2.take("bias_row", [1, DIM])
    cnt = pr2.take("cnt", [128, NCHUNK])
    cnt_neg = pr2.take("cnt_neg", [128, NCHUNK])
    filt_w = pr2.take("filt_w", [FFREQ + 1, DIM])
    filt_b = pr2.take("filt_basis", [FFREQ + 1, NTOK])
    filt_p = pr2.take("filt_pad", [HALF, 2, GPADW])
    nodes = pr2.take("nodes", [NODEX, DIM])
    node_m = pr2.take("node_mean", [NODEX, 1])
    cls_h = pr2.take("cls_h", [128, HCOL])
    cls6 = pr2.take("cls6", [128, 6])
    cls_v = pr2.take("cls_v", [128, 1])

    r2 = Region(big)
    win = r2.take("win", [HALF + 1, 2, 3 * DIM + DIMN])
    win_hi = r2.take("win_hi", [HALF + 1, 2, 3 * DIM + DIMN], F32R)
    win_lo = r2.take("win_lo", [HALF + 1, 2, 3 * DIM + DIMN], F32R)
    hin = [r2.take(f"hin{s}", [128, QUAD, HCOL]) for s in range(2)]
    xn = [r2.take(f"xn{s}", [128, QUAD, DIM]) for s in range(2)]
    xnT = [r2.take(f"xnT{s}", [HALF, 2, QUAD + 2, 128]) for s in range(2)]
    xn_hi = [r2.take(f"xn_hi{s}", [HALF + 1, 2, QUAD * 128], F32R) for s in range(2)]
    xn_lo = [r2.take(f"xn_lo{s}", [HALF + 1, 2, QUAD * 128], F32R) for s in range(2)]
    silu = [r2.take(f"silu{p}", [128, 2, DIM]) for p in range(2)]
    szv = [r2.take(f"szv{p}", [128, 2, DIMN]) for p in range(2)]
    gate = [r2.take(f"gate{s}", [128, QUAD, DIMN]) for s in range(2)]
    short = [r2.take(f"short{s}", [HALF, 2, QUAD * 128]) for s in range(2)]
    proj = [r2.take(f"proj{s}", [HALF, 2, QUAD, 128]) for s in range(2)]

    woT = zeros[0:HALF, 0:2 * (DIM + 1)].rearrange("p (h k) -> p h k", h=2)

    r3 = Region(big)
    Y = r3.take("Y", [128, PTOK, DIM])
    after_y = r3.at
    src0 = [r3.take(f"src0_{s}", [TAP0, CG, 128]) for s in range(2)]
    src1 = [r3.take(f"src1_{s}", [TAP1L, CG, 128]) for s in range(2)]
    toep = [r3.take(f"toep{s}", [TAP0, CG, HANK]) for s in range(2)]

    r4 = Region(after_y)
    gy = [r4.take(f"gy{s}", [128, QUAD, DIMN]) for s in range(2)]
    raw = [r4.take(f"raw{s}", [128, QUAD, NODEX]) for s in range(2)]
    lgh = [r4.take(f"lgh{s}", [128, QUAD, NODEX]) for s in range(2)]
    sh = [r4.take(f"sh{s}", [HALF, 2, QUAD * 128]) for s in range(2)]
    hb = [r4.take(f"hb{s}", [128, QUAD, HCOL]) for s in range(2)]
    h2 = [r4.take(f"h2_{s}", [128, QUAD, DIM]) for s in range(2)]
    ob = [r4.take(f"ob{s}", [128, QUAD, DIM]) for s in range(2)]
    uT = [r4.take(f"uT{s}", [HALF + 1, 2, QUAD * 128]) for s in range(2)]
    bn4 = r4.take("bn4", [128, QUAD, 6])
    mv4 = r4.take("mv4", [128, QUAD, 2])
    var4 = r4.take("var4", [128, QUAD])
    rstd4 = [r4.take(f"rstd4_{s}", [128, QUAD]) for s in range(2)]
    logit = r4.take("logit", [128, QUAD, NODEX])
    gel = r4.take("gel", [128, QUAD, NODEX])
    branch = r4.take("branch", [128, QUAD, INNER, 2])
    visit = r4.take("visit", [128, QUAD, NODEX])
    act = r4.take("act", [128, QUAD, NODEX])
    coef = r4.take("coef", [128, QUAD, NODEX])
    tail = r4.take("tail", [128, QUAD])
    coefT = r4.take("coefT", [128, 128])
    assert max(r1.at, r2.at, r3.at, r4.at) <= nc.sbuf_usable_end, (r1.at, r2.at, r3.at, r4.at)
    assert r2.at <= big + 8 * BAND * PITCH
    assert pr.at <= big + 8 * BAND * PITCH and pr2.at <= prep_end, (pr.at, pr2.at, prep_end)

    ps = nc.alloc_psum_tensor("psum", [128, 8, 512], F32)

    S = nc.alloc_semaphore

    LATE_STEPS = 3
    BIAS_STEP = 13
    carried = S("carried")
    phase_left = S("phase_left")
    w_loaded, gb_loaded, tables_loaded, small_loaded = S("w_loaded"), S("gb_loaded"), S("tables_loaded"), S("small_loaded")
    consts_set, ident_set, cls_step = S("consts_set"), S("ident_set"), S("cls_step")
    prep_dve, prep_pe, prep_pool = S("prep_dve"), S("prep_pe"), S("prep_pool")
    cleared = S("cleared")
    scaled_stored, filter_stored, half_scaled = S("scaled_stored"), S("filter_stored"), S("half_scaled")
    shifted_loaded = [S(f"shifted_loaded{s}") for s in range(NSHIFT)]
    pads_stored, cls_stored = S("pads_stored"), S("cls_stored")
    band_loaded = [S(f"band_loaded{s}") for s in range(2)]
    left_loaded = S("left_loaded")
    ring_zeroed = S("ring_zeroed")
    patch_dve, patch_pool, patch_act = S("patch_dve"), S("patch_pool"), S("patch_act")
    xT_in_psum, xT_hi_ready, xT_lo_ready = S("xT_in_psum"), S("xT_hi_ready"), S("xT_lo_ready")
    tok_in_psum, tok_copied, tok_summed = S("tok_in_psum"), S("tok_copied"), S("tok_summed")
    core_squared, edge_squared, edge_dif, edges_summed = S("core_squared"), S("edge_squared"), S("edge_dif"), S("edges_summed")
    tvar_ready, trstd_ready, h_ready, hstat_ready = S("tvar_ready"), S("trstd_ready"), S("h_ready"), S("hstat_ready")
    h_stored = [S(f"h_stored{s}") for s in range(2)]
    h_made, bn_made = S("h_made"), S("bn_made")
    dve_step = S("dve_step")
    pool_step = S("pool_step")
    win_loaded, win_split, win_his, win_nodes = S("win_loaded"), S("win_split"), S("win_his"), S("win_nodes")
    hin_loaded = [S(f"hin_loaded{s}") for s in range(2)]
    xn_ready, xnT_in_psum, xnT_ready, xn_hi_ready, xn_lo_ready = (
        S("xn_ready"), S("xnT_in_psum"), S("xnT_ready"), S("xn_hi_ready"), S("xn_lo_ready"))
    ones_set = S("ones_set")
    halo_ready, centre_ready, short_ready = S("halo_ready"), S("centre_ready"), S("short_ready")
    zv_in_psum, silu_ready, gate_ready = S("zv_in_psum"), S("silu_ready"), S("gate_ready")
    proj_in_psum, proj_ready = S("proj_in_psum"), S("proj_ready")
    gate_stored = [S(f"gate_stored{s}") for s in range(2)]
    short_stored = [S(f"short_stored{s}") for s in range(2)]
    proj_stored = [S(f"proj_stored{s}") for s in range(2)]
    taps_loaded = [[S(f"taps_loaded{s}{q}") for q in range(2)] for s in range(2)]
    conv_in_psum, conv_kept_act, conv_kept_dve, y_padded = (
        S("conv_in_psum"), S("conv_kept_act"), S("conv_kept_dve"), S("y_padded"))
    gy_loaded = [S(f"gy_loaded{s}") for s in range(2)]
    hb_loaded = [S(f"hb_loaded{s}") for s in range(2)]
    wo_turned, wo_copied, wo_nodes = S("wo_turned"), S("wo_copied"), S("wo_nodes")
    y_ready, yT_in_psum, u_ready, mix_in_psum, h2_ready = (
        S("y_ready"), S("yT_in_psum"), S("u_ready"), S("mix_in_psum"), S("h2_ready"))
    var_ready, rstd_ready = S("var_ready"), S("rstd_ready")
    raw_ready = S("raw_ready")
    lgh_ready, logit_ready, visit_step = S("lgh_ready"), S("logit_ready"), S("visit_step")
    VISITS = 6
    gel_ready, coef_ready, coefT_in_psum, coefT_ready = (
        S("gel_ready"), S("coef_ready"), S("coefT_in_psum"), S("coefT_ready"))
    node_in_psum, out_ready, tree_set = S("node_in_psum"), S("out_ready"), S("tree_set")
    out_stored = [S(f"out_stored{s}") for s in range(2)]

    def wait(eng, sem, value):
        if not isinstance(value, int) or value > 0:
            eng.wait_ge(sem, value)

    def hold(eng, sem, value):
        if not isinstance(value, int) or value > 0:
            eng.wait_ge(sem, value)
            if not isinstance(value, int):
                eng.sem_inc(carried, 1)

    def leave(eng, n):
        eng.drain().then_inc(phase_left, 1)
        eng.wait_ge(phase_left, 5 * n)

    def bands(eng, tile):
        for hh in range(3):
            tile(hh, hh % 2, hh // 2, hh == 0, False)
        with eng.Fori(0, (GRID - 4) // 2) as j:
            tile(2 * j + 3, 1, j + 1, False, False)
            tile(2 * j + 4, 0, j + 2, False, False)
        tile(GRID - 1, 1, (GRID - 1) // 2, False, True)

    def batches(eng, step, lag, n=NBATCH, lead=2):
        def peeled(i):
            step(i, i % 2, i // 2, lambda d: 0 <= i - d < n)

        first = 4
        pairs = (n - first - lead) // 2
        for i in range(first):
            peeled(i)
        with eng.Fori(0, pairs) as j:
            for k in range(2):
                i = first + k
                step(2 * j + i, i % 2, j + i // 2, lambda d: True)
        for i in range(first + 2 * pairs, n + lag):
            peeled(i)

    def prepared(eng):
        eng.wait_ge(prep_dve, 3)
        eng.wait_ge(prep_pool, 3)
        eng.wait_ge(filter_stored, 16)
        eng.wait_ge(cls_stored, 16)

    def lay_out(eng, n, s, ww):
        slot = PATCH_SLOT[ww]
        back = next(d for d in range(1, GRID + 1) if PATCH_SLOT[(ww - d) % GRID] == slot)
        if not isinstance(n, int) or n >= back:
            hold(eng, xT_in_psum, n - back + 1) if eng is nc.gpsimd else eng.wait_ge(xT_in_psum, n - back + 1)
        at = LEAD - CH + PXF * ww
        dst, src = patch[slot][:, 0:PATF].rearrange("p (r f) -> p r f", f=RINGF), band[s][:, :, at:at + RINGF]
        return eng.activation(dst, src, ACT.Copy) if eng is nc.scalar else eng.tensor_copy(dst, src)

    def load_h(eng, i, s):
        eng.dma_start(hb[s][:, :, :], h_scr[:, bass.ds(QUAD * i, QUAD), :]).then_inc(hb_loaded[s], 16)

    def place_weights(eng, odd):
        eng.wait_ge(*((prep_dve, 1) if odd else (half_scaled, 1)))
        for i in range(PATCH):
            src = w_sc[8 * i:8 * i + 8, CH * NSHIFT * odd:CH * NSHIFT * (odd + 1), :].rearrange("p (s c) d -> p s (c d)", c=CH)
            dst = bass.AP(tensor=wscr.tensor, offset=(111 + i * RINGF + CH * odd) * DIM,
                          ap=[[2 * CH * DIM, 8], [COPY_GAP * DIM, NSHIFT], [1, CH * DIM]])
            eng.dma_start(dst, src).then_inc(scaled_stored, 16)

    def rep(row, n):
        return bass.AP(tensor=row.tensor, offset=row.offset, ap=[[0, n]] + [list(a) for a in row.ap])

    with nc.Block() as block:
        @block.sync
        def _(sp):
            sp.dma_start(w_nat[:, :, :], W.rearrange("(p k) d -> p k d", k=KROW)).then_inc(w_loaded, 16)
            sp.dma_start(gam[:, :], gamma.rearrange("(p k) -> p k", k=KROW)).then_inc(gb_loaded, 16)
            sp.dma_start(bet[:, :], beta.rearrange("(p k) -> p k", k=KROW)).then_inc(gb_loaded, 16)
            sp.dma_start(bias_row[:, :], rep(tok_b, 1)).then_inc(gb_loaded, 16)
            for dst, src in ((cnt[:, :], c_count),
                             (filt_w[0:FFREQ, :], w_filt), (filt_w[FFREQ:FFREQ + 1, :], rep(b_filt, 1)),
                             (filt_b[:, :], c_basis), (nodes[0:NODES, :], wn_in),
                             (nodes[NODES:NODEX, :], rep(wn_in[NODES - 1, :], NODEX - NODES)),
                             (cls_h[:, 0:DIM], rep(cls_tok[0, 0, :], 128))):
                sp.dma_start(dst, src).then_inc(tables_loaded, 16)
            sp.wait_ge(consts_set, 7)
            sp.wait_ge(prep_pool, 1)
            first, behind = 111, 111 + (PATCH - 1) * RINGF + PXF
            gap = (RINGF - PXF) * DIM

            def clear(row, parts, times, width, part_step, time_step):
                z = wf[:, :, :]
                sp.dma_start(bass.AP(tensor=wscr.tensor, offset=row * DIM, ap=[[part_step, parts], [time_step, times], [1, width]]),
                             bass.AP(tensor=z.tensor, offset=z.offset, ap=[[z.ap[0][0], parts], [0, times], [1, width]]))\
                    .then_inc(cleared, 16)

            clear(first + PXF, PATCH - 1, NSHIFT, gap, RINGF * DIM, COPY_GAP * DIM)
            clear(behind, (COPY_GAP + first - behind) * DIM // gap, NSHIFT - 1, gap, gap, COPY_GAP * DIM)
            clear(0, first // 3, 1, 3 * DIM, 3 * DIM, 0)
            clear((NSHIFT - 1) * COPY_GAP + behind, (COPY_GAP - behind) // 3, 1, 3 * DIM, 3 * DIM, 0)
            assert (COPY_GAP + first - behind) * DIM % gap == 0 and first % 3 == 0 and (COPY_GAP - behind) % 3 == 0
            sp.dma_start(band[0][:, 0, LEAD:LEAD + ROWF], zeros[:, :]).then_inc(ring_zeroed, 16)
            sp.wait_ge(ring_zeroed, 16)

            def load_band(hh, s, lo, hi):
                src = x.rearrange("b h w c -> b (h w c)")[:, bass.ds((PATCH * hh - 1 + lo) * ROWF, (hi - lo) * ROWF)]
                sp.dma_start(band[s][:, lo:hi, LEAD:LEAD + ROWF],
                             src.rearrange("b (r f) -> b r f", f=ROWF)).then_inc(band_loaded[s], 16)

            place_weights(sp, 0)
            sp.wait_ge(prep_dve, 2)
            sp.dma_start(filt_scr.rearrange("(h p) k -> p h k", p=HALF), filt_p[:, :, :]).then_inc(filter_stored, 16)
            sp.wait_ge(prep_pool, 2)
            sp.dma_start(h_scr[:, 0, :], cls_h[:, :]).then_inc(cls_stored, 16)
            sp.wait_ge(scaled_stored, 32 * PATCH)
            sp.wait_ge(cleared, 64)
            for s in range(NSHIFT):
                sp.dma_start(w_sh[:, s, :, :], wscr[COPY_AT[s]:COPY_AT[s] + 128 * NCHUNK, :].rearrange("(c p) d -> p c d", p=128))\
                    .then_inc(shifted_loaded[s], 16)
            rows0 = x.rearrange("b h w c -> b (h w c)")[:, 0:(BAND - 1) * ROWF].rearrange("b (r f) -> b r f", f=ROWF)
            for f0, f1, sem in ((0, LEFTF, left_loaded), (LEFTF, ROWF, band_loaded[0])):
                sp.dma_start(band[0][:, 1:, LEAD + f0:LEAD + f1], rows0[:, :, f0:f1]).then_inc(sem, 16)
            sp.dma_start(h_scr[:, NTOK:PTOK, :], zeros[:, 0:(PTOK - NTOK) * HCOL].rearrange("p (l d) -> p l d", d=HCOL))\
                .then_inc(pads_stored, 16)
            sp.dma_start(short_scr[:, :, PTOK, :], zeros[0:HALF, 0:256].rearrange("p (h b) -> p h b", h=2))\
                .then_inc(pads_stored, 16)
            sp.dma_start(w_out_sb[0:HALF, :, 0:DIM], w_out.rearrange("(h p) d -> p h d", p=HALF)).then_inc(small_loaded, 16)
            sp.dma_start(w_out_sb[HALF:HALF + 1, 1, 0:DIM], rep(b_out, 1)).then_inc(small_loaded, 16)
            sp.dma_start(taps[:, :, :], w_short.rearrange("(h p) o k -> p h (o k)", p=HALF)).then_inc(small_loaded, 16)
            sp.dma_start(taps_b[:, :], b_short.rearrange("(h p) -> p h", p=HALF), allow_slow_non_contiguous=True).then_inc(small_loaded, 16)
            for q in range(QUAD):
                sp.dma_start(node_out[NODEX * q:NODEX * q + NODES, q, :], wn_out).then_inc(small_loaded, 16)
                sp.dma_start(node_out[NODEX * q + NODES:NODEX * (q + 1), q, :],
                             rep(wn_out[NODES - 1, :], NODEX - NODES)).then_inc(small_loaded, 16)
            sp.wait_ge(prep_dve, 3)
            sp.wait_ge(prep_pe, 4)
            sp.wait_ge(prep_pool, 3)

            def store_h(hh, s):
                sp.wait_ge(hstat_ready, hh + 1)
                sp.dma_start(h_scr[:, bass.ds(GRID * hh + 1, GRID), :], htile[s][:, :, :]).then_inc(h_stored[s], 16)

            def left_band(hh):
                hold(sp, patch_dve, len(OWN_DVE) * (hh - 1))
                hold(sp, patch_act, len(COPY_ACT) * (hh - 1))
                hold(sp, patch_pool, len(COPY_POOL) * (hh - 1))

            load_band(1, 1, 0, BAND)
            with sp.Fori(0, (GRID - 4) // 2) as j:
                for k in range(2):
                    hh = 2 * j + 2 + k
                    left_band(hh)
                    hold(sp, edge_squared, EDGE_OPS * (hh - 1))
                    sp.wait_ge(core_squared, GRID * (hh - 1))
                    load_band(hh, k, 0, BAND)
                    store_h(hh - 2, k)
            for hh in (GRID - 2, GRID - 1):
                s = hh % 2
                left_band(hh)
                hold(sp, edge_squared, EDGE_OPS * (hh - 1))
                sp.wait_ge(core_squared, GRID * (hh - 1))
                if hh == GRID - 1:
                    sp.dma_start(band[s][:, BAND - 1, LEAD:LEAD + ROWF], zeros[:, :]).then_inc(ring_zeroed, 16)
                    sp.wait_ge(ring_zeroed, 32)
                    load_band(hh, s, 0, BAND - 1)
                else:
                    load_band(hh, s, 0, BAND)
                store_h(hh - 2, s)
            sp.wait_ge(pads_stored, 32)
            sp.wait_ge(cls_stored, 16)
            sp.wait_ge(filter_stored, 16)
            left_band(GRID)
            sp.wait_ge(edge_squared, EDGE_OPS * (GRID - 1))
            sp.wait_ge(core_squared, GRID * (GRID - 1))
            sp.dma_start(win[0:HALF, :, 0:4 * DIM], w_in.rearrange("(h p) n -> p h n", p=HALF)).then_inc(win_loaded, 16)
            sp.dma_start(win[HALF:HALF + 1, 1, 0:4 * DIM], rep(b_in, 1)).then_inc(win_loaded, 16)

            def load_hin(i, s):
                sp.dma_start(hin[s][:, :, :], h_scr[:, bass.ds(QUAD * i, QUAD), :]).then_inc(hin_loaded[s], 16)

            sp.wait_ge(h_stored[0], 16)
            load_hin(0, 0)
            load_hin(1, 1)
            store_h(GRID - 2, 0)
            for s in range(2):
                sp.wait_ge(h_stored[s], 16 * (GRID // 2 - s))
            leave(sp, 1)


            def step2(i, s, turn, on):
                if on(-2):
                    if not isinstance(i, int):
                        sp.wait_ge(h_stored[1], 16 * GRID // 2)
                    hold(sp, xn_ready, i + 1)
                    load_hin(i + 2, s)
                if on(1):
                    b, p = i - 1, 1 - s
                    sp.wait_ge(short_ready, 2 * b + 2)
                    sp.dma_start(short_scr[:, :, bass.ds(QUAD * b, QUAD), :].rearrange("p h l b -> p h (l b)"),
                                 short[p][:, :, :]).then_inc(short_stored[p], 16)
                    for hf in range(2):
                        sp.wait_ge(proj_ready, 2 * b + hf + 1)
                        dst = proj_scr[bass.ds(QUAD * b, QUAD), hf * HALF:(hf + 1) * HALF, :]
                        sp.dma_start(dst.rearrange("l d b -> d l b"), proj[p][:, hf, :, :]).then_inc(proj_stored[p], 16)
                    sp.wait_ge(gate_ready, 2 * b + 2)
                    sp.dma_start(gate_scr[:, bass.ds(QUAD * b, QUAD), :], gate[p][:, :, :]).then_inc(gate_stored[p], 16)
                if isinstance(i, int) and i == LATE_STEPS:
                    store_h(GRID - 1, 1)

            batches(sp, step2, 1)
            for s in range(2):
                n = NBATCH // 2
                sp.wait_ge(short_stored[s], 16 * n)
                sp.wait_ge(proj_stored[s], 32 * n)
                sp.wait_ge(gate_stored[s], 16 * n)
            leave(sp, 2)

            def load_half(g, s, q):
                sem, at, to = taps_loaded[s][q], g * CG + q * HCG, slice(q * HCG, (q + 1) * HCG)
                windows = bass.AP(tensor=filt_scr.tensor, offset=at * GPADW, ap=[[1, TAP0], [GPADW, HCG], [1, HANK]])
                sp.dma_start(toep[s][:, to, :], windows).then_inc(sem, 16)
                sp.dma_start(src0[s][:, to, :], proj_scr[0:TAP0, bass.ds(at, HCG), :]).then_inc(sem, 16)
                sp.dma_start(src1[s][:, to, :], proj_scr[TAP0:PTOK, bass.ds(at, HCG), :]).then_inc(sem, 16)

            for g in range(2):
                for q in range(2):
                    load_half(g, g, q)
            with sp.Fori(0, NGROUP // 2 - 1) as j:
                for s in range(2):
                    for q in range(2):
                        hold(sp, conv_in_psum, 4 * j + 2 * s + q + 1)
                        load_half(2 * j + s + 2, s, q)
            leave(sp, 3)

            def load_gates(i, s):
                sp.dma_start(gy[s][:, :, :], gate_scr[:, bass.ds(QUAD * i, QUAD), :]).then_inc(gy_loaded[s], 16)
                sp.dma_start(sh[s][:, :, :], short_scr[:, :, bass.ds(QUAD * i + 1, QUAD), :].rearrange("p h l b -> p h (l b)"))\
                    .then_inc(gy_loaded[s], 16)

            def gates_left(i):
                hold(sp, yT_in_psum, 2 * i + 2)
                hold(sp, u_ready, 2 * i + 2)
                hold(sp, raw_ready, i + 1)

            for i in range(2):
                load_gates(i, i)
                load_h(sp, i, i)
            gates_left(0)
            load_gates(2, 0)

            def step4(i, s, turn, on):
                if on(-3):
                    gates_left(i + 1)
                    load_gates(i + 3, 1 - s)
                if on(2):
                    b = i - 2
                    hold(sp, out_ready, 2 * b + 2)
                    n = NTOK - QUAD * (NBATCH - 1) if isinstance(b, int) and b == NBATCH - 1 else QUAD
                    sp.dma_start(out[:, bass.ds(QUAD * b, n), :], ob[s][:, 0:n, :]).then_inc(out_stored[s], 16)

            batches(sp, step4, 2, lead=3)
            for s in range(2):
                sp.wait_ge(out_stored[s], 16 * NBATCH // 2)

        @block.gpsimd
        def _(pool):
            nc.gpsimd.memset(ident[:, :], 0.0).then_inc(ident_set, 1)
            nc.gpsimd.memset(wf[:, :, :], 0.0).then_inc(prep_pool, 1)
            pool.wait_ge(ident_set, 1)
            nc.gpsimd.affine_select(out=ident[:, :], in_=ident[:, :], compare_op=ALU.not_equal, fill=1.0,
                                    base=0, pattern=[[-1, 128]], channel_multiplier=1).then_inc(ident_set, 1)
            pool.wait_ge(prep_dve, 2)
            pool.wait_ge(consts_set, 7)
            nc.gpsimd.tensor_tensor(cls_h[:, DIM + 1:DIM + 2], cls_v[:, :], half_neg[:, 0:1], ALU.pow).then_inc(cls_step, 1)
            pool.wait_ge(cls_step, 1)
            nc.gpsimd.tensor_tensor(cls_h[:, DIM + 2:HCOL], cls_v[:, :], cls_h[:, DIM + 1:DIM + 2], ALU.mult).then_inc(prep_pool, 1)
            pool.wait_ge(prep_dve, 3)
            pool.wait_ge(prep_pe, 4)
            pool.wait_ge(scaled_stored, 32 * PATCH)
            nc.gpsimd.memset(band[1][:, :, 0:LEAD], 0.0)
            nc.gpsimd.memset(band[1][:, :, LEAD + ROWF:PITCH], 0.0)
            for s in range(3):
                nc.gpsimd.memset(patch[s][:, PATF:], 0.0)
            pool.drain().then_inc(prep_pool, 1)

            def rsqrt_tokens(hh, s):
                pool.wait_ge(tvar_ready, hh + 1)
                nc.gpsimd.tensor_tensor(trstd[s][:, :], tvar[:, :], half_neg[:, 0:GRID], ALU.pow).then_inc(trstd_ready, 1)

            def rsqrt_h(hh, s):
                hold(pool, h_ready, hh + 1)
                nc.gpsimd.tensor_scalar(hvar[:, :], htile[s][:, :, DIM + 1], LN_EPS, None, ALU.add).then_inc(pool_step, 1)
                pool.wait_ge(pool_step, 2 * hh + 1)
                nc.gpsimd.tensor_tensor(htile[s][:, :, DIM + 1], hvar[:, :], half_neg[:, 0:GRID], ALU.pow).then_inc(pool_step, 1)
                pool.wait_ge(pool_step, 2 * hh + 2)
                nc.gpsimd.tensor_tensor(htile[s][:, :, DIM + 2], hvar[:, :], htile[s][:, :, DIM + 1], ALU.mult)\
                    .then_inc(hstat_ready, 1)

            def tile(hh, s, turn, first, last):
                if not first:
                    rsqrt_tokens(hh - 1, 1 - s)
                hold(pool, band_loaded[s], 16 * (turn + 1))
                for ww in COPY_POOL:
                    lay_out(nc.gpsimd, GRID * hh + ww, s, ww).then_inc(patch_pool, 1)
                    if ww == COPY_POOL[1]:
                        pool.wait_ge(edge_squared, EDGE_OPS * hh + 4)
                        nc.gpsimd.tensor_tensor(rows_in, rows_in, rows_out, ALU.subtract).then_inc(edge_dif, 1)
                        pool.wait_ge(edge_squared, EDGE_OPS * hh + 6)
                        nc.gpsimd.tensor_tensor(sq_cols[:, :, :, 0:CH], sq_cols[:, :, :, 0:CH], sq_cols[:, :, :, CH:],
                                                ALU.subtract).then_inc(edge_dif, 1)
                if not first:
                    rsqrt_h(hh - 1, 1 - s)
                if last:
                    rsqrt_tokens(hh, s)

            bands(pool, tile)
            leave(pool, 1)

            nc.gpsimd.memset(xnT[0][:, :, 0:2, :], 0.0).then_inc(halo_ready, 1)
            for s in range(2):
                nc.gpsimd.memset(xn_hi[s][HALF:HALF + 1, 1, :].bitcast(F32), 1.0).then_inc(halo_ready, 1)
                nc.gpsimd.memset(xn_lo[s][HALF:HALF + 1, 1, :].bitcast(F32), 0.0).then_inc(halo_ready, 1)

            def step2(i, s, turn, on):
                if on(-1):
                    hold(pool, xnT_ready, 2 * i + 2)
                    hold(pool, short_ready, 2 * i)
                    nc.gpsimd.tensor_copy(xnT[1 - s][:, :, 0:2, :], xnT[s][:, :, QUAD:QUAD + 2, :]).then_inc(halo_ready, 1)
                if isinstance(i, int) and i == LATE_STEPS:
                    rsqrt_h(GRID - 1, 1)

            batches(pool, step2, 0)
            leave(pool, 2)

            nc.gpsimd.memset(Y[:, NTOK:PTOK, :], 0.0).then_inc(y_padded, 1)
            leave(pool, 3)

            def gated(i, s, loads):
                pool.wait_ge(gy_loaded[s], 32 * loads)
                nc.gpsimd.tensor_tensor(gy[s][:, :, 0:DIM], gy[s][:, :, 0:DIM], Y[:, bass.ds(QUAD * i, QUAD), :], ALU.mult)\
                    .then_inc(y_ready, 1)

            def nodes_of_h(i, s, loads):
                pool.wait_ge(hb_loaded[s], 16 * loads)
                pool.wait_ge(raw_ready, i + 1)
                wait(pool, logit_ready, i - 1)
                nc.gpsimd.tensor_tensor(lgh[s][:, :, :], raw[s][:, :, :],
                                        hb[s][:, :, DIM + 2:HCOL].to_broadcast([128, QUAD, NODEX]), ALU.mult).then_inc(lgh_ready, 1)

            def walk(b, k):
                if k == 0:
                    hold(pool, coef_ready, b)
                    hold(pool, logit_ready, b + 1)
                elif k > 1:
                    pool.wait_ge(visit_step, VISITS * b + k)
                if k < 2:
                    ins = nc.gpsimd.tensor_scalar(branch[:, :, :, k], logit[:, :, 0:INNER], 0.0, None, (ALU.is_le, ALU.is_gt)[k])
                else:
                    n = 2 ** (k - 2)
                    p0 = n - 1
                    kids = visit[:, :, 2 * p0 + 1:2 * p0 + 1 + 2 * n].rearrange("p q (n c) -> p q n c", c=2)
                    ins = nc.gpsimd.tensor_tensor(kids, branch[:, :, p0:p0 + n, :],
                                                  visit[:, :, p0:p0 + n].unsqueeze(3).to_broadcast([128, QUAD, n, 2]), ALU.mult)
                ins.then_inc(visit_step, 1)

            pool.wait_ge(tree_set, 4)
            gated(0, 0, 1)
            nodes_of_h(0, 0, 1)
            gated(1, 1, 1)

            def step4(i, s, turn, on):
                if on(-2):
                    gated(i + 2, s, turn + 2)
                if on(-1):
                    nodes_of_h(i + 1, 1 - s, turn + s + 1)
                if on(0):
                    for k in range(VISITS):
                        if k == 4:
                            pool.wait_ge(var_ready, i + 1)
                            nc.gpsimd.tensor_tensor(rstd4[s][:, :], var4[:, :], half_neg[:, 0:QUAD], ALU.pow).then_inc(rstd_ready, 1)
                        walk(i, k)

            batches(pool, step4, 0)

        @block.scalar
        def _(act_e):
            place_weights(act_e, 1)
            prepared(act_e)

            sq_core = ps[:, 6:8, :].rearrange("p k b -> p (k b)")[:, 0:PATCH * PXF].rearrange("p (r f) -> p r f", f=PXF)

            def tile(hh, s, turn, first, last):
                act_e.wait_ge(left_loaded if first else band_loaded[s], 16 * (turn + 1))
                for ww in range(GRID):
                    if first and ww == 3:
                        act_e.wait_ge(band_loaded[s], 16)
                    n = GRID * hh + ww
                    nfirst = first and ww < 2
                    act_e.wait_ge(xT_in_psum, n + 1)
                    if not nfirst:
                        act_e.wait_ge(tok_in_psum, n - 1)
                    k = 2 * (ww % 2)
                    nc.scalar.activation(xT_hi[ww % 2][:, :, :].rearrange("p c b -> p (c b)"),
                                         ps[:, k:k + 2, :].rearrange("p k b -> p (k b)"), ACT.Copy).then_inc(xT_hi_ready, 1)
                    if ww == 0 and not first:
                        wait(act_e, tvar_ready, hh - 1)
                    v = LEAD + PXF * ww
                    wait(act_e, core_squared, n)
                    nc.scalar.activation(sq_core, band[s][:, 1:1 + PATCH, v:v + PXF], ACT.Square,
                                         accum_out=core_sum[s][:, ww:ww + 1]).then_inc(core_squared, 1)
                    if ww + 2 in COPY_ACT:
                        lay_out(nc.scalar, n + 2, s, ww + 2).then_inc(patch_act, 1)
                    if not (first and ww == 0):
                        copy_token(n - 1, s if ww else 1 - s, (ww - 1) % GRID, hh if ww else hh - 1, first)
                    edge_squares(hh, s, ww)
                if last:
                    copy_token(GRID * GRID - 1, s, GRID - 1, hh, False)

            def edge_squares(hh, s, ww):
                if ww == 3:
                    wait(act_e, edges_summed, 2 * hh)
                if 3 <= ww <= 6:
                    a, b = (ww - 3) // 2, (ww - 3) % 2
                    nc.scalar.activation(sq_rows[:, a, b, :], band[s][:, PATCH * b + a, LEAD:LEAD + ROWF], ACT.Square)\
                        .then_inc(edge_squared, 1)
                elif ww in (7, 8):
                    r0 = (ww - 7) * PATCH // 2
                    cols = bass.AP(tensor=band[s][:, :, :].tensor, offset=band[s][:, 1 + r0, LEAD - CH:LEAD].offset,
                                   ap=[band[s][:, :, :].ap[0], [PXF, GRID + 1], [PITCH, PATCH // 2], [1, 6]])
                    nc.scalar.activation(sq_cols[:, :, r0:r0 + PATCH // 2, :], cols, ACT.Square).then_inc(edge_squared, 1)

            def copy_token(n, s, ww, hh, first):
                act_e.wait_ge(tok_in_psum, n + 1)
                if ww == 0 and not first:
                    wait(act_e, h_ready, hh - 1)
                nc.scalar.activation(praw[s][:, ww, :], ps[:, 4 + ww % 2, WCOL:2 * WCOL], ACT.Copy).then_inc(tok_copied, 1)

            bands(act_e, tile)
            act_e.wait_ge(win_loaded, 32)
            act_e.wait_ge(win_nodes, 2)
            nc.scalar.activation(win_hi[0:HALF, 0, :], win[0:HALF, 0, :], ACT.Copy).then_inc(win_his, 1)
            nc.scalar.activation(win_hi[:, 1, :], win[:, 1, :], ACT.Copy).then_inc(win_his, 1)
            leave(act_e, 1)

            def step2(i, s, turn, on):
                if on(0):
                    for hf in range(2):
                        act_e.wait_ge(xnT_in_psum, 2 * i + hf + 1)
                        if hf == 0 and not (isinstance(i, int) and i < 2):
                            act_e.wait_ge(short_ready, 2 * i - 2)
                            act_e.wait_ge(halo_ready, 5 + i - 1)
                            act_e.wait_ge(xn_lo_ready, 2 * i - 2)
                        nc.scalar.activation(xnT[s][:, hf, 2:2 + QUAD, :], ps[0:HALF, hf, :], ACT.Copy).then_inc(xnT_ready, 1)
                    for hf in range(2):
                        act_e.wait_ge(xnT_ready, 2 * i + hf + 1)
                        if hf == 0:
                            wait(act_e, proj_in_psum, 2 * i - 2)
                            wait(act_e, zv_in_psum, 4 * i - 4)
                        nc.scalar.activation(xn_hi[s][0:HALF, hf, :], xnT[s][:, hf, 2:2 + QUAD, :], ACT.Copy).then_inc(xn_hi_ready, 1)
                    act_e.wait_ge(halo_ready, 5 + i)
                    for hf in range(2):
                        if hf == 0:
                            wait(act_e, short_stored[s], 16 * turn)
                        nc.scalar.activation(short[s][:, hf, :], xnT[s][:, hf, 1:1 + QUAD, :], ACT.Identity,
                                             bias=taps_b[:, hf:hf + 1], scale=taps[:, hf, 1:2]).then_inc(centre_ready, 1)
                if on(1):
                    b, p = i - 1, 1 - s
                    for pr_ in range(2):
                        act_e.wait_ge(zv_in_psum, 4 * b + 2 * pr_ + 1)
                        nc.scalar.activation(silu[pr_][:, :, :], ps[:, 2 + 3 * pr_:4 + 3 * pr_, 0:DIM], ACT.Silu).then_inc(silu_ready, 1)
                        if pr_ == 0:
                            for hf in range(2):
                                act_e.wait_ge(proj_in_psum, 2 * b + hf + 1)
                                if hf == 0:
                                    wait(act_e, proj_stored[p], 32 * (turn - 1 if s == 0 else turn))
                                nc.scalar.activation(proj[p][:, hf, :, :], ps[0:HALF, hf, :], ACT.Copy).then_inc(proj_ready, 1)

            batches(act_e, step2, 1)
            leave(act_e, 2)

            with act_e.Fori(0, NGROUP // 2) as j:
                for s in range(2):
                    g = 2 * j + s
                    act_e.wait_ge(conv_in_psum, 2 * g + 1)
                    v = ps[:, 4 * s:4 * s + 2, 0:2 * NTOK].rearrange("p k (c l) -> p l k c", c=2)[:, ::-1, :, :]
                    dst = Y[:, 0:NTOK, bass.ds(CG * g, 4)].rearrange("p l (k c) -> p l k c", k=2)
                    nc.scalar.activation(dst, v, ACT.Copy).then_inc(conv_kept_act, 1)
            leave(act_e, 3)

            def keep_nodes(i, s, loads):
                act_e.wait_ge(gy_loaded[s], 32 * loads)
                hold(act_e, lgh_ready, i - 1)
                nc.scalar.activation(raw[s][:, :, :], gy[s][:, :, DIM:DIMN], ACT.Copy).then_inc(raw_ready, 1)

            for i in range(2):
                keep_nodes(i, i, 1)

            def step4(i, s, turn, on):
                if on(-2):
                    keep_nodes(i + 2, s, turn + 2)
                if on(1):
                    b = i - 1
                    act_e.wait_ge(coefT_in_psum, b + 1)
                    wait(act_e, node_in_psum, 2 * b)
                    nc.scalar.activation(coefT[:, :], ps[:, 4, 0:128], ACT.Copy).then_inc(coefT_ready, 1)
                if on(-2):
                    hold(act_e, h2_ready, 2 * i + 2)
                    hold(act_e, lgh_ready, i + 1)
                    load_h(act_e, i + 2, s)
                if on(0):
                    act_e.wait_ge(logit_ready, i + 1)
                    act_e.wait_ge(rstd_ready, i + 1)
                    wait(act_e, coef_ready, i)
                    for q in range(QUAD):
                        nc.scalar.activation(gel[:, q, :], logit[:, q, :], ACT.Gelu,
                                             scale=rstd4[s][:, q:q + 1]).then_inc(gel_ready, 1)

            batches(act_e, step4, 1)

        @block.vector
        def _(dve):
            count = [0]

            def own(ins):
                count[0] += 1
                ins.then_inc(dve_step, 1)
                dve.wait_ge(dve_step, count[0])

            for t, v in ((zeros[:, :], 0.0), (half_neg[:, :], -0.5), (ones[:, :], 1.0), (filt_p[:, :, :], 0.0),
                         (node_out[:, :, :], 0.0),
                         (band[0][:, :, 0:LEAD], 0.0), (band[0][:, :, LEAD + ROWF:PITCH], 0.0)):
                nc.vector.memset(t, v).then_inc(consts_set, 1)
            dve.wait_ge(w_loaded, 16)
            dve.wait_ge(gb_loaded, 48)
            for k0, done in ((0, half_scaled), (KROW // 2, prep_dve)):
                ks = slice(k0, k0 + KROW // 2)
                nc.vector.tensor_tensor(w_sc[:, ks, :], w_nat[:, ks, :], gam[:, ks].unsqueeze(2).to_broadcast([128, KROW // 2, DIM]),
                                        ALU.mult).then_inc(done, 1)
            dve.wait_ge(tables_loaded, 16 * 7)
            own(nc.vector.tensor_reduce(node_m[:, :], nodes[:, :], AXIS.X, ALU.add))
            own(nc.vector.tensor_scalar(node_m[:, :], node_m[:, :], 1.0 / DIM, None, ALU.mult))
            own(nc.vector.tensor_scalar(nodes[:, :], nodes[:, :], node_m[:, 0:1], None, ALU.subtract))
            own(nc.vector.bn_stats(cls6[:, :], cls_h[:, 0:DIM]))
            own(nc.vector.bn_aggr(cls_h[:, DIM:DIM + 2], cls6[:, :]))
            own(nc.vector.tensor_scalar(cls_v[:, :], cls_h[:, DIM + 1:DIM + 2], LN_EPS, None, ALU.add))
            own(nc.vector.tensor_scalar(cnt_neg[:, :], cnt[:, :], -1.0, None, ALU.mult))
            dve.wait_ge(prep_pe, 1)
            for hf in range(2):
                own(nc.vector.tensor_copy(filt_p[:, hf, SPAD:SPAD + NTOK], ps[0:HALF, hf, 0:NTOK]))
                own(nc.vector.tensor_copy(node_inT[:, hf, :], ps[0:HALF, 2 + hf, 0:NODEX]))
            dve.drain().then_inc(prep_dve, 1)
            dve.wait_ge(prep_pe, 2)
            own(nc.vector.tensor_copy(csum[:, :], ps[:, 4, 0:DIM]))
            dve.wait_ge(prep_pe, 3)
            own(nc.vector.tensor_tensor(bias_row[:, :], ps[0:1, 5, 0:DIM], bias_row[:, :], ALU.add))
            dve.wait_ge(prep_pe, 4)
            own(nc.vector.tensor_copy(tok_bias[:, :], ps[:, 6, 0:DIM]))
            for s in range(2):
                dve.wait_ge(shifted_loaded[s], 16)
            dve.wait_ge(prep_pool, 1)
            own(nc.vector.tensor_tensor(wf[:, :, 0:DIM], w_sh[:, 0, :, :], w_sh[:, 1, :, :], ALU.add))
            for s in range(2, NSHIFT):
                dve.wait_ge(shifted_loaded[s], 16)
                own(nc.vector.tensor_tensor(wf[:, :, 0:DIM], wf[:, :, 0:DIM], w_sh[:, s, :, :], ALU.add))
            for j in range(NCHUNK):
                own(nc.vector.scalar_tensor_tensor(wf[:, j, 0:DIM], csum[:, :], cnt_neg[:, j:j + 1], wf[:, j, 0:DIM],
                                                   ALU.mult, ALU.add))
            own(nc.vector.tensor_copy(wf[:, :, DIM], cnt[:, :]))
            own(nc.vector.tensor_copy(wf_hi, wf[:, :, :]))
            own(nc.vector.tensor_tensor(wf_lo, wf[:, :, :], wf_hi.bitcast(F32), ALU.subtract))
            dve.drain().then_inc(prep_dve, 1)

            chain = count[0]
            CHAIN = 5

            def dve_patch(hh, s, turn, ww):
                if isinstance(hh, int) and hh == 0:
                    if ww in (0, GRID // 2):
                        dve.wait_ge(band_loaded[0] if ww else left_loaded, 16)
                elif ww == 0:
                    dve.wait_ge(band_loaded[s], 16 * (turn + 1))
                if ww in OWN_DVE:
                    lay_out(nc.vector, GRID * hh + ww, s, ww).then_inc(patch_dve, 1)

            def tile(hh, s, turn, first, last):
                if first:
                    dve_patch(hh, s, turn, 0)
                for ww in range(GRID):
                    n = GRID * hh + ww
                    if ww + 1 < GRID:
                        dve_patch(hh, s, turn, ww + 1)
                    elif not last:
                        dve_patch(hh + 1, 1 - s, turn + s, 0)
                    dve.wait_ge(xT_hi_ready, n + 1)
                    if not (first and ww < 2):
                        dve.wait_ge(tok_in_psum, n - 1)
                    k = 2 * (ww % 2)
                    nc.vector.tensor_tensor(xT_lo[ww % 2][:, :, :].rearrange("p c b -> p (c b)"),
                                            ps[:, k:k + 2, :].rearrange("p k b -> p (k b)"),
                                            xT_hi[ww % 2][:, :, :].rearrange("p c b -> p (c b)").bitcast(F32),
                                            ALU.subtract).then_inc(xT_lo_ready, 1)
                    if not (first and ww == 0):
                        sum_token(n - 1, s if ww else 1 - s, (ww - 1) % GRID, hh if ww else hh - 1, first)
                    if ww in (11, 13):
                        edge_sums(hh, s, (ww - 11) // 2)
                    if not first:
                        finish(hh - 1, 1 - s, ww)
                if last:
                    sum_token(GRID * GRID - 1, s, GRID - 1, hh, False)
                    finish(hh, s, 0)

            def sum_token(n, s, ww, hh, first):
                dve.wait_ge(tok_copied, n + 1)
                nc.vector.tensor_tensor(praw[s][:, ww, :], ps[:, 4 + ww % 2, 0:WCOL], praw[s][:, ww, :], ALU.add).then_inc(tok_summed, 1)

            def link(ins, hh, k):
                ins.then_inc(dve_step, 1)
                dve.wait_ge(dve_step, chain + CHAIN * hh + k + 1)

            def edge_sums(hh, s, part):
                dve.wait_ge(edge_dif, 2 * hh + part + 1)
                if part == 0:
                    nc.vector.tensor_reduce(row_sum[:, :], rows_in.rearrange("p a (w f) -> p w a f", f=PXF),
                                            AXIS.XY, ALU.add).then_inc(edges_summed, 1)
                else:
                    nc.vector.tensor_reduce(col_sum[:, :], sq_cols[:, :, :, 0:CH], AXIS.XY, ALU.add).then_inc(edges_summed, 1)

            def finish(hh, s, ww):
                if ww == 0:
                    dve.wait_ge(core_squared, GRID * hh + GRID)
                    dve.wait_ge(edges_summed, 2 * hh + 2)
                    dve.wait_ge(tok_summed, GRID * hh + GRID)
                    link(nc.vector.tensor_tensor(sum_b[:, :], col_sum[:, 0:GRID], col_sum[:, 1:GRID + 1], ALU.subtract), hh, 0)
                    link(nc.vector.scalar_tensor_tensor(sum_a[:, :], core_sum[s][:, :], 5.0, row_sum[:, :], ALU.mult, ALU.add), hh, 1)
                    link(nc.vector.tensor_tensor(sum_a[:, :], sum_a[:, :], sum_b[:, :], ALU.add), hh, 2)
                    link(nc.vector.tensor_tensor(musq[:, :], praw[s][:, :, DIM], praw[s][:, :, DIM], ALU.mult), hh, 3)
                    link(nc.vector.scalar_tensor_tensor(sum_a[:, :], sum_a[:, :], 1.0 / NFEAT, musq[:, :], ALU.mult, ALU.subtract), hh, 4)
                    wait(dve, trstd_ready, hh)
                    nc.vector.tensor_scalar(tvar[:, :], sum_a[:, :], 0.0, TOK_EPS, ALU.max, ALU.add).then_inc(tvar_ready, 1)
                end = ww == GRID - 1
                if ww == 2:
                    dve.wait_ge(trstd_ready, hh + 1)
                    if not isinstance(hh, int) or hh >= 2:
                        dve.wait_ge(h_stored[s], 16 * slot_turn(hh, s))
                for w in FINISH[0][ww]:
                    nc.vector.scalar_tensor_tensor(htile[s][:, w, 0:DIM], praw[s][:, w, 0:DIM], trstd[s][:, w:w + 1],
                                                   tok_bias[:, :], ALU.mult, ALU.add).then_inc(h_made, 1)
                for w in FINISH[1][ww]:
                    dve.wait_ge(h_made, GRID * hh + w + 1)
                    nc.vector.bn_stats(bn6[:, w, :], htile[s][:, w, 0:DIM]).then_inc(bn_made, 1)
                if FINISH[2][ww]:
                    hold(dve, bn_made, GRID * hh + FINISH[2][ww][-1] + 1)
                for w in FINISH[2][ww]:
                    ins = nc.vector.bn_aggr(htile[s][:, w, DIM:DIM + 2], bn6[:, w, :])
                if end:
                    ins.then_inc(h_ready, 1)

            def slot_turn(hh, s):
                return hh // 2 if isinstance(hh, int) else turn_of[0]

            turn_of = [0]
            first_slice = [2 + 11 * w // GRID for w in range(GRID)]
            FINISH = [[[w for w in range(GRID) if min(first_slice[w] + d, GRID - 1) == ww] for ww in range(GRID)]
                      for d in range(3)]

            def tile_outer(hh, s, turn, first, last):
                turn_of[0] = turn if s == 1 else turn - 1
                tile(hh, s, turn, first, last)

            bands(dve, tile_outer)

            dve.wait_ge(win_loaded, 32)
            nc.vector.memset(win[HALF:HALF + 1, 1, 4 * DIM:], 0.0).then_inc(win_nodes, 1)
            nc.vector.tensor_copy(win[0:HALF, :, 4 * DIM:], node_inT[:, :, :]).then_inc(win_nodes, 1)
            for hf, parts in ((0, HALF), (1, HALF + 1)):
                dve.wait_ge(win_his, hf + 1)
                nc.vector.tensor_tensor(win_lo[0:parts, hf, :], win[0:parts, hf, :], win_hi[0:parts, hf, :].bitcast(F32),
                                        ALU.subtract).then_inc(win_split, 1)

            def norm(i, s, turn):
                dve.wait_ge(hin_loaded[s], 16 * (turn + 1))
                if not (isinstance(i, int) and i < 2):
                    dve.wait_ge(xnT_in_psum, 2 * (i - 1))
                for q in range(QUAD):
                    ins = nc.vector.tensor_scalar(xn[s][:, q, :], hin[s][:, q, 0:DIM], hin[s][:, q, DIM:DIM + 1],
                                                  hin[s][:, q, DIM + 1:DIM + 2], ALU.subtract, ALU.mult)
                ins.then_inc(xn_ready, 1)

            norm(0, 0, 0)
            leave(dve, 1)
            steps2 = count[0]

            def step2(i, s, turn, on):
                if on(0):
                    if on(-1):
                        norm(i + 1, 1 - s, turn + (1 if s == 1 else 0))
                    for hf in range(2):
                        dve.wait_ge(xn_hi_ready, 2 * i + hf + 1)
                        if hf == 0:
                            wait(dve, proj_in_psum, 2 * i - 2)
                            wait(dve, zv_in_psum, 4 * i - 4)
                        nc.vector.tensor_tensor(xn_lo[s][0:HALF, hf, :], xnT[s][:, hf, 2:2 + QUAD, :].rearrange("p l b -> p (l b)"),
                                                xn_hi[s][0:HALF, hf, :].bitcast(F32), ALU.subtract).then_inc(xn_lo_ready, 1)
                    for hf in range(2):
                        dve.wait_ge(centre_ready, 2 * i + hf + 1)
                        nc.vector.scalar_tensor_tensor(short[s][:, hf, :], xnT[s][:, hf, 0:QUAD, :].rearrange("p l b -> p (l b)"),
                                                       taps[:, hf, 0:1], short[s][:, hf, :], ALU.mult, ALU.add).then_inc(left_ready, 1)
                    for hf in range(2):
                        dve.wait_ge(left_ready, 2 * i + hf + 1)
                        nc.vector.scalar_tensor_tensor(short[s][:, hf, :], xnT[s][:, hf, 2:2 + QUAD, :].rearrange("p l b -> p (l b)"),
                                                       taps[:, hf, 2:3], short[s][:, hf, :], ALU.mult, ALU.add).then_inc(short_ready, 1)
                if on(1):
                    b, p = i - 1, 1 - s
                    for pr_ in range(2):
                        dve.wait_ge(silu_ready, 2 * b + pr_ + 1)
                        nc.vector.tensor_tensor(szv[pr_][:, :, 0:DIM], ps[:, 2 + 3 * pr_:4 + 3 * pr_, DIM:2 * DIM],
                                                silu[pr_][:, :, :], ALU.mult).then_inc(szv_ready, 1)
                        dve.wait_ge(szv_ready, 2 * b + pr_ + 1)
                        dve.wait_ge(zv_in_psum, 4 * b + 2 * pr_ + 2)
                        if pr_ == 0:
                            wait(dve, gate_stored[p], 16 * (turn - 1 if s == 0 else turn))
                        nc.vector.tensor_tensor(gate[p][:, 2 * pr_:2 * pr_ + 2, :],
                                                ps[:, 4 + 3 * pr_, 0:2 * DIMN].rearrange("p (l d) -> p l d", l=2),
                                                szv[pr_][:, :, :], ALU.mult).then_inc(gate_ready, 1)

            def step2_late(i, s, turn, on):
                step2(i, s, turn, on)
                if isinstance(i, int) and i < LATE_STEPS:
                    for ww in range(1 + 13 * i // LATE_STEPS, 1 + 13 * (i + 1) // LATE_STEPS):
                        finish(GRID - 1, 1, ww)

            left_ready, szv_ready = S("left_ready"), S("szv_ready")
            for p in range(2):
                nc.vector.memset(szv[p][:, :, DIM:], 1.0).then_inc(ones_set, 1)
            dve.wait_ge(ones_set, 2)
            batches(dve, step2_late, 1)
            leave(dve, 2)

            dve.wait_ge(wo_turned, 1)
            nc.vector.tensor_copy(woT[:, :, :], ps[0:HALF, 0:2, 0:DIM + 1]).then_inc(wo_copied, 1)
            dve.wait_ge(wo_turned, 2)
            nc.vector.tensor_copy(w_out_sb[0:HALF, 0, DIM:DIMN], ps[0:HALF, 2, 0:NODEX]).then_inc(wo_nodes, 1)
            nc.vector.tensor_copy(w_out_sb[:, 1, DIM:DIMN], ps[0:HALF + 1, 3, 0:NODEX]).then_inc(wo_nodes, 1)
            with dve.Fori(0, NGROUP // 2) as j:
                for s in range(2):
                    g = 2 * j + s
                    dve.wait_ge(conv_in_psum, 2 * g + 2)
                    v = ps[:, 4 * s + 2:4 * s + 4, 0:2 * NTOK].rearrange("p k (c l) -> p l k c", c=2)[:, ::-1, :, :]
                    dst = Y[:, 0:NTOK, bass.ds(CG * g + 4, 4)].rearrange("p l (k c) -> p l k c", k=2)
                    nc.vector.tensor_copy(dst, v).then_inc(conv_kept_dve, 1)
            leave(dve, 3)

            for s in range(2):
                nc.vector.memset(uT[s][HALF:HALF + 1, 1, :], 1.0).then_inc(tree_set, 1)
            nc.vector.memset(visit[:, :, :], 1.0).then_inc(tree_set, 1)
            nc.vector.memset(coef[:, :, :], 0.0).then_inc(tree_set, 1)
            dve.wait_ge(tree_set, 4)
            stat_step, act_step = S("stat_step"), S("act_step")

            def add_short(i, s, loads):
                dve.wait_ge(gy_loaded[s], 32 * loads)
                for hf in range(2):
                    dve.wait_ge(yT_in_psum, 2 * i + hf + 1)
                    if hf == 0:
                        wait(dve, mix_in_psum, 2 * i - 2)
                    nc.vector.tensor_tensor(uT[s][0:HALF, hf, :], ps[0:HALF, hf, :], sh[s][:, hf, :], ALU.add)\
                        .then_inc(u_ready, 1)

            def add_h(b, s, k):
                dve.wait_ge(node_in_psum, 2 * b + k + 1)
                nc.vector.tensor_tensor(ob[s][:, 2 * k:2 * k + 2, :],
                                        ps[:, 6 + k, 0:2 * DIM].rearrange("p (l d) -> p l d", l=2),
                                        h2[s][:, 2 * k:2 * k + 2, :], ALU.add).then_inc(out_ready, 1)

            def coefficients(b, between):
                dve.wait_ge(gel_ready, QUAD * (b + 1))
                dve.wait_ge(visit_step, VISITS * (b + 1))
                nc.vector.tensor_tensor(act[:, :, 0:NODEX - 1], visit[:, :, 0:NODEX - 1], gel[:, :, 0:NODEX - 1], ALU.mult)\
                    .then_inc(act_step, 1)
                between(0)
                dve.wait_ge(act_step, 2 * b + 1)
                nc.vector.tensor_reduce(tail[:, :], act[:, :, INNER:NODEX - 1], AXIS.X, ALU.add).then_inc(act_step, 1)
                wait(dve, coefT_in_psum, b)
                kids = coef[:, :, 1:NODEX - 1].rearrange("p q (n c) -> p q n c", c=2)
                nc.vector.tensor_tensor(kids, branch[:, :, :, :],
                                        act[:, :, 0:INNER].unsqueeze(3).to_broadcast([128, QUAD, INNER, 2]), ALU.mult)
                dve.wait_ge(act_step, 2 * b + 2)
                nc.vector.scalar_tensor_tensor(coef[:, :, NODEX - 1], gel[:, :, NODES - 1], 5.0, tail[:, :], ALU.mult, ALU.add)\
                    .then_inc(coef_ready, 1)
                between(1)

            add_short(0, 0, 1)

            def step4(i, s, turn, on):
                if on(-1):
                    add_short(i + 1, 1 - s, turn + s + 1)

                def between(k):
                    if on(2):
                        if k == 0:
                            wait(dve, out_stored[s], 16 * (turn - 1))
                        add_h(i - 2, s, k)

                if on(1):
                    coefficients(i - 1, between)
                else:
                    between(0)
                    between(1)
                if on(0):
                    dve.wait_ge(hb_loaded[s], 16 * (turn + 1))
                    for k in range(2):
                        dve.wait_ge(mix_in_psum, 2 * i + k + 1)
                        if k == 0:
                            wait(dve, out_ready, 2 * i - 2)
                        nc.vector.tensor_tensor(h2[s][:, 2 * k:2 * k + 2, :],
                                                ps[:, 2 + k, 0:2 * DIMN].rearrange("p (l d) -> p l d", l=2)[:, :, 0:DIM],
                                                hb[s][:, 2 * k:2 * k + 2, 0:DIM], ALU.add).then_inc(h2_ready, 1)
                    dve.wait_ge(lgh_ready, i + 1)
                    wait(dve, gel_ready, QUAD * i)
                    wait(dve, visit_step, VISITS * i)
                    nc.vector.tensor_tensor(logit[:, :, :].rearrange("p (k l) n -> p k l n", k=2),
                                            ps[:, 2:4, 0:2 * DIMN].rearrange("p k (l d) -> p k l d", l=2)[:, :, :, DIM:DIMN],
                                            lgh[s][:, :, :].rearrange("p (k l) n -> p k l n", k=2), ALU.add).then_inc(logit_ready, 1)
                    dve.wait_ge(h2_ready, 2 * i + 2)
                    for q in range(QUAD):
                        ins = nc.vector.bn_stats(bn4[:, q, :], h2[s][:, q, :])
                    ins.then_inc(stat_step, 1)
                    hold(dve, stat_step, 2 * i + 1)
                    for q in range(QUAD):
                        ins = nc.vector.bn_aggr(mv4[:, q, :], bn4[:, q, :])
                    ins.then_inc(stat_step, 1)
                    dve.wait_ge(stat_step, 2 * i + 2)
                    wait(dve, rstd_ready, i)
                    nc.vector.tensor_scalar(var4[:, :], mv4[:, :, 1], LN_EPS, None, ALU.add).then_inc(var_ready, 1)

            batches(dve, step4, 2)

        @block.tensor
        def _(pe):
            pe.wait_ge(ident_set, 2)
            pe.wait_ge(tables_loaded, 16 * 7)
            pe.wait_ge(dve_step, 3)
            for hf in range(2):
                nc.tensor.matmul(ps[0:HALF, hf, 0:NTOK], filt_w[:, hf * HALF:(hf + 1) * HALF], filt_b[:, :], start=True, stop=True)
                last = nc.tensor.transpose(ps[0:HALF, 2 + hf, 0:NODEX], nodes[:, hf * HALF:(hf + 1) * HALF], ident[0:NODEX, 0:NODEX])
            last.then_inc(prep_pe, 1)
            pe.wait_ge(prep_dve, 1)
            pe.wait_ge(consts_set, 7)
            for k in range(KROW):
                last = nc.tensor.matmul(ps[:, 4, 0:DIM], ones[:, :], w_sc[:, k, :], start=(k == 0), stop=(k == KROW - 1))
            last.then_inc(prep_pe, 1)
            for k in range(KROW):
                last = nc.tensor.matmul(ps[0:1, 5, 0:DIM], bet[:, k:k + 1], w_nat[:, k, :], start=(k == 0), stop=(k == KROW - 1))
            last.then_inc(prep_pe, 1)
            pe.wait_ge(dve_step, BIAS_STEP)
            nc.tensor.matmul(ps[:, 6, 0:DIM], ones[0:1, :], bias_row[:, :], start=True, stop=True).then_inc(prep_pe, 1)

            def transposes(n, s, ww, hh, first):
                if ww in COPY_POOL:
                    pe.wait_ge(patch_pool, len(COPY_POOL) * hh + COPY_POOL.index(ww) + 1)
                elif ww in COPY_ACT:
                    pe.wait_ge(patch_act, len(COPY_ACT) * hh + COPY_ACT.index(ww) + 1)
                else:
                    pe.wait_ge(patch_dve, len(OWN_DVE) * hh + OWN_DVE.index(ww) + 1)
                if not (first and ww < 2):
                    pe.wait_ge(xT_lo_ready, n - 1)
                for c in range(NCHUNK):
                    last = nc.tensor.transpose(ps[:, 2 * (ww % 2) + c // 4, 128 * (c % 4):128 * (c % 4) + 128],
                                               patch[PATCH_SLOT[ww]][:, 128 * c:128 * c + 128], ident[:, :])
                last.then_inc(xT_in_psum, 1)

            def products(n, w, first):
                o = ps[:, 4 + w % 2, 0:2 * WCOL]
                if not (first and w < 2):
                    pe.wait_ge(tok_summed, n - 1)
                hi, lo = xT_hi[w % 2], xT_lo[w % 2]
                pe.wait_ge(xT_hi_ready, n + 1)
                for c in range(NCHUNK):
                    nc.tensor.matmul(o, hi[:, c, :], wf_parts[:, c, :], start=(c == 0), stop=False)
                pe.wait_ge(xT_lo_ready, n + 1)
                for c in range(NCHUNK):
                    last = nc.tensor.matmul(o[:, 0:WCOL], lo[:, c, :], wf_hi[:, c, :], start=False, stop=(c == NCHUNK - 1))
                last.then_inc(tok_in_psum, 1)

            prepared(pe)

            def tile(hh, s, turn, first, last_band):
                for ww in range(GRID):
                    n = GRID * hh + ww
                    transposes(n, s, ww, hh, first)
                    if not (first and ww == 0):
                        products(n - 1, (ww - 1) % GRID, first)
                if last_band:
                    products(GRID * GRID - 1, GRID - 1, False)

            bands(pe, tile)
            leave(pe, 1)

            pe.wait_ge(win_split, 2)
            pe.wait_ge(halo_ready, 5)
            K = (HALF, HALF + 1)

            def split3(o, lhs, rhs, hf_list=(0, 1)):
                for hf in hf_list:
                    (ah, al), (bh, bl) = lhs(hf), rhs(hf)
                    nc.tensor.matmul(o, ah, bh, start=(hf == 0), stop=False)
                    nc.tensor.matmul(o, ah, bl, start=False, stop=False)
                    last = nc.tensor.matmul(o, al, bh, start=False, stop=(hf == 1))
                return last

            def step2(i, s, turn, on):
                if on(0):
                    pe.wait_ge(xn_ready, i + 1)
                    for hf in range(2):
                        if isinstance(i, int) and i == 1:
                            pe.wait_ge(xnT_ready, hf + 1)
                        elif not isinstance(i, int) or i >= 2:
                            pe.wait_ge(proj_ready, 2 * (i - 2) + hf + 1)
                        for q in range(QUAD):
                            last = nc.tensor.transpose(ps[0:HALF, hf, 128 * q:128 * q + 128],
                                                       xn[s][:, q, hf * HALF:(hf + 1) * HALF], ident[:, :])
                        last.then_inc(xnT_in_psum, 1)
                if on(1):
                    b, p = i - 1, 1 - s

                    def tok(q):
                        return lambda hf: (xn_hi[p][0:K[hf], hf, 128 * q:128 * q + 128], xn_lo[p][0:K[hf], hf, 128 * q:128 * q + 128])

                    pe.wait_ge(xn_hi_ready, 2 * b + 2)
                    pe.wait_ge(xn_lo_ready, 2 * b + 2)
                    for pr_ in range(2):
                        if not isinstance(b, int) or b >= 1:
                            pe.wait_ge(gate_ready, 2 * (b - 1) + pr_ + 1)
                        for q in range(2):
                            last = split3(ps[:, 2 + 3 * pr_ + q, 0:2 * DIM], tok(2 * pr_ + q),
                                          lambda hf: (win_hi[0:K[hf], hf, DIM:3 * DIM], win_lo[0:K[hf], hf, DIM:3 * DIM]))
                        last.then_inc(zv_in_psum, 1)
                        for q in range(2):
                            last = split3(ps[:, 4 + 3 * pr_, DIMN * q:DIMN * (q + 1)], tok(2 * pr_ + q),
                                          lambda hf: (win_hi[0:K[hf], hf, 3 * DIM:], win_lo[0:K[hf], hf, 3 * DIM:]))
                        last.then_inc(zv_in_psum, 1)
                        if pr_ == 0:
                            for mh in range(2):
                                if on(0):
                                    pe.wait_ge(xnT_ready, 2 * i + mh + 1)
                                else:
                                    pe.wait_ge(proj_ready, 2 * b - 1 + mh)
                                last = split3(ps[0:HALF, mh, :],
                                              lambda hf: (win_hi[0:K[hf], hf, mh * HALF:(mh + 1) * HALF],
                                                          win_lo[0:K[hf], hf, mh * HALF:(mh + 1) * HALF]),
                                              lambda hf: (xn_hi[p][0:K[hf], hf, :], xn_lo[p][0:K[hf], hf, :]))
                                last.then_inc(proj_in_psum, 1)

            batches(pe, step2, 1)
            leave(pe, 2)

            def convolve(g, s, turn, first):
                for c in range(CG):
                    if c % HCG == 0:
                        pe.wait_ge(taps_loaded[s][c // HCG], 48 * (turn + 1))
                    if c == 0 and not first:
                        pe.wait_ge(conv_kept_act, g - 1)
                    if c == CG // 2 and not first:
                        pe.wait_ge(conv_kept_dve, g - 1)
                    o = ps[:, 4 * s + c // 2, NTOK * (c % 2):NTOK * (c % 2) + NTOK]
                    nc.tensor.matmul(o, src0[s][:, c, :], toep[s][:, c, 0:NTOK], start=True, stop=False)
                    last = nc.tensor.matmul(o, src1[s][0:TAP1, c, :], toep[s][0:TAP1, c, TAP0:TAP0 + NTOK], start=False, stop=True)
                    if c % 4 == 3:
                        last.then_inc(conv_in_psum, 1)

            pe.wait_ge(small_loaded, 16 * (4 + 2 * QUAD))
            for dh in range(2):
                for hf in range(2):
                    last = nc.tensor.transpose(ps[0:HALF, dh, HALF * hf:HALF * hf + K[hf]],
                                               w_out_sb[0:K[hf], hf, HALF * dh:HALF * dh + HALF], ident[0:K[hf], 0:K[hf]])
            last.then_inc(wo_turned, 1)
            pe.wait_ge(wo_copied, 1)
            for hf in range(2):
                for dh in range(2):
                    last = nc.tensor.matmul(ps[0:K[hf], 2 + hf, 0:NODEX], woT[:, dh, HALF * hf:HALF * hf + K[hf]],
                                            node_inT[:, dh, :], start=(dh == 0), stop=(dh == 1))
            last.then_inc(wo_turned, 1)
            pe.wait_ge(wo_nodes, 2)
            convolve(0, 0, 0, True)
            convolve(1, 1, 0, True)
            with pe.Fori(0, NGROUP // 2 - 1) as j:
                for s in range(2):
                    convolve(2 * j + 2 + s, s, j + 1, False)
            leave(pe, 3)

            pe.wait_ge(tree_set, 4)

            def turn_y(i, s):
                pe.wait_ge(y_ready, i + 1)
                for hf in range(2):
                    wait(pe, u_ready, 2 * i - 1 + hf if not isinstance(i, int) or i >= 1 else 0)
                    for q in range(QUAD):
                        last = nc.tensor.transpose(ps[0:HALF, hf, 128 * q:128 * q + 128],
                                                   gy[s][:, q, hf * HALF:(hf + 1) * HALF], ident[:, :])
                    last.then_inc(yT_in_psum, 1)

            turn_y(0, 0)

            def step4(i, s, turn, on):
                if on(-1):
                    turn_y(i + 1, 1 - s)
                if on(2):
                    b = i - 2
                    pe.wait_ge(coefT_ready, b + 1)
                    wait(pe, out_ready, 2 * b)
                    for k in range(2):
                        nc.tensor.matmul(ps[:, 6 + k, 0:2 * DIM], coefT[:, :],
                                         node_out[:, 2 * k:2 * k + 2, :].rearrange("p l d -> p (l d)"), start=True, stop=True)\
                            .then_inc(node_in_psum, 1)
                if on(0):
                    pe.wait_ge(u_ready, 2 * i + 2)
                    wait(pe, logit_ready, i)
                    for k in range(2):
                        for q in range(2):
                            for hf in range(2):
                                kk = K[hf]
                                last = nc.tensor.matmul(ps[:, 2 + k, DIMN * q:DIMN * (q + 1)],
                                                        uT[s][0:kk, hf, 128 * (2 * k + q):128 * (2 * k + q) + 128],
                                                        w_out_sb[0:kk, hf, :], start=(hf == 0), stop=(hf == 1))
                        last.then_inc(mix_in_psum, 1)
                if on(1):
                    pe.wait_ge(coef_ready, i)
                    nc.tensor.transpose(ps[:, 4, 0:128], coef[:, :, :].rearrange("p q n -> p (q n)"), ident[:, :])\
                        .then_inc(coefT_in_psum, 1)

            batches(pe, step4, 2)


NAMES = ["x", "cls_tok", "L0_tok_gamma", "L0_tok_beta", "L0_tok_W", "L0_tok_b", "L0_attn_w_in", "L0_attn_b_in",
         "L0_attn_w_filt", "L0_attn_b_filt", "L0_attn_w_short", "L0_attn_b_short", "L0_attn_w_out", "L0_attn_b_out",
         "L0_ffn_weights_in", "L0_ffn_weights_out"]


def kernel(**inputs):
    import concourse.bacc as bacc
    from concourse.bass_utils import run_bass_kernel_spmd

    nc = bacc.Bacc("TRN2", target_bir_lowering=False, num_devices=1)
    arrays = {n: np.ascontiguousarray(inputs[n]) for n in NAMES}
    arrays.update(constants())
    args = [nc.dram_tensor(f"in_{n}", a.shape, F32, kind="ExternalInput").ap() for n, a in arrays.items()]
    result = nc.dram_tensor("out_0", (NIMG, NTOK, DIM), F32, kind="ExternalOutput").ap()
    build(nc, *args, result)
    r = run_bass_kernel_spmd(nc, [{f"in_{n}": a for n, a in arrays.items()}], core_ids=[0])
    return r.results[0]["out_0"]
```
